# Optimizing a Trainium2 kernel written in Bass

```python
import numpy as np
import jax
import jax.numpy as jnp

def _softmax(x, axis=-1):
    return jax.nn.softmax(x, axis=axis)

def _gelu(x):
    return jax.nn.gelu(x, approximate=True)

def _silu(x):
    return jax.nn.silu(x)

def _sigmoid(x):
    return jax.nn.sigmoid(x)

def _layernorm(x, axis=-1, eps=1e-05):
    m = jnp.mean(x, axis=axis, keepdims=True)
    v = jnp.var(x, axis=axis, keepdims=True)
    return (x - m) / jnp.sqrt(v + eps)

def _scatter_add(tgt, idx, src, axis=0):
    return tgt.at[idx].add(src)

def _segment_sum(src, seg, n):
    return jax.ops.segment_sum(src, seg, n)
kernel_name = 'mk_decoder_postln_d2_seqx_r8_f33798'

def setup_inputs(seed: int=0):
    np.random.seed(seed)
    _w = jnp.asarray

    def _rec_inputs():
        import jax
        import jax.numpy as jnp
        _rk = jax.random.key(seed)
        x = -0.0003929 + 0.9999 * jax.random.normal(jax.random.fold_in(_rk, 1), (1, 1024, 128), jnp.float32)
        _lenS = 1024 - jax.random.randint(jax.random.fold_in(_rk, 7), (1,), 0, max(1, 1024 // 4) + 1, jnp.int32)
        _lenS2 = 6404 - jax.random.randint(jax.random.fold_in(_rk, 8), (1,), 0, max(1, 6404 // 4) + 1, jnp.int32)
        _ctx_1024P = jax.random.normal(jax.random.fold_in(_rk, 11), (1, 16, 128), jnp.float32)
        _ctx_1024c = jax.random.dirichlet(jax.random.fold_in(_rk, 511), 0.3 * jnp.ones((16,), jnp.float32), (1, 6404))
        _ctx_1024t = jnp.einsum('bsk,bkd->bsd', _ctx_1024c, _ctx_1024P)
        _ctx_1024t = _ctx_1024t * jax.lax.rsqrt(jnp.mean(jnp.square(_ctx_1024t)) + 1e-12) * 0.953939
        ctx_1024 = -3.05549e-07 + 0.0199987 * (_ctx_1024t + 0.3 * jax.random.normal(jax.random.fold_in(_rk, 611), (1, 6404, 128), jnp.float32))
        _validS = jnp.arange(1024)[None, :] < _lenS[:, None]
        _validS2 = jnp.arange(6404)[None, :] < _lenS2[:, None]
        _causal = jnp.tril(jnp.ones((1024, 1024), dtype=bool))
        mask_1x1xSxS2_ik1 = jnp.where(jnp.broadcast_to(_validS2[0:1, None, None, :], (1, 1, 1024, 6404)), 1, 0).astype(jnp.int32)
        return (x, ctx_1024, mask_1x1xSxS2_ik1)
    x, ctx_1024, mask_1x1xSxS2_ik1 = _rec_inputs()

    def _L0_attn_setup():
        import jax, jax.numpy as jnp
        import numpy as np
        HEADS = 16
        DIMS = [64, 64, 64, 64]
        EPS = 0.0001
        P_POW = 2

        def _cdist(Q, K):
            q2 = jnp.sum(Q * Q, axis=-1)
            k2 = jnp.sum(K * K, axis=-1)
            qk = jnp.einsum('hbtd,hbsd->hbts', Q, K)
            d2 = q2[..., :, None] + k2[..., None, :] - 2.0 * qk
            return jnp.sqrt(jnp.maximum(d2, 0.0))
        key = jax.random.key(seed)
        ks = jax.random.split(key, 4)
        b, t, d_in = (2, 256, 128)
        d_proj = HEADS * sum(DIMS)
        X = jax.random.normal(ks[0], (b, t, d_in), dtype=jnp.float32)
        W_in = jax.random.normal(ks[1], (d_in, d_proj), dtype=jnp.float32) * d_in ** (-0.5)
        b_in = jnp.zeros((d_proj,), dtype=jnp.float32)
        W_out = jax.random.normal(ks[2], (HEADS * DIMS[2], d_in), dtype=jnp.float32) * (HEADS * DIMS[2]) ** (-0.5)
        b_out = jnp.zeros((d_in,), dtype=jnp.float32)
        return {'X': X, 'W_in': W_in, 'b_in': b_in, 'W_out': W_out, 'b_out': b_out}
    _L0_attn_all = _L0_attn_setup()
    _L0_attn_in = {k: v for k, v in _L0_attn_all.items() if k in ('W_in', 'b_in', 'W_out', 'b_out')}
    del _L0_attn_all

    def _L0_xattn_setup():
        import jax, jax.numpy as jnp
        import numpy as np
        E, T, H, F = (8, 256, 128, 512)
        key = jax.random.key(seed)
        k1, k2, k3 = jax.random.split(key, 3)
        x = jax.random.normal(k1, (E, T, H), dtype=jnp.float32)
        w1 = jax.random.normal(k2, (E, F, H), dtype=jnp.float32) * 0.02
        w2 = jax.random.normal(k3, (E, F, H), dtype=jnp.float32) * 0.02
        return {'x': x, 'w1': w1, 'w2': w2}
    _L0_xattn_all = _L0_xattn_setup()
    _L0_xattn_in = {k: v for k, v in _L0_xattn_all.items() if k in ()}
    del _L0_xattn_all

    def _L0_ffn_setup():
        import jax, jax.numpy as jnp
        import numpy as np
        D_MODEL = 128
        D_FF = 512
        N_EXPERTS = 8
        INIT_SCALE = 0.1

        def _trunc_normal(key, shape, std):
            return std * jax.random.truncated_normal(key, -2.0, 2.0, shape, dtype=jnp.float32)
        key = jax.random.key(seed)
        ks = jax.random.split(key, 5)
        x = jax.random.normal(ks[0], (4, 128, D_MODEL), dtype=jnp.float32)
        router_W = _trunc_normal(ks[1], (D_MODEL, N_EXPERTS), INIT_SCALE / np.sqrt(D_MODEL))
        router_b = jnp.zeros((N_EXPERTS,), dtype=jnp.float32)
        W1 = _trunc_normal(ks[2], (N_EXPERTS, D_MODEL, D_FF), INIT_SCALE / np.sqrt(D_MODEL))
        b1 = jnp.zeros((N_EXPERTS, D_FF), dtype=jnp.float32)
        W2 = _trunc_normal(ks[3], (N_EXPERTS, D_FF, D_MODEL), INIT_SCALE / np.sqrt(D_FF))
        b2 = jnp.zeros((N_EXPERTS, D_MODEL), dtype=jnp.float32)
        return {'x': x, 'router_W': router_W, 'router_b': router_b, 'W1': W1, 'b1': b1, 'W2': W2, 'b2': b2}
    _L0_ffn_all = _L0_ffn_setup()
    _L0_ffn_in = {k: v for k, v in _L0_ffn_all.items() if k in ('router_W', 'router_b', 'W1', 'b1', 'W2', 'b2')}
    del _L0_ffn_all

    def _L1_attn_setup():
        import jax, jax.numpy as jnp
        import numpy as np
        HEADS = 16
        KV_HEADS = 8
        DIMS = 64
        IN_DIMS = 128
        B, S = (2, 256)

        def rope(x):
            seq_len, dim = (x.shape[-2], x.shape[-1])
            thetas = 1.0 / 1250 ** (jnp.arange(0, dim, 2) / dim)
            ang = jnp.arange(1, seq_len + 1)[:, None] * thetas[None, :]
            cos, sin = (jnp.cos(ang), jnp.sin(ang))
            xe, xo = (x[..., ::2], x[..., 1::2])
            real = xe * cos - xo * sin
            imag = xe * sin + xo * cos
            return jnp.stack([real, imag], axis=-1).reshape(x.shape)
        key = jax.random.key(seed)
        k1, k2, k3, k4, k5 = jax.random.split(key, 5)
        q = jax.random.normal(k1, (B, S, IN_DIMS), dtype=jnp.float32)
        sd = 1.0 / np.sqrt(IN_DIMS)
        Wq = jax.random.normal(k2, (IN_DIMS, HEADS * DIMS), dtype=jnp.float32) * sd
        Wk = jax.random.normal(k3, (IN_DIMS, KV_HEADS * DIMS), dtype=jnp.float32) * sd
        Wv = jax.random.normal(k4, (IN_DIMS, KV_HEADS * DIMS), dtype=jnp.float32) * sd
        Wo = jax.random.normal(k5, (HEADS * DIMS, IN_DIMS), dtype=jnp.float32) / np.sqrt(HEADS * DIMS)
        return {'q': q, 'Wq': Wq, 'Wk': Wk, 'Wv': Wv, 'Wo': Wo}
    _L1_attn_all = _L1_attn_setup()
    _L1_attn_in = {k: v for k, v in _L1_attn_all.items() if k in ('Wq', 'Wk', 'Wv', 'Wo')}
    del _L1_attn_all

    def _L1_xattn_setup():
        import jax, jax.numpy as jnp
        import numpy as np
        EMBED = 128
        HEADS = 16
        HEAD_DIM = EMBED // HEADS
        N, S = (2, 256)
        key = jax.random.key(seed)
        ks = jax.random.split(key, 9)
        values = jax.random.normal(ks[0], (N, S, EMBED), dtype=jnp.float32)
        keys_in = jax.random.normal(ks[1], (N, S, EMBED), dtype=jnp.float32)
        query = jax.random.normal(ks[2], (N, S, EMBED), dtype=jnp.float32)
        mask = jax.random.randint(ks[3], (1, 1, S, S), 0, 2, dtype=jnp.int32)
        sc = 1.0 / np.sqrt(HEAD_DIM)
        Wv = jax.random.normal(ks[4], (HEAD_DIM, HEAD_DIM), dtype=jnp.float32) * sc
        Wk = jax.random.normal(ks[5], (HEAD_DIM, HEAD_DIM), dtype=jnp.float32) * sc
        Wq = jax.random.normal(ks[6], (HEAD_DIM, HEAD_DIM), dtype=jnp.float32) * sc
        Wo = jax.random.normal(ks[7], (EMBED, EMBED), dtype=jnp.float32) * (1.0 / np.sqrt(EMBED))
        bo = jax.random.normal(ks[8], (EMBED,), dtype=jnp.float32) * 0.01
        return {'values': values, 'keys': keys_in, 'query': query, 'mask': mask, 'heads': HEADS, 'Wv': Wv, 'Wk': Wk, 'Wq': Wq, 'Wo': Wo, 'bo': bo}
    _L1_xattn_all = _L1_xattn_setup()
    _L1_xattn_in = {k: v for k, v in _L1_xattn_all.items() if k in ('Wv', 'Wk', 'Wq', 'Wo', 'bo')}
    del _L1_xattn_all

    def _L1_ffn_setup():
        import jax, jax.numpy as jnp
        import numpy as np
        B, N, D, H, E = (4, 128, 128, 16, 8)
        DK = D // H
        HID = 4 * D
        EPS = 1e-05

        def _layernorm(x, w, b):
            m = jnp.mean(x, axis=-1, keepdims=True)
            v = jnp.mean(jnp.square(x - m), axis=-1, keepdims=True)
            return (x - m) * jax.lax.rsqrt(v + EPS) * w + b

        def _msa(x, w_qkv, w_proj):
            b, n, d = x.shape
            qkv = (x @ w_qkv).reshape(b, n, 3, H, DK)
            q = qkv[:, :, 0].transpose(0, 2, 1, 3)
            k = qkv[:, :, 1].transpose(0, 2, 1, 3)
            v = qkv[:, :, 2].transpose(0, 2, 1, 3)
            attn = jnp.einsum('bhnd,bhmd->bhnm', q, k) * (1.0 / np.sqrt(DK))
            attn = jax.nn.softmax(attn, axis=-1)
            y = jnp.einsum('bhnm,bhmd->bhnd', attn, v)
            y = y.transpose(0, 2, 1, 3).reshape(b, n, d)
            return y @ w_proj

        def _moe_mlp(x, gate_w, gate_b, w1, w2):
            b, n, d = x.shape
            xf = x.reshape(b * n, d)
            logits = xf @ gate_w + gate_b
            one_hot = jax.nn.one_hot(jnp.argmax(logits, axis=-1), E, dtype=xf.dtype)
            h = jax.nn.gelu(jnp.einsum('td,edh->teh', xf, w1), approximate=True)
            y = jnp.einsum('teh,ehd->ted', h, w2)
            out = jnp.einsum('te,ted->td', one_hot, y)
            return out.reshape(b, n, d)
        key = jax.random.key(seed)
        ks = jax.random.split(key, 8)
        s = 0.02
        return {'x': jax.random.normal(ks[0], (B, N, D), jnp.float32), 'ln1_w': jnp.ones((D,), jnp.float32), 'ln1_b': jnp.zeros((D,), jnp.float32), 'w_qkv': jax.random.normal(ks[1], (D, 3 * D), jnp.float32) * s, 'w_proj': jax.random.normal(ks[2], (D, D), jnp.float32) * s, 'ln2_w': jnp.ones((D,), jnp.float32), 'ln2_b': jnp.zeros((D,), jnp.float32), 'gate_w': jax.random.normal(ks[3], (D, E), jnp.float32) * s, 'gate_b': jnp.zeros((E,), jnp.float32), 'w1': jax.random.normal(ks[4], (E, D, HID), jnp.float32) * s, 'w2': jax.random.normal(ks[5], (E, HID, D), jnp.float32) * s}
    _L1_ffn_all = _L1_ffn_setup()
    _L1_ffn_in = {k: v for k, v in _L1_ffn_all.items() if k in ('ln1_w', 'ln1_b', 'w_qkv', 'w_proj', 'ln2_w', 'ln2_b', 'gate_w', 'gate_b', 'w1', 'w2')}
    del _L1_ffn_all
    return {'x': x, 'ctx_1024': ctx_1024, 'mask_1x1xSxS2_ik1': mask_1x1xSxS2_ik1, 'L0_attn_W_in': _L0_attn_in['W_in'], 'L0_attn_b_in': _L0_attn_in['b_in'], 'L0_attn_W_out': _L0_attn_in['W_out'], 'L0_attn_b_out': _L0_attn_in['b_out'], 'L0_ffn_router_W': _L0_ffn_in['router_W'], 'L0_ffn_router_b': _L0_ffn_in['router_b'], 'L0_ffn_W1': _L0_ffn_in['W1'], 'L0_ffn_b1': _L0_ffn_in['b1'], 'L0_ffn_W2': _L0_ffn_in['W2'], 'L0_ffn_b2': _L0_ffn_in['b2'], 'L1_attn_Wq': _L1_attn_in['Wq'], 'L1_attn_Wk': _L1_attn_in['Wk'], 'L1_attn_Wv': _L1_attn_in['Wv'], 'L1_attn_Wo': _L1_attn_in['Wo'], 'L1_xattn_Wv': _L1_xattn_in['Wv'], 'L1_xattn_Wk': _L1_xattn_in['Wk'], 'L1_xattn_Wq': _L1_xattn_in['Wq'], 'L1_xattn_Wo': _L1_xattn_in['Wo'], 'L1_xattn_bo': _L1_xattn_in['bo'], 'L1_ffn_ln1_w': _L1_ffn_in['ln1_w'], 'L1_ffn_ln1_b': _L1_ffn_in['ln1_b'], 'L1_ffn_w_qkv': _L1_ffn_in['w_qkv'], 'L1_ffn_w_proj': _L1_ffn_in['w_proj'], 'L1_ffn_ln2_w': _L1_ffn_in['ln2_w'], 'L1_ffn_ln2_b': _L1_ffn_in['ln2_b'], 'L1_ffn_gate_w': _L1_ffn_in['gate_w'], 'L1_ffn_gate_b': _L1_ffn_in['gate_b'], 'L1_ffn_w1': _L1_ffn_in['w1'], 'L1_ffn_w2': _L1_ffn_in['w2']}

def reference(x, ctx_1024, mask_1x1xSxS2_ik1, L0_attn_W_in, L0_attn_b_in, L0_attn_W_out, L0_attn_b_out, L0_ffn_router_W, L0_ffn_router_b, L0_ffn_W1, L0_ffn_b1, L0_ffn_W2, L0_ffn_b2, L1_attn_Wq, L1_attn_Wk, L1_attn_Wv, L1_attn_Wo, L1_xattn_Wv, L1_xattn_Wk, L1_xattn_Wq, L1_xattn_Wo, L1_xattn_bo, L1_ffn_ln1_w, L1_ffn_ln1_b, L1_ffn_w_qkv, L1_ffn_w_proj, L1_ffn_ln2_w, L1_ffn_ln2_b, L1_ffn_gate_w, L1_ffn_gate_b, L1_ffn_w1, L1_ffn_w2):
    import jax
    import jax.numpy as jnp

    def _L0_attn_ref(X, W_in, b_in, W_out, b_out):
        import jax, jax.numpy as jnp
        import numpy as np
        HEADS = 16
        DIMS = [64, 64, 64, 64]
        EPS = 0.0001
        P_POW = 2

        def _cdist(Q, K):
            q2 = jnp.sum(Q * Q, axis=-1)
            k2 = jnp.sum(K * K, axis=-1)
            qk = jnp.einsum('hbtd,hbsd->hbts', Q, K)
            d2 = q2[..., :, None] + k2[..., None, :] - 2.0 * qk
            return jnp.sqrt(jnp.maximum(d2, 0.0))
        b, t, _ = X.shape
        P = X @ W_in + b_in
        P = P.reshape(b, t, HEADS, sum(DIMS))
        P = jnp.transpose(P, (2, 0, 1, 3))
        splits = np.cumsum(DIMS)[:-1]
        Q, K, V, G = jnp.split(P, splits, axis=-1)
        W = jnp.power(EPS + _cdist(Q, K), -P_POW)
        W = W / (EPS + jnp.sum(W, axis=-1, keepdims=True))
        A = jnp.einsum('hbts,hbse->hbte', W, V)
        H = G * A
        H = jnp.transpose(H, (1, 2, 0, 3)).reshape(b, t, HEADS * DIMS[2])
        return H @ W_out + b_out

    def _L0_xattn_ref(x, w1, w2):
        import jax, jax.numpy as jnp
        import numpy as np
        E, T, H, F = (8, 256, 128, 512)
        h = jnp.einsum('eth,efh->etf', x, w1)
        a = jax.nn.gelu(h, approximate=True)
        return jnp.einsum('etf,efh->eth', a, w2)

    def _L0_ffn_ref(x, router_W, router_b, W1, b1, W2, b2):
        import jax, jax.numpy as jnp
        import numpy as np
        D_MODEL = 128
        D_FF = 512
        N_EXPERTS = 8
        INIT_SCALE = 0.1

        def _trunc_normal(key, shape, std):
            return std * jax.random.truncated_normal(key, -2.0, 2.0, shape, dtype=jnp.float32)
        logits = jnp.einsum('bsd,de->bse', x.astype(jnp.float32), router_W) + router_b
        probs = jax.nn.softmax(logits, axis=-1)
        top1 = jnp.argmax(probs, axis=-1)
        mask = jax.nn.one_hot(top1, N_EXPERTS, dtype=x.dtype)
        gates = mask * probs.astype(x.dtype)
        h = jax.nn.relu(jnp.einsum('bsd,edf->besf', x, W1) + b1[:, None, :])
        y = jnp.einsum('besf,efd->besd', h, W2) + b2[:, None, :]
        out = jnp.einsum('bse,besd->bsd', gates, y)
        return out

    def _L1_attn_ref(q, Wq, Wk, Wv, Wo):
        import jax, jax.numpy as jnp
        import numpy as np
        HEADS = 16
        KV_HEADS = 8
        DIMS = 64
        IN_DIMS = 128
        B, S = (2, 256)

        def rope(x):
            seq_len, dim = (x.shape[-2], x.shape[-1])
            thetas = 1.0 / 1250 ** (jnp.arange(0, dim, 2) / dim)
            ang = jnp.arange(1, seq_len + 1)[:, None] * thetas[None, :]
            cos, sin = (jnp.cos(ang), jnp.sin(ang))
            xe, xo = (x[..., ::2], x[..., 1::2])
            real = xe * cos - xo * sin
            imag = xe * sin + xo * cos
            return jnp.stack([real, imag], axis=-1).reshape(x.shape)
        batch, seq_len, in_dims = q.shape
        kv = q
        xq = rope(q @ Wq)
        xk = rope(kv @ Wk)
        xv = kv @ Wv
        xk = jnp.repeat(xk, 2, axis=-1)
        xv = jnp.repeat(xv, 2, axis=-1)
        xq = xq.reshape(batch, seq_len, HEADS, DIMS).transpose(0, 2, 1, 3)
        xk = xk.reshape(batch, seq_len, HEADS, DIMS).transpose(0, 2, 3, 1)
        xv = xv.reshape(batch, seq_len, HEADS, DIMS).transpose(0, 2, 1, 3)
        scale = (DIMS / HEADS) ** (-0.5)
        scores = jax.nn.softmax(xq @ xk * scale, axis=-1)
        out = (scores @ xv).transpose(0, 2, 1, 3).reshape(batch, seq_len, -1)
        return out @ Wo

    def _L1_xattn_ref(values, keys, query, mask, heads, Wv, Wk, Wq, Wo, bo):
        import jax, jax.numpy as jnp
        import numpy as np
        EMBED = 128
        HEADS = 16
        HEAD_DIM = EMBED // HEADS
        N, S = (2, 256)
        n, q_len, embed = query.shape
        v_len, k_len = (values.shape[1], keys.shape[1])
        d = embed // heads
        v = values.reshape(n, v_len, heads, d)
        k = keys.reshape(n, k_len, heads, d)
        q = query.reshape(n, q_len, heads, d)
        v = jnp.einsum('nlhd,ed->nlhe', v, Wv)
        k = jnp.einsum('nlhd,ed->nlhe', k, Wk)
        q = jnp.einsum('nlhd,ed->nlhe', q, Wq)
        energy = jnp.einsum('nqhd,nkhd->nhqk', q, k)
        energy = jnp.where(mask == 0, jnp.float32(-1e+20), energy)
        attn = jax.nn.softmax(energy / jnp.sqrt(jnp.float32(embed)), axis=3)
        out = jnp.einsum('nhql,nlhd->nqhd', attn, v).reshape(n, q_len, embed)
        out = out @ Wo.T + bo
        return out

    def _L1_ffn_ref(x, ln1_w, ln1_b, w_qkv, w_proj, ln2_w, ln2_b, gate_w, gate_b, w1, w2):
        import jax, jax.numpy as jnp
        import numpy as np
        B, N, D, H, E = (4, 128, 128, 16, 8)
        DK = D // H
        HID = 4 * D
        EPS = 1e-05

        def _layernorm(x, w, b):
            m = jnp.mean(x, axis=-1, keepdims=True)
            v = jnp.mean(jnp.square(x - m), axis=-1, keepdims=True)
            return (x - m) * jax.lax.rsqrt(v + EPS) * w + b

        def _msa(x, w_qkv, w_proj):
            b, n, d = x.shape
            qkv = (x @ w_qkv).reshape(b, n, 3, H, DK)
            q = qkv[:, :, 0].transpose(0, 2, 1, 3)
            k = qkv[:, :, 1].transpose(0, 2, 1, 3)
            v = qkv[:, :, 2].transpose(0, 2, 1, 3)
            attn = jnp.einsum('bhnd,bhmd->bhnm', q, k) * (1.0 / np.sqrt(DK))
            attn = jax.nn.softmax(attn, axis=-1)
            y = jnp.einsum('bhnm,bhmd->bhnd', attn, v)
            y = y.transpose(0, 2, 1, 3).reshape(b, n, d)
            return y @ w_proj

        def _moe_mlp(x, gate_w, gate_b, w1, w2):
            b, n, d = x.shape
            xf = x.reshape(b * n, d)
            logits = xf @ gate_w + gate_b
            one_hot = jax.nn.one_hot(jnp.argmax(logits, axis=-1), E, dtype=xf.dtype)
            h = jax.nn.gelu(jnp.einsum('td,edh->teh', xf, w1), approximate=True)
            y = jnp.einsum('teh,ehd->ted', h, w2)
            out = jnp.einsum('te,ted->td', one_hot, y)
            return out.reshape(b, n, d)
        x = x + _msa(_layernorm(x, ln1_w, ln1_b), w_qkv, w_proj)
        x = x + _moe_mlp(_layernorm(x, ln2_w, ln2_b), gate_w, gate_b, w1, w2)
        return x
    x = _layernorm(x + _L0_attn_ref(x, L0_attn_W_in, L0_attn_b_in, L0_attn_W_out, L0_attn_b_out), axis=-1)
    x = _layernorm(x + _L0_xattn_ref(x, ctx_1024, ctx_1024), axis=-1)
    x = _layernorm(x + _L0_ffn_ref(x, L0_ffn_router_W, L0_ffn_router_b, L0_ffn_W1, L0_ffn_b1, L0_ffn_W2, L0_ffn_b2), axis=-1)
    x = _layernorm(x + _L1_attn_ref(x, L1_attn_Wq, L1_attn_Wk, L1_attn_Wv, L1_attn_Wo), axis=-1)
    x = _layernorm(x + _L1_xattn_ref(ctx_1024, ctx_1024, x, mask_1x1xSxS2_ik1, 16, L1_xattn_Wv, L1_xattn_Wk, L1_xattn_Wq, L1_xattn_Wo, L1_xattn_bo), axis=-1)
    x = _layernorm(x + _L1_ffn_ref(x, L1_ffn_ln1_w, L1_ffn_ln1_b, L1_ffn_w_qkv, L1_ffn_w_proj, L1_ffn_ln2_w, L1_ffn_ln2_b, L1_ffn_gate_w, L1_ffn_gate_b, L1_ffn_w1, L1_ffn_w2), axis=-1)
    return x

_drawn_inputs = setup_inputs


def setup_inputs(seed=0):
    import zlib

    import numpy as np

    out = dict(_drawn_inputs(seed))
    spreads = {'L0_attn_b_in': (0.0, 0.1),
     'L0_attn_b_out': (0.0, 0.1),
     'L0_ffn_router_b': (0.0, 0.276),
     'L0_ffn_b1': (0.0, 0.8),
     'L0_ffn_b2': (0.0, 0.305),
     'L1_ffn_ln1_w': (1.0, 0.6),
     'L1_ffn_ln1_b': (0.0, 0.8),
     'L1_ffn_ln2_w': (1.0, 0.6),
     'L1_ffn_ln2_b': (0.0, 2.0),
     'L1_ffn_gate_b': (0.0, 1.731)}
    factors = {'L0_ffn_router_W': 3.0,
     'L0_ffn_W1': 8.0,
     'L0_ffn_W2': 8.0,
     'L1_xattn_Wv': 5.444,
     'L1_xattn_Wk': 8.0,
     'L1_xattn_Wq': 8.0,
     'L1_xattn_Wo': 6.803,
     'L1_xattn_bo': 5.303,
     'L1_ffn_w_qkv': 8.0,
     'L1_ffn_w_proj': 8.0,
     'L1_ffn_gate_w': 3.533,
     'L1_ffn_w1': 3.059,
     'L1_ffn_w2': 3.01}
    for name, (base, spread) in spreads.items():
        noise = np.random.default_rng([zlib.crc32(name.encode()), seed]).standard_normal(out[name].shape)
        drawn = base * np.exp(spread * noise) if base else spread * noise
        out[name] = jnp.asarray(drawn.astype(out[name].dtype))
    for name, factor in factors.items():
        out[name] = (out[name] * factor).astype(out[name].dtype)
    return out
```

```python
from contextlib import ExitStack, nullcontext

import numpy as np

import concourse.bass as bass
from concourse import mybir
from concourse.alu_op_type import AluOpType as ALU

F32 = mybir.dt.float32
BF16 = mybir.dt.bfloat16
I32 = mybir.dt.int32
ACT = mybir.ActivationFunctionType
AX = mybir.AxisListType

P = 128
T = 1024
HALF = 512
NT = T // P
KEYS = 6404
NC = -(-KEYS // P)
KPAD = NC * P
HEADS = 16
GROUPS = HEADS // 4
PAIRS = HEADS // 2
D0 = 64
D1 = 32
D8 = 8
EXPERTS = 8
FF = 512
FC = FF // P
LN_EPS = 1e-5
DIST_EPS = 1e-4
MASKED = -1e20
PADDED = -1e38
BOUND_LIMIT = 30.0


class Names:

    def __init__(self, nc, ctx, stage):
        self.nc, self.ctx, self.stage, self.sems = nc, ctx, stage, []
        ctx.callback(self.clear)

    def sem(self, name):
        self.sems.append(self.nc.alloc_semaphore(f"{self.stage}_{name}"))
        return self.sems[-1]

    def sb(self, name, shape, dt=F32):
        return self.ctx.enter_context(self.nc.sbuf_tensor(f"{self.stage}_{name}", shape, dt))

    def clear(self):
        if self.sems:
            with self.nc.Block() as block:
                @block.gpsimd
                def _(pool):
                    self.nc.clear_and_free_semaphores(self.sems)


class Count:

    def __init__(self, eng, sem, base=0):
        self.eng, self.sem, self.base, self.n = eng, sem, base, 0

    def up(self, ins):
        ins.then_inc(self.sem, 1)
        self.n += 1

    def done(self):
        self.eng.wait_ge(self.sem, self.base + self.n)


def half(ap, h):
    return ap[:, h * HALF:(h + 1) * HALF]


def distance_attention(nc, PS, x, w, Y):
    MADE = 8 + 2 * NT
    BODY = MADE + 1
    DVE_STEP = 4 + 4
    with ExitStack() as ctx:
        n = Names(nc, ctx, "dist")
        wp = n.sb("wp", [P, 2, 5 * P])
        bqk = n.sb("bqk", [D0, HEADS * 2])
        bg = n.sb("bg", [P, PAIRS])
        bv = n.sb("bv", [P, PAIRS * P])
        Q = n.sb("Q", [P, 2, T])
        K = n.sb("K", [P, 2, T])
        sq = n.sb("sq", [P, T])
        V = n.sb("V", [P, 2, NT, P])
        G = n.sb("G", [P, 2, T])
        D = n.sb("D", [P, 4, NT, T])
        wsum = n.sb("wsum", [P, 2, T])
        ones = n.sb("ones", [P, D0])
        eps = n.sb("eps", [P, 1])
        rec = n.sb("rec", [P, T])
        H = n.sb("H", [P, T])
        norms = n.sb("norms", [P, 34])
        rows = n.sb("rows", [P, 2])
        s_const, s_set = n.sem("const"), n.sem("set")
        s_w = [n.sem("w0"), n.sem("w1")]
        s_unit = n.sem("unit")
        s_taken = n.sem("taken")
        s_sq = n.sem("sq")
        s_dve = n.sem("dve")
        s_act = n.sem("act")
        s_exp = n.sem("exp")
        s_wsum = n.sem("wsum")
        s_pool = n.sem("pool")
        s_pv = n.sem("pv")
        s_h = n.sem("h")
        s_proj = n.sem("proj")

        def ring(u):
            return PS[:, 2 * (u % 2):2 * (u % 2) + 2, :]

        with nc.Block() as block:
            @block.sync
            def _(sp):
                sp.dma_start(wp[:, 0, :], w["wpair"][0]).then_inc(s_w[0], 16)
                for to, of in ((bqk, "bqk"), (bg, "bg"), (bv, "bv"), (norms, "norms"), (rows, "rows")):
                    sp.dma_start(to[:, :], w[of]).then_inc(s_const, 16)
                sp.dma_start(wp[:, 1, :], w["wpair"][1]).then_inc(s_w[1], 16)

                def more(p, par):
                    sp.wait_ge(s_proj, p)
                    sp.dma_start(wp[:, par, :], w["wpair"][bass.ds(p, 1)].rearrange("a p f -> (a p) f")
                                 ).then_inc(s_w[par], 16)

                with sp.Fori(0, PAIRS // 2 - 1) as i:
                    more(2 * i + 2, 0)
                    more(2 * i + 3, 1)

            @block.tensor
            def _(pe):
                def slot(u):
                    pe.wait_ge(s_taken, u + 1)

                def make(p, par, u0, k0):
                    wv = wp[:, par, :]
                    pe.wait_ge(s_w[par], ((p - par) // 2 + 1) * 16 if isinstance(p, int) else (p - par) * 8 + 16)
                    slot(u0)
                    for c in range(NT):
                        last = pe.matmul(ring(k0)[:, c // 4, (c % 4) * P:(c % 4 + 1) * P], x[:, c * P:(c + 1) * P],
                                         wv[:, 256:384], start=True, stop=True, skip_group_check=True)
                    last.then_inc(s_unit, 1)
                    slot(u0 + 1)
                    for h in range(2):
                        last = pe.matmul(ring(k0 + 1)[:, h, :], wv[:, 384:512], half(x, h), start=True, stop=True)
                    last.then_inc(s_unit, 1)
                    for k in range(4):
                        slot(u0 + 2 + k)
                        for h in range(2):
                            last = pe.matmul(ring(k0 + k)[0:D0, h, :], wv[:, D0 * k:D0 * (k + 1)], half(x, h),
                                             start=True, stop=True)
                        last.then_inc(s_unit, 1)
                    for k in range(2):
                        slot(u0 + 6 + k)
                        pe.wait_ge(s_sq, 2 * p + k + 1)
                        for h in range(2):
                            last = pe.matmul(ring(k0 + k)[64:98, h, :], norms[:, :], half(sq, h), start=True, stop=True)
                        last.then_inc(s_unit, 1)
                    pe.wait_ge(s_taken, u0 + 10)
                    for k in range(2):
                        for c in range(NT):
                            slot(u0 + 8 + k * NT + c)
                            for h in range(2):
                                last = pe.matmul(ring(k0 + c)[:, h, :], K[:, k, c * P:(c + 1) * P],
                                                 Q[:, k, h * HALF:(h + 1) * HALF], start=True, stop=True)
                            last.then_inc(s_unit, 1)

                def use(p, par, u, k, first=False):
                    pe.wait_ge(s_exp, 2 * p + 2)
                    pe.wait_ge(s_h, p + 1)
                    for c in range(NT):
                        for h in range(2):
                            for k2 in range(2):
                                last = pe.matmul(PS[64 * k2:64 * k2 + 64, 4 + h, :], V[:, par, c, 64 * k2:64 * k2 + 64],
                                                 D[:, 2 * par + k2, c, h * HALF:(h + 1) * HALF],
                                                 start=(c == 0), stop=(c == NT - 1), skip_group_check=True)
                    last.then_inc(s_pv, 1)
                    slot(u)
                    pe.wait_ge(s_wsum, 2 * p + 4)
                    for h in range(2):
                        for k2 in range(2):
                            last = pe.matmul(ring(k)[64 * k2:64 * k2 + 64, h, :], ones[:, :],
                                             wsum[:, k2, h * HALF:(h + 1) * HALF], start=True, stop=True,
                                             skip_group_check=True)
                    last.then_inc(s_unit, 1)
                    pe.wait_ge(s_h, p + 2)
                    for h in range(2):
                        last = pe.matmul(PS[:, Y + h, :], wp[:, par, 512:640], half(H, h), start=first,
                                         stop=isinstance(p, int) and p == PAIRS - 1, skip_group_check=True)
                    last.then_inc(s_proj, 1)

                pe.wait_ge(s_const, 5 * 16)
                pe.wait_ge(s_set, 5)
                make(0, 0, 0, 0)

                def step(p, par, k, first=False):
                    u = MADE + BODY * p
                    make(p + 1, 1 - par, u, k)
                    use(p, par, u + MADE, k + MADE, first)

                step(0, 0, 0, True)
                with pe.Fori(0, PAIRS // 2 - 1) as i:
                    step(2 * i + 1, 1, 1)
                    step(2 * i + 2, 0, 0)
                use(PAIRS - 1, 1, MADE + BODY * (PAIRS - 1), 1)

            @block.vector
            def _(dve):
                dve.memset(ones[:, :], 1.0).then_inc(s_set, 1)
                dve.memset(eps[:, :], DIST_EPS).then_inc(s_set, 1)
                dve.memset(Q[:, :, :], 0.0).then_inc(s_set, 1)
                dve.memset(K[:, :, :], 0.0).then_inc(s_set, 1)
                dve.memset(PS[:, :, :], 0.0).then_inc(s_set, 1)
                dve.sem_inc(s_taken, 2)
                dve.sem_inc(s_wsum, 2)
                dve.sem_inc(s_pv, 1)
                dve.sem_inc(s_h, 1)
                dve.sem_inc(s_proj, 1)
                dve.wait_ge(s_const, 5 * 16)
                dve.wait_ge(s_set, 5)

                def take(p, par, u0, k0, own):
                    dve.wait_ge(s_pv, p)
                    dve.wait_ge(s_unit, u0 + 1)
                    dve.tensor_tensor(V[:, par, :, :], ring(k0).rearrange("q a (b c) -> q (a b) c", c=P),
                                      bv[:, bass.ds(p * P, P)].unsqueeze(1).to_broadcast([P, NT, P]), ALU.add
                                      ).then_inc(s_taken, 1)
                    dve.wait_ge(s_unit, u0 + 2)
                    dve.tensor_scalar(G[:, par, :], ring(k0 + 1).rearrange("q a b -> q (a b)"), bg[:, bass.ds(p, 1)],
                                      None, ALU.add).then_inc(s_taken, 1)
                    dve.wait_ge(s_unit, u0 + 1)
                    for k in range(2):
                        dve.wait_ge(s_unit, u0 + 3 + 2 * k)
                        dve.tensor_scalar(Q[0:D0, k, :], ring(k0)[0:D0].rearrange("q a b -> q (a b)"),
                                          bqk[:, bass.ds(4 * p + 2 * k, 1)], None, ALU.add).then_inc(s_taken, 1)
                        dve.wait_ge(s_unit, u0 + 4 + 2 * k)
                        dve.tensor_scalar(K[0:D0, k, :], ring(k0 + 1)[0:D0].rearrange("q a b -> q (a b)"),
                                          bqk[:, bass.ds(4 * p + 2 * k + 1, 1)], -2.0, ALU.add, ALU.mult
                                          ).then_inc(s_taken, 1)
                    for k in range(2):
                        dve.wait_ge(s_taken, u0 + 6 + 2 + k)
                        own.up(dve.tensor_tensor(sq[0:D0, :], Q[0:D0, k, :], Q[0:D0, k, :], ALU.mult))
                        own.done()
                        dve.tensor_tensor(sq[D0:P, :], K[0:D0, k, :], K[0:D0, k, :], ALU.mult).then_inc(s_sq, 1)
                        dve.wait_ge(s_unit, u0 + 7 + k)
                        own.up(dve.tensor_scalar(Q[64:66, k, :], ring(k0 + k)[64:66].rearrange("q a b -> q (a b)"),
                                                 rows[64:66, 0:1], None, ALU.add))
                        own.done()
                        dve.tensor_scalar(K[64:66, k, :], ring(k0 + k)[96:98].rearrange("q a b -> q (a b)"),
                                          rows[96:98, 1:2], None, ALU.add).then_inc(s_taken, 1)
                    for k in range(2):
                        for c in range(NT):
                            dve.wait_ge(s_unit, u0 + 9 + k * NT + c)
                            if k == 0 and c == 0:
                                dve.wait_ge(s_wsum, 2 * p)
                            dve.tensor_scalar(D[:, 2 * par + k, c, :], ring(k0 + c).rearrange("q a b -> q (a b)"), 0.0,
                                              None, ALU.max).then_inc(s_taken, 1)

                def finish(p, par, u, k, own):
                    dve.wait_ge(s_unit, u + 1)
                    dve.tensor_scalar(rec[:, :], ring(k).rearrange("q a b -> q (a b)"), DIST_EPS, None, ALU.add
                                      ).then_inc(s_taken, 1)
                    dve.wait_ge(s_taken, u + 3)
                    own.up(dve.reciprocal(rec[:, :], rec[:, :]))
                    own.done()
                    own.up(dve.tensor_tensor(rec[:, :], rec[:, :], G[:, par, :], ALU.mult))
                    own.done()
                    dve.wait_ge(s_pv, p + 2)
                    dve.wait_ge(s_proj, p + 1)
                    dve.tensor_tensor(H[:, :], PS[:, 4:6, :].rearrange("q a b -> q (a b)"), rec[:, :], ALU.mult
                                      ).then_inc(s_h, 1)
                    dve.wait_ge(s_h, p + 2)

                OWN = 4 + 2
                own = Count(dve, s_dve)
                take(0, 0, 0, 0, own)
                assert own.n == 4

                def step(p, par, k):
                    own = Count(dve, s_dve, 4 + OWN * p)
                    u = MADE + BODY * p
                    take(p + 1, 1 - par, u, k, own)
                    finish(p, par, u + MADE, k + MADE, own)
                    assert own.n == OWN

                step(0, 0, 0)
                with dve.Fori(0, PAIRS // 2 - 1) as i:
                    step(2 * i + 1, 1, 1)
                    step(2 * i + 2, 0, 0)
                p = PAIRS - 1
                finish(p, 1, MADE + BODY * p, 1, Count(dve, s_dve, 4 + OWN * p))

            @block.scalar
            def _(act):
                act.wait_ge(s_set, 5)

                def weights(p, par):
                    for k in range(2):
                        act.wait_ge(s_taken, BODY * p + 8 + NT * (k + 1) + 2)
                        act.activation(D[:, 2 * par + k, :, :], D[:, 2 * par + k, :, :], ACT.Sqrt).then_inc(s_act, 1)
                    for k in range(2):
                        act.wait_ge(s_act, 4 * p + 1 + k)
                        act.activation(D[:, 2 * par + k, :, :], D[:, 2 * par + k, :, :], ACT.Ln, bias=eps[:, 0:1]
                                       ).then_inc(s_act, 1)
                    for k in range(2):
                        act.wait_ge(s_act, 4 * p + 3 + k)
                        act.activation(D[:, 2 * par + k, :, :], D[:, 2 * par + k, :, :], ACT.Exp, scale=-2.0
                                       ).then_inc(s_exp, 1)

                with act.Fori(0, PAIRS // 2) as i:
                    weights(2 * i, 0)
                    weights(2 * i + 1, 1)

            @block.gpsimd
            def _(pool):
                def total(p, par):
                    for k in range(2):
                        pool.wait_ge(s_exp, 2 * p + k + 1)
                        pool.wait_ge(s_taken, BODY * p + 2)
                        W = D[:, 2 * par + k, :, :]
                        own = Count(pool, s_pool, (2 * p + k) * 6)
                        own.up(pool.tensor_tensor(wsum[:, k, :], W[:, 0, :], W[:, 1, :], ALU.add))
                        for c in range(2, NT - 1):
                            own.done()
                            own.up(pool.tensor_tensor(wsum[:, k, :], wsum[:, k, :], W[:, c, :], ALU.add))
                        own.done()
                        pool.tensor_tensor(wsum[:, k, :], wsum[:, k, :], W[:, NT - 1, :], ALU.add).then_inc(s_wsum, 1)

                with pool.Fori(0, PAIRS // 2) as i:
                    total(2 * i, 0)
                    total(2 * i + 1, 1)


def layer_norm(nc, PS, name, onesd, resid, to, Y=None, bias=None, keep=None, also=None, scale=None, shift=None):
    with ExitStack() as ctx:
        n = Names(nc, ctx, name)
        z = keep if keep is not None else n.sb("z", [P, T])
        sq = n.sb("sq", [P, T])
        d = n.sb("d", [P, T])
        r = n.sb("r", [P, T])
        eps = n.sb("eps", [P, 1])
        s_set, s_z, s_mean, s_d, s_sq, s_var, s_ln, s_r, s_m, s_out = (
            n.sem(k) for k in ("set", "z", "mean", "d", "sq", "var", "ln", "r", "m", "out"))
        free = [b for b in range(8) if Y is None or b not in (Y, Y + 1)]
        MEAN, VAR = free[0:2], free[2:4]
        src = z if Y is not None else resid

        with nc.Block() as block:
            @block.vector
            def _(dve):
                dve.memset(eps[:, :], LN_EPS).then_inc(s_set, 1)
                for h in range(2):
                    if Y is not None:
                        if bias is None:
                            dve.tensor_tensor(half(z, h), PS[:, Y + h, :], half(resid, h), ALU.add).then_inc(s_z, 1)
                        else:
                            dve.scalar_tensor_tensor(half(z, h), PS[:, Y + h, :], bias, half(resid, h), ALU.add, ALU.add
                                                     ).then_inc(s_z, 1)
                for h in range(2):
                    dve.wait_ge(s_mean, h + 1)
                    dve.tensor_tensor(half(d, h), half(src, h), PS[:, MEAN[h], :], ALU.subtract).then_inc(s_d, 1)
                if also is not None:
                    dve.wait_ge(s_z, 2)
                    dve.tensor_tensor(also[0][:, :], src[:, :], also[1][:, :], ALU.add).then_inc(s_out, 1)
                for h in range(2):
                    dve.wait_ge(s_r, h + 1)
                    dve.wait_ge(s_d, h + 1)
                    if scale is None:
                        dve.tensor_tensor(half(to, h), half(d, h), half(r, h), ALU.mult).then_inc(s_out, 1)
                    else:
                        dve.tensor_tensor(half(d, h), half(d, h), half(r, h), ALU.mult).then_inc(s_m, 1)
                        dve.wait_ge(s_m, h + 1)
                        dve.tensor_scalar(half(to, h), half(d, h), scale, shift, ALU.mult, ALU.add).then_inc(s_out, 1)

            @block.tensor
            def _(pe):
                for h in range(2):
                    if Y is not None:
                        pe.wait_ge(s_z, h + 1)
                    pe.matmul(PS[:, MEAN[h], :], onesd[:, :], half(src, h), start=True, stop=True).then_inc(s_mean, 1)
                for h in range(2):
                    pe.wait_ge(s_sq, h + 1)
                    pe.matmul(PS[:, VAR[h], :], onesd[:, :], half(sq, h), start=True, stop=True).then_inc(s_var, 1)

            @block.scalar
            def _(act):
                act.wait_ge(s_set, 1)
                for h in range(2):
                    act.wait_ge(s_d, h + 1)
                    act.activation(half(sq, h), half(d, h), ACT.Square).then_inc(s_sq, 1)
                for h in range(2):
                    act.wait_ge(s_var, h + 1)
                    act.activation(half(r, h), PS[:, VAR[h], :], ACT.Ln, bias=eps[:, 0:1]).then_inc(s_ln, 1)
                    act.wait_ge(s_ln, h + 1)
                    act.activation(half(r, h), half(r, h), ACT.Exp, scale=-0.5).then_inc(s_r, 1)


def context_mlp(nc, PS, x, w, Y, bad, kaux):
    RING = 3
    ITERS = NC // RING
    assert NC % RING == 0 and Y == 6
    with ExitStack() as ctx:
        n = Names(nc, ctx, "mlp")
        C = n.sb("C", [P, RING, 2 * P])
        A = n.sb("A", [P, RING, T])
        row = n.sb("row", [P, KEYS], I32)
        hidden0 = n.sb("hidden0", [P, KEYS], BF16)
        M = n.sb("M", [P, 2, KEYS], I32)
        differ = n.sb("differ", [P, KEYS], BF16)
        counts = n.sb("counts", [P, NT])
        kbias = n.sb("kbias", [1, KPAD], BF16)
        s_row, s_bias, s_aux = n.sem("row"), n.sem("bias"), n.sem("aux")
        s_mask, s_looked, s_dve = [n.sem("mask0"), n.sem("mask1")], n.sem("looked"), n.sem("dve")
        s_c = [n.sem(f"c{k}") for k in range(RING)]
        s_h, s_gelu, s_out = n.sem("h"), n.sem("gelu"), n.sem("out")

        with nc.Block() as block:
            @block.sync
            def _(sp):
                for k in range(RING):
                    sp.dma_start(C[:, k, :], w["ctx"][k]).then_inc(s_c[k], 16)
                with sp.Fori(1, ITERS) as i:
                    for k in range(RING):
                        sp.wait_ge(s_out, i * RING + k + 1)
                        sp.dma_start(C[:, k, :], w["ctx"][bass.ds(i * RING + k, 1)].rearrange("a p f -> (a p) f")
                                     ).then_inc(s_c[k], 16)

            @block.tensor
            def _(pe):
                pe.sem_inc(s_out, RING)

                def hidden(i, k):
                    c = i * RING + k
                    pe.wait_ge(s_c[k], i * 16 + 16)
                    pe.wait_ge(s_gelu, c + 1)
                    for h in range(2):
                        last = pe.matmul(PS[:, 2 * k + h, :], C[:, k, 0:P], half(x, h), start=True, stop=True)
                    last.then_inc(s_h, 1)

                def back(i, k, start=False, stop=False):
                    pe.wait_ge(s_gelu, i * RING + k + RING + 1)
                    for h in range(2):
                        last = pe.matmul(PS[:, Y + h, :], C[:, k, P:2 * P], A[:, k, h * HALF:(h + 1) * HALF],
                                         start=start, stop=stop, skip_group_check=True)
                    last.then_inc(s_out, 1)

                hidden(0, 0)
                for k in range(1, RING):
                    hidden(0, k)
                    back(0, k - 1, start=(k == 1))
                with pe.Fori(1, ITERS) as i:
                    for k in range(RING):
                        hidden(i, k)
                        back(i if k else i - 1, (k - 1) % RING)
                back(ITERS - 1, RING - 1, stop=True)

            @block.gpsimd
            def _(pool):
                pool.dma_start(row[:, :], w["mask"][0].partition_broadcast(P)).then_inc(s_row, 16)
                for t in range(NT):
                    if t >= 2:
                        pool.wait_ge(s_looked, t - 1)
                    pool.dma_start(M[:, t % 2, :], w["mask"][t * P:(t + 1) * P, :]).then_inc(s_mask[t % 2], 16)
                pool.dma_start(kaux[1:4, :], w["kaux"][1:4, :]).then_inc(s_aux, 16)
                pool.wait_ge(s_bias, 2)
                pool.dma_start(kaux[0:1, :], kbias[:, :]).then_inc(s_aux, 16)
                pool.wait_ge(s_aux, 32)

            @block.vector
            def _(dve):
                own = Count(dve, s_dve)
                dve.memset(kbias[:, KEYS:KPAD], PADDED).then_inc(s_bias, 1)
                own.up(dve.memset(bad[:, :], 0.0))
                dve.wait_ge(s_row, 16)
                own.up(dve.tensor_scalar(hidden0[:, :], row[:, :], 0, None, ALU.is_equal))
                own.done()
                dve.tensor_scalar(kbias[:, 0:KEYS], hidden0[0:1, :], MASKED, None, ALU.mult).then_inc(s_bias, 1)
                own.up(dve.tensor_reduce(bad[0:1, 1:2], hidden0[0:1, :], AX.X, ALU.add))
                own.done()
                own.up(dve.tensor_scalar(bad[0:1, 1:2], bad[0:1, 1:2], float(KEYS), None, ALU.is_equal))
                for t in range(NT):
                    dve.wait_ge(s_mask[t % 2], 16 * (t // 2 + 1))
                    if t:
                        dve.wait_ge(s_looked, t)
                    dve.scalar_tensor_tensor(differ[:, :], M[:, t % 2, :], 0.0, hidden0[:, :], ALU.is_equal, ALU.not_equal,
                                             accum_out=counts[:, t:t + 1]).then_inc(s_looked, 1)
                dve.wait_ge(s_looked, NT)
                own.up(dve.tensor_reduce(bad[:, 0:1], counts[:, :], AX.X, ALU.add))
                own.done()

            @block.scalar
            def _(act):
                act.sem_inc(s_gelu, RING)
                with act.Fori(0, ITERS) as i:
                    for k in range(RING):
                        act.wait_ge(s_h, i * RING + k + 1)
                        act.wait_ge(s_out, i * RING + k + 1)
                        act.activation(A[:, k, :], PS[:, 2 * k:2 * k + 2, :].rearrange("q a b -> q (a b)"),
                                       ACT.Gelu_apprx_tanh).then_inc(s_gelu, 1)


def routed_mlp(nc, PS, name, x, ident, w, func, weighted):
    Y = (4, 6)
    with ExitStack() as ctx:
        n = Names(nc, ctx, name)
        W = n.sb("W", [P, 2, 2 * FF])
        A = n.sb("A", [P, 2, T])
        acc = n.sb("acc", [P, NT, P])
        small = n.sb("small", [P, 320])
        wr = small[:, 0:EXPERTS]
        bias1 = small[:, EXPERTS:EXPERTS + EXPERTS * FC]
        o = 64
        routers = small[:, o:o + 64].rearrange("q (t e) -> q t e", e=EXPERTS)
        backward = small[:, o + 64:o + 128].rearrange("q (t e) -> q t e", e=EXPERTS)
        b2 = small[0:EXPERTS, o + 128:o + 256]
        L = n.sb("L", [P, NT, EXPERTS])
        E = n.sb("E", [P, NT, EXPERTS])
        top = n.sb("top", [P, NT, 1])
        G = n.sb("G", [P, NT, EXPERTS])
        GT = n.sb("GT", [EXPERTS, T])
        s_small, s_w = n.sem("small"), [n.sem("w0"), n.sem("w1")]
        s_logits, s_dve, s_e, s_gates, s_gt, s_gtc = (n.sem(k) for k in ("logits", "dve", "e", "gates", "gt", "gtc"))
        s_h, s_a, s_y, s_comb = (n.sem(k) for k in ("h", "a", "y", "comb"))

        def flat(t):
            return t.rearrange("q a b -> q (a b)")

        with nc.Block() as block:
            @block.sync
            def _(sp):
                sp.dma_start(small[:, 0:320], w["small"]).then_inc(s_small, 16)
                for e in range(2):
                    sp.dma_start(W[:, e, :], w["experts"][e]).then_inc(s_w[e], 16)
                with sp.Fori(1, EXPERTS // 2) as i:
                    for k in range(2):
                        sp.wait_ge(s_y, (2 * i + k - 1) * FC + 2)
                        sp.dma_start(W[:, k, :], w["experts"][bass.ds(2 * i + k, 1)].rearrange("a p f -> (a p) f")
                                     ).then_inc(s_w[k], 16)

            @block.tensor
            def _(pe):
                pe.sem_inc(s_y, 2)
                pe.wait_ge(s_small, 16)
                for t in range(NT):
                    last = pe.matmul(PS[:, 6, t * EXPERTS:(t + 1) * EXPERTS], x[:, t * P:(t + 1) * P], wr,
                                     start=True, stop=True, skip_group_check=True)
                last.then_inc(s_logits, 1)

                def hidden(e, k, f):
                    pe.wait_ge(s_a, e * FC + f + 1)
                    for h in range(2):
                        last = pe.matmul(PS[:, 2 * (f % 2) + h, :], W[:, k, f * P:(f + 1) * P], half(x, h),
                                         start=True, stop=True)
                    last.then_inc(s_h, 1)

                def back(e, k, f):
                    pe.wait_ge(s_a, e * FC + f + 3)
                    if f == 0:
                        pe.wait_ge(s_comb, e * NT + NT)
                    for t in range(NT):
                        last = pe.matmul(PS[:, Y[k] + t // 4, (t % 4) * P:(t % 4 + 1) * P],
                                         A[:, f % 2, t * P:(t + 1) * P], W[:, k, FF + f * P:FF + (f + 1) * P],
                                         start=(f == 0 and t % 4 == 0), stop=(f == FC - 1), skip_group_check=True)
                    last.then_inc(s_y, 1)

                def expert(e, k, first=False):
                    pe.wait_ge(s_w[k], ((e - k) // 2 + 1) * 16 if isinstance(e, int) else (e - k) * 8 + 16)
                    for f in range(FC):
                        hidden(e, k, f)
                        if f:
                            back(e, k, f - 1)
                        elif not first:
                            back(e - 1, 1 - k, FC - 1)

                expert(0, 0, True)
                pe.wait_ge(s_gates, 1)
                expert(1, 1)
                with pe.Fori(1, EXPERTS // 2) as i:
                    expert(2 * i, 0)
                    expert(2 * i + 1, 1)
                back(EXPERTS - 1, 1, FC - 1)
                if weighted:
                    for t in range(NT):
                        last = pe.transpose(PS[0:EXPERTS, 2 + t // 4, (t % 4) * P:(t % 4 + 1) * P], G[:, t, :], ident[:, :])
                    last.then_inc(s_gt, 1)
                pe.wait_ge(s_comb, EXPERTS * NT + NT)
                for t in range(NT):
                    last = pe.matmul(PS[:, t // 4, (t % 4) * P:(t % 4 + 1) * P], acc[:, t, :], ident[:, :],
                                     start=(t % 4 == 0), stop=not weighted, skip_group_check=True)
                if weighted:
                    pe.wait_ge(s_gtc, 1)
                    for h in range(2):
                        pe.matmul(PS[:, h, :], b2, half(GT, h), start=False, stop=True, skip_group_check=True)

            @block.scalar
            def _(act):
                act.sem_inc(s_a, 2)
                if weighted:
                    act.wait_ge(s_dve, 4)
                    act.activation(flat(E), flat(E), ACT.Exp).then_inc(s_e, 1)
                act.wait_ge(s_small, 16)

                def activate(e, f):
                    act.wait_ge(s_h, e * FC + f + 1)
                    act.wait_ge(s_y, e * FC + f + 1)
                    of = flat(PS[:, 2 * (f % 2):2 * (f % 2) + 2, :])
                    if weighted:
                        act.activation(A[:, f % 2, :], of, func, bias=bias1[:, bass.ds(e * FC + f, 1)]).then_inc(s_a, 1)
                    else:
                        act.activation(A[:, f % 2, :], of, func).then_inc(s_a, 1)

                with act.Fori(0, EXPERTS) as e:
                    for f in range(FC):
                        activate(e, f)

            @block.vector
            def _(dve):
                own = Count(dve, s_dve)
                dve.sem_inc(s_comb, NT)
                own.up(dve.memset(acc[:, :, :], 0.0))
                dve.wait_ge(s_logits, 1)
                dve.wait_ge(s_small, 16)
                all8 = [P, NT, EXPERTS]
                own.up(dve.tensor_tensor(L[:, :, :], PS[:, 6, 0:NT * EXPERTS].rearrange("q (t e) -> q t e", e=EXPERTS),
                                         routers, ALU.add))
                own.done()
                own.up(dve.tensor_reduce(top[:, :, 0], L[:, :, :], AX.X, ALU.max))
                own.done()
                own.up(dve.tensor_tensor(E[:, :, :], L[:, :, :], top[:, :, :].to_broadcast(all8), ALU.subtract))
                own.done()
                own.up(dve.tensor_tensor(L[:, :, :], L[:, :, :], top[:, :, :].to_broadcast(all8), ALU.is_equal))
                own.done()
                own.up(dve.tensor_tensor(L[:, :, :], L[:, :, :], backward, ALU.mult))
                own.done()
                own.up(dve.tensor_reduce(top[:, :, 0], L[:, :, :], AX.X, ALU.max))
                own.done()
                gates = dve.tensor_tensor(G[:, :, :], L[:, :, :], top[:, :, :].to_broadcast(all8), ALU.is_equal)
                if weighted:
                    own.up(gates)
                    dve.wait_ge(s_e, 1)
                    own.done()
                    own.up(dve.tensor_reduce(top[:, :, 0], E[:, :, :], AX.X, ALU.add))
                    own.done()
                    own.up(dve.reciprocal(top[:, :, 0], top[:, :, 0]))
                    own.done()
                    gates = dve.tensor_tensor(G[:, :, :], G[:, :, :], top[:, :, :].to_broadcast(all8), ALU.mult)
                gates.then_inc(s_gates, 1)
                dve.wait_ge(s_gates, 1)
                own.done()

                def combine(e, k):
                    dve.wait_ge(s_y, e * FC + FC + 2)
                    dve.wait_ge(s_comb, e * NT + NT)
                    for t in range(NT):
                        dve.scalar_tensor_tensor(acc[:, t, :], PS[:, Y[k] + t // 4, (t % 4) * P:(t % 4 + 1) * P],
                                                 flat(G)[:, bass.ds(e + t * EXPERTS, 1)], acc[:, t, :], ALU.mult, ALU.add
                                                 ).then_inc(s_comb, 1)

                with dve.Fori(0, EXPERTS // 2) as i:
                    combine(2 * i, 0)
                    combine(2 * i + 1, 1)
                if weighted:
                    dve.wait_ge(s_gt, 1)
                    dve.tensor_copy(GT[:, :], flat(PS[0:EXPERTS, 2:4, :])).then_inc(s_gtc, 1)


NARROW_BLOCKS = [[(i, j) for j in range(3) for i in range(3)]]
WIDE_BLOCKS = [[(0, 0), (0, 1), (1, 0)], [(1, 1), (0, 2), (2, 0)]]


def when(eng, flag, value):
    return nullcontext() if flag is None else eng.If(eng.value_load(flag[0:1, 0:1], min_val=0, max_val=1) == value)


def attention(nc, PS, name, w, wide, cus, scale, maxes, V, out, ident, identb, flag=None):
    d = D1 if wide else D8
    blocks = WIDE_BLOCKS if wide else NARROW_BLOCKS
    tiles = len(blocks)
    B = len(blocks[0]) * d
    per = 2 if wide else 1
    nk = w["k"].shape[2]
    loads = 16 * (sum(2 * len(b) for b in blocks) + 2 + (0 if maxes else 1))
    MU = 2 * 4 * NT
    with ExitStack() as ctx:
        n = Names(nc, ctx, name)
        Q = [n.sb(f"Q{b}", [P, tiles, 4, T], BF16) for b in range(2)]
        K = [n.sb(f"K{b}", [P, tiles, 4, nk], BF16) for b in range(2)]
        E = n.sb("E", [P, 2, 4, T])
        vst = n.sb("vst", [P, 2, per, 4, 32])
        ones = n.sb("ones", [P, 32])
        O = n.sb("O", [P, T])
        rc = n.sb("rc", [P, HALF])
        mx = n.sb("mx", [P, 2, 4, NT])
        mr = n.sb("mr", [P, 2, 4 * NT])
        mb = n.sb("mb", [P, 3, 4 * NT], BF16)
        mt = n.sb("mt", [P, P], BF16)
        s_set = n.sem("set")
        s_ld = [n.sem("ld0"), n.sem("ld1")]
        s_mr = [n.sem("mr0"), n.sem("mr1")]
        s_mw = n.sem("mw")
        s_s = n.sem("s")
        s_e = n.sem("e")
        s_pv = n.sem("pv")
        s_v = n.sem("v")
        s_acc = n.sem("acc")
        s_m = n.sem("m")
        s_mt = n.sem("mt")
        s_mb = n.sem("mb")
        s_tm = n.sem("tm")
        s_mc = n.sem("mc")
        s_to = n.sem("to")
        s_ot = n.sem("ot")
        s_dve = n.sem("dve")

        def flat(t):
            return t.rearrange("q a b -> q (a b)")

        def passes(eng, body):
            def run(at):
                body(1, (at + 1) % 2, True)
                pairs = (cus - 2) // 2
                if pairs > 1:
                    with eng.Fori(0, pairs) as i:
                        body(2 * i + 2, at % 2, False)
                        body(2 * i + 3, (at + 1) % 2, False)
                elif pairs:
                    body(2, at % 2, False)
                    body(3, (at + 1) % 2, False)
                if cus % 2:
                    body(cus - 1, (at + cus - 1) % 2, False)
            return run

        with nc.Block() as block:
            @block.sync
            def _(sp):
              with when(sp, flag, 1):
                sp.wait_ge(s_set, 5)

                def load(g):
                    b = g % 2
                    if g >= 2:
                        sp.wait_ge(s_s, (g - 1) * per * cus * 4)
                    rows = slice(g * 4 * d, (g + 1) * 4 * d)
                    for tile, bl in enumerate(blocks):
                        for r, (i, j) in enumerate(bl):
                            for to, of, part in ((Q[b], w["q"], i), (K[b], w["k"], j)):
                                sp.dma_start(to[r * d:(r + 1) * d, tile, :, :],
                                             of[part, rows, :].rearrange("(j i) t -> i j t", i=d)).then_inc(s_ld[b], 16)
                    sp.dma_start(K[b][B:B + 4, 0, :, :], w["kaux"].unsqueeze(1).to_broadcast([4, 4, nk])
                                 ).then_inc(s_ld[b], 16)
                    if maxes:
                        sp.dma_start(Q[b][B:B + 4, 0, :, :], w["qaux"].unsqueeze(1).to_broadcast([4, 4, T])
                                     ).then_inc(s_ld[b], 16)
                    else:
                        sp.dma_start(Q[b][B:B + 1, 0, :, :], w["qaux"][0:1].unsqueeze(1).to_broadcast([1, 4, T])
                                     ).then_inc(s_ld[b], 16)
                        sp.dma_start(Q[b][B + 1:B + 4, 0, :, :], w["mrow"][:, 4 * g:4 * g + 4, :]).then_inc(s_ld[b], 16)

                def maxima(g):
                    b = g % 2
                    sp.wait_ge(s_mc, g + 1)
                    sp.dma_start(w["mrow"][g], mt[0:3 * 4 * NT, :]).then_inc(s_mw, 16)
                    sp.wait_ge(s_mw, 16 * (g + 1))
                    sp.wait_ge(s_ld[b], (g // 2 + 1) * loads)
                    sp.wait_ge(s_m, MU * (g + 1))
                    sp.dma_start(Q[b][B + 1:B + 4, 0, :, :],
                                 w["mrow"][g].rearrange("(r j t) p -> r j (t p)", r=3, j=4)).then_inc(s_mr[b], 16)

                load(0)
                load(1)
                for g in range(GROUPS):
                    if maxes:
                        maxima(g)
                    if g + 2 < GROUPS:
                        load(g + 2)

            @block.tensor
            def _(pe):
              with when(pe, flag, 1):
                pe.sem_inc(s_pv, 2)
                pe.wait_ge(s_set, 5)

                def max_unit(g, j, t):
                    b = g % 2
                    if j == 0:
                        if g >= 1:
                            pe.wait_ge(s_mc, g)
                        if g >= 2 and not wide:
                            pe.wait_ge(s_ot, 2 * (g - 1))
                    for h in range(2):
                        pe.wait_ge(s_mt, g * MU + (t * 4 + j) * 2 + h + 1)
                        pe.matmul(PS[:, 4 + h, :], Q[b][:, 0, j, bass.ds(t * P, P)],
                                  K[b][:, 0, j, h * HALF:(h + 1) * HALF], start=True, stop=True).then_inc(s_m, 1)

                def turn_maxima(g):
                    pe.wait_ge(s_mb, g + 1)
                    pe.transpose(PS[:, 4, :].bitcast(BF16)[0:3 * 4 * NT, 0:P], flat(mb), identb[:, :]).then_inc(s_tm, 1)

                def turn_output(g):
                    pe.wait_ge(s_acc, g + 2)
                    if maxes and g + 1 < GROUPS:
                        pe.wait_ge(s_mc, g + 2)
                    elif g >= 1:
                        pe.wait_ge(s_ot, 2 * g)
                    for h in range(2):
                        for t in range(4):
                            last = pe.transpose(PS[:, 4 + h, t * P:(t + 1) * P],
                                                O[:, (4 * h + t) * P:(4 * h + t + 1) * P], ident[:, :])
                        last.then_inc(s_to, 1)

                def scores(sg, cu, j):
                    g, qh = sg // per, sg % per
                    pe.wait_ge(s_e, (sg * cus + cu) * 4 + j + 1)
                    for s in range(2):
                        key, q = (2 * cu + s, qh * HALF) if wide else (cu, s * HALF)
                        for tile in range(tiles):
                            last = pe.matmul(PS[:, 2 * (j % 2) + s, :], K[g % 2][:, tile, j, bass.ds(key * P, P)],
                                             Q[g % 2][:, tile, j, q:q + HALF], start=(tile == 0), stop=(tile == tiles - 1))
                    last.then_inc(s_s, 1)
                    if maxes and g + 1 < GROUPS:
                        if j == 0 and qh == 0 and isinstance(cu, int) and cu == 0:
                            pe.wait_ge(s_ld[1 - g % 2], ((g + 1) // 2 + 1) * loads)
                        max_unit(g + 1, j, qh * cus + cu if wide else cu)

                def values(gc, s, par, start, stop):
                    if s == 0:
                        pe.wait_ge(s_e, gc * 4 + 4 + 2)
                        pe.wait_ge(s_v, gc + 1)
                    src = [E[:, par, j, s * HALF:(s + 1) * HALF] for j in range(4)]
                    for j in range(4):
                        last = pe.matmul(PS[32 * j:32 * j + 32, 6 if wide else 6 + s, :], vst[:, par, s if wide else 0, j, :],
                                         src[j], start=start and not (wide and s), stop=stop, skip_group_check=True)
                    if wide:
                        for j in range(4):
                            last = pe.matmul(PS[32 * j:32 * j + 32, 7, :], ones[:, :], src[j],
                                             start=start and s == 0, stop=stop, skip_group_check=True)
                    if s == 1:
                        last.then_inc(s_pv, 1)

                if maxes:
                    pe.wait_ge(s_ld[0], loads)
                    with pe.Fori(0, NT) as t:
                        for j in range(4):
                            max_unit(0, j, t)
                    turn_maxima(0)

                for sg in range(GROUPS * per):
                    g = sg // per
                    if sg % per == 0:
                        pe.wait_ge(s_ld[g % 2], (g // 2 + 1) * loads)
                        if maxes:
                            pe.wait_ge(s_mr[g % 2], (g // 2 + 1) * 16)
                    for j in range(4):
                        scores(sg, 0, j)
                    pe.wait_ge(s_acc, sg + 1)

                    def body(cu, par, first):
                        gc = sg * cus + cu
                        for j in range(4):
                            scores(sg, cu, j)
                            if j % 2:
                                values(gc - 1, j // 2, 1 - par, first, False)

                    passes(pe, body)(sg * cus)
                    last_gc = sg * cus + cus - 1
                    for s in range(2):
                        values(last_gc, s, last_gc % 2, False, True)
                    if maxes and sg % per == per - 1 and g + 1 < GROUPS:
                        turn_maxima(g + 1)
                    if not wide:
                        turn_output(g)

            @block.scalar
            def _(act):
              with when(act, flag, 1):
                act.sem_inc(s_e, 2)
                for sg in range(GROUPS * per):
                    def unit(cu, par, first=False):
                        gc = sg * cus + cu
                        act.wait_ge(s_pv, gc + 1)
                        for j in range(4):
                            act.wait_ge(s_s, gc * 4 + j + 1)
                            act.activation(E[:, par, j, :], flat(PS[:, 2 * (j % 2):2 * (j % 2) + 2, :]), ACT.Exp,
                                           scale=scale).then_inc(s_e, 1)
                    unit(0, sg * cus % 2)
                    passes(act, unit)(sg * cus)

            @block.vector
            def _(dve):
              with when(dve, flag, 1):
                own = Count(dve, s_dve)
                dve.sem_inc(s_acc, 1)
                dve.sem_inc(s_mt, 2)
                for t in Q:
                    dve.memset(flat(t.rearrange("q a b c -> q (a b) c") if tiles > 1 else t[:, 0]), 0.0).then_inc(s_set, 1)
                for t in K:
                    dve.memset(flat(t.rearrange("q a b c -> q (a b) c") if tiles > 1 else t[:, 0]), 0.0).then_inc(s_set, 1)
                own.up(dve.memset(vst[:, :, :, :, :].rearrange("q a b c e -> q (a b c e)"), 1.0))
                dve.memset(ones[:, :], 1.0).then_inc(s_set, 1)
                own.done()

                def reduce(g, j, t):
                    for h in range(2):
                        dve.wait_ge(s_m, g * MU + (t * 4 + j) * 2 + h + 1)
                        dve.tensor_reduce(mx[:, h, j, bass.ds(t, 1)], PS[:, 4 + h, :], AX.X, ALU.max).then_inc(s_mt, 1)

                def parts(g):
                    m = [mx[:, h, :, :].rearrange("q a b -> q (a b)") for h in range(2)]
                    dve.wait_ge(s_mt, (g + 1) * MU + 2)
                    own.up(dve.tensor_tensor(mr[:, 0, :], m[0], m[1], ALU.max))
                    own.done()
                    if g:
                        dve.wait_ge(s_tm, g)
                    own.up(dve.tensor_scalar(mb[:, 0, :], mr[:, 0, :], -1.0, None, ALU.mult))
                    own.done()
                    own.up(dve.scalar_tensor_tensor(mr[:, 1, :], mr[:, 0, :], -1.0, mb[:, 0, :], ALU.mult, ALU.subtract))
                    own.done()
                    own.up(dve.tensor_copy(mb[:, 1, :], mr[:, 1, :]))
                    own.done()
                    own.up(dve.tensor_tensor(mr[:, 0, :], mr[:, 1, :], mb[:, 1, :], ALU.subtract))
                    own.done()
                    dve.tensor_copy(mb[:, 2, :], mr[:, 0, :]).then_inc(s_mb, 1)
                    dve.wait_ge(s_tm, g + 1)
                    if g:
                        dve.wait_ge(s_mw, 16 * g)
                    dve.tensor_copy(mt[0:3 * 4 * NT, :], PS[:, 4, :].bitcast(BF16)[0:3 * 4 * NT, 0:P]).then_inc(s_mc, 1)

                if maxes:
                    with dve.Fori(0, NT) as t:
                        for j in range(4):
                            reduce(0, j, t)
                    parts(0)

                for sg in range(GROUPS * per):
                    g, qh = sg // per, sg % per

                    def unit(cu, par, first=False):
                        gc = sg * cus + cu
                        dve.wait_ge(s_pv, gc + 1)
                        if wide:
                            of = V[:, bass.ds(2 * cu, 2), g * P:(g + 1) * P]
                            dve.tensor_copy(vst[:, par, :, :, :].rearrange("q a b c -> q a (b c)"), of).then_inc(s_v, 1)
                        else:
                            of = V[:, bass.ds(cu, 1), g * 32:(g + 1) * 32].rearrange("q a (b c) -> q (a b) c", c=D8)
                            dve.tensor_copy(vst[:, par, 0, :, 0:D8], of).then_inc(s_v, 1)
                        if maxes and g + 1 < GROUPS:
                            for j in range(4):
                                reduce(g + 1, j, qh * cus + cu if wide else cu)

                    unit(0, sg * cus % 2)
                    passes(dve, unit)(sg * cus)
                    if wide:
                        dve.wait_ge(s_pv, (sg + 1) * cus + 2)
                        own.up(dve.reciprocal(rc[:, :], PS[:, 7, :]))
                        own.done()
                        dve.tensor_tensor(out[:, g, qh * HALF:(qh + 1) * HALF], PS[:, 6, :], rc[:, :], ALU.mult
                                          ).then_inc(s_acc, 1)
                    else:
                        if g:
                            dve.wait_ge(s_to, 2 * g)
                        dve.wait_ge(s_pv, (sg + 1) * cus + 2)
                        dve.tensor_copy(O[:, :], flat(PS[:, 6:8, :])).then_inc(s_acc, 1)
                    if maxes and qh == per - 1 and g + 1 < GROUPS:
                        parts(g + 1)
                    if not wide:
                        for h in range(2):
                            dve.wait_ge(s_to, 2 * g + h + 1)
                            turned = PS[:, 4 + h, :].rearrange("q (t j c) -> q t j c", t=4, c=32)
                            r = rc[:, 0:16].rearrange("q (t j c) -> q t j c", t=4, c=1)
                            own.up(dve.reciprocal(r, turned[:, :, :, D8:D8 + 1]))
                            own.done()
                            dve.tensor_tensor(
                                out[:, 4 * h:4 * h + 4, g * 32:(g + 1) * 32].rearrange("q t (j c) -> q t j c", c=D8),
                                turned[:, :, :, 0:D8], r.to_broadcast([P, 4, 4, D8]), ALU.mult).then_inc(s_ot, 1)
                            dve.wait_ge(s_ot, 2 * g + h + 1)


def project(nc, PS, name, weight, H, groups, ident=None):
    with ExitStack() as ctx:
        n = Names(nc, ctx, name)
        HT = n.sb("HT", [P, T])
        s_t, s_c, s_p = n.sem("t"), n.sem("c"), n.sem("p")
        with nc.Block() as block:
            @block.tensor
            def _(pe):
                if ident is not None:
                    for t in range(NT):
                        last = pe.transpose(PS[:, 2 + t // 4, (t % 4) * P:(t % 4 + 1) * P], H[:, t, :], ident[:, :])
                    last.then_inc(s_t, 1)
                    pe.wait_ge(s_c, 1)
                for h in range(2):
                    for g in range(groups):
                        of = half(HT, h) if ident is not None else H[:, g, h * HALF:(h + 1) * HALF]
                        pe.matmul(PS[:, h, :], weight[:, g * P:(g + 1) * P], of, start=(g == 0), stop=(g == groups - 1)
                                  ).then_inc(s_p, 1)

            @block.vector
            def _(dve):
                if ident is not None:
                    dve.wait_ge(s_t, 1)
                    dve.tensor_copy(HT[:, :], PS[:, 2:4, :].rearrange("q a b -> q (a b)")).then_inc(s_c, 1)


def rotary_operands(nc, PS, name, x, w, V, wo):
    OPS = 2 * GROUPS
    with ExitStack() as ctx:
        n = Names(nc, ctx, name)
        W = n.sb("W", [P, 2, 2 * P])
        C = n.sb("C", [P, 2, 2, T])
        wv = n.sb("wv", [P, HALF])
        wo2 = n.sb("wo2", [P, 2, HALF])
        A = n.sb("A", [P, 2, T])
        R = n.sb("R", [P, 2, T])
        parts = n.sb("parts", [P, 2, 3, T], BF16)
        s_w, s_v = [n.sem("w0"), n.sem("w1")], n.sem("v")
        s_eo, s_ta = n.sem("eo"), n.sem("ta")
        s_vals, s_dve, s_act, s_sum = n.sem("vals"), n.sem("dve"), n.sem("act"), n.sem("sum")
        s_rest, s_st = n.sem("rest"), [n.sem("st0"), n.sem("st1")]

        def flat(t):
            return t.rearrange("q a b -> q (a b)")

        with nc.Block() as block:
            @block.sync
            def _(sp):
                sp.dma_start(wv[:, :], w["wv"]).then_inc(s_v, 16)
                sp.dma_start(wo2[:, :, :], w["wo2"]).then_inc(s_v, 16)
                for o in range(OPS):
                    b = o % 2
                    if o >= 2:
                        sp.wait_ge(s_ta, 2 * (o - 1))
                    sp.dma_start(W[:, b, :], w["weq"][o]).then_inc(s_w[b], 16)
                    sp.dma_start(C[:, b, :, :], w["tables"][o]).then_inc(s_w[b], 16)

            @block.gpsimd
            def _(pool):
                for o in range(OPS):
                    to = w["k"] if o >= GROUPS else w["q"]
                    g = o % GROUPS
                    pool.wait_ge(s_act, 3 * o + 3)
                    pool.dma_start(to[:, g * P:(g + 1) * P, :].rearrange("r f t -> f r t"), parts[:, o % 2, :, :]
                                   ).then_inc(s_st[o % 2], 16)
                for b in range(2):
                    pool.wait_ge(s_st[b], 16 * OPS // 2)

            @block.tensor
            def _(pe):
                pe.wait_ge(s_v, 32)
                for o in range(OPS):
                    b = o % 2
                    pe.wait_ge(s_w[b], 32 * (o // 2 + 1))
                    for eo in range(2):
                        if o:
                            pe.wait_ge(s_ta, 2 * o - 1 + eo)
                        for h in range(2):
                            last = pe.matmul(PS[:, 2 * eo + h, :], W[:, b, eo * P:(eo + 1) * P], half(x, h),
                                             start=True, stop=True)
                        last.then_inc(s_eo, 1)
                for c in range(NT):
                    if c >= 4:
                        pe.wait_ge(s_vals, c - 3)
                    pe.matmul(PS[:, 4 + c % 4, :], x[:, c * P:(c + 1) * P], wv[:, :], start=True, stop=True).then_inc(s_sum, 1)

            @block.scalar
            def _(act):
                for o in range(OPS):
                    b = o % 2
                    act.wait_ge(s_rest, 3 * o + 1)
                    if o >= 2:
                        act.wait_ge(s_st[b], 16 * (o // 2))
                    act.activation(parts[:, b, 0, :], A[:, 0, :], ACT.Copy).then_inc(s_act, 1)
                    for r in range(2):
                        act.wait_ge(s_rest, 3 * o + 2 + r)
                        act.activation(parts[:, b, r + 1, :], R[:, r, :], ACT.Copy).then_inc(s_act, 1)

            @block.vector
            def _(dve):
                own = Count(dve, s_dve)
                for o in range(OPS):
                    b = o % 2
                    if o:
                        dve.wait_ge(s_act, 3 * o)
                        dve.wait_ge(s_rest, 3 * o)
                    for eo in range(2):
                        dve.wait_ge(s_eo, 2 * o + eo + 1)
                        dve.tensor_tensor(A[:, eo, :], flat(PS[:, 2 * eo:2 * eo + 2, :]), C[:, b, eo, :], ALU.mult
                                          ).then_inc(s_ta, 1)
                    dve.wait_ge(s_ta, 2 * o + 2)
                    dve.tensor_tensor(A[:, 0, :], A[:, 0, :], A[:, 1, :], ALU.add).then_inc(s_rest, 1)
                    dve.wait_ge(s_act, 3 * o + 1)
                    dve.wait_ge(s_rest, 3 * o + 1)
                    dve.tensor_tensor(R[:, 0, :], A[:, 0, :], parts[:, b, 0, :], ALU.subtract).then_inc(s_rest, 1)
                    dve.wait_ge(s_act, 3 * o + 2)
                    dve.wait_ge(s_rest, 3 * o + 2)
                    dve.tensor_tensor(R[:, 1, :], R[:, 0, :], parts[:, b, 1, :], ALU.subtract).then_inc(s_rest, 1)
                for c in range(NT):
                    dve.wait_ge(s_sum, c + 1)
                    dve.tensor_copy(V[:, c, :], PS[:, 4 + c % 4, :]).then_inc(s_vals, 1)
                dve.tensor_tensor(wo[:, :], wo2[:, 0, :], wo2[:, 1, :], ALU.add).then_inc(s_vals, 1)
                dve.wait_ge(s_vals, NT + 1)


def plain_operands(nc, PS, name, x, weights, q, k, V, wproj):
    with ExitStack() as ctx:
        n = Names(nc, ctx, name)
        R = n.sb("R", [P, 2, 3, T])
        parts = n.sb("parts", [P, 2, 3, T], BF16)
        W = n.sb("W", [P, 3 * P])
        s_w, s_qk, s_act, s_rest, s_v, s_vals, s_st = (n.sem(t) for t in ("w", "qk", "act", "rest", "v", "vals", "st"))

        with nc.Block() as block:
            @block.sync
            def _(sp):
                sp.dma_start(W[:, :], weights[:, 0:3 * P]).then_inc(s_w, 16)
                sp.dma_start(wproj[:, :], weights[:, 3 * P:4 * P]).then_inc(s_w, 16)
                for o, to in enumerate((q, k)):
                    sp.wait_ge(s_act, 3 * o + 3)
                    sp.dma_start(to.rearrange("r f t -> f r t"), parts[:, o, :, :]).then_inc(s_st, 16)
                sp.wait_ge(s_st, 32)

            @block.tensor
            def _(pe):
                pe.wait_ge(s_w, 32)
                for o in range(2):
                    for h in range(2):
                        last = pe.matmul(PS[:, 2 * o + h, :], W[:, o * P:(o + 1) * P], half(x, h), start=True, stop=True)
                    last.then_inc(s_qk, 1)
                for c in range(NT):
                    last = pe.matmul(PS[:, 4 + c // 4, (c % 4) * P:(c % 4 + 1) * P], x[:, c * P:(c + 1) * P],
                                     W[:, 2 * P:3 * P], start=True, stop=True, skip_group_check=True)
                last.then_inc(s_v, 1)

            @block.scalar
            def _(act):
                for o in range(2):
                    for r in range(3):
                        if r == 0:
                            act.wait_ge(s_rest, 3 * o + 1)
                        else:
                            act.wait_ge(s_rest, 3 * o + 1 + r)
                        act.activation(parts[:, o, r, :], R[:, o, r, :], ACT.Copy).then_inc(s_act, 1)

            @block.vector
            def _(dve):
                for o in range(2):
                    dve.wait_ge(s_qk, o + 1)
                    dve.tensor_copy(R[:, o, 0, :], PS[:, 2 * o:2 * o + 2, :].rearrange("q a b -> q (a b)")).then_inc(s_rest, 1)
                    for r in range(1, 3):
                        dve.wait_ge(s_act, 3 * o + r)
                        dve.wait_ge(s_rest, 3 * o + r)
                        dve.tensor_tensor(R[:, o, r, :], R[:, o, r - 1, :], parts[:, o, r - 1, :], ALU.subtract
                                          ).then_inc(s_rest, 1)
                dve.wait_ge(s_v, 1)
                dve.tensor_copy(V[:, :, :], PS[:, 4:6, :].rearrange("q a (b c) -> q (a b) c", c=P)).then_inc(s_vals, 1)
                dve.wait_ge(s_vals, 1)


def rotary_attention(nc, PS, x, a, ident, identb):
    with ExitStack() as ctx:
        n = Names(nc, ctx, "rot")
        V = n.sb("V", [P, NT, HALF])
        wo = n.sb("wo", [P, HALF])
        H = n.sb("H", [P, GROUPS, T])
        w = {"q": nc.dram_tensor("rot_q", (3, HALF, T), BF16).ap(), "k": nc.dram_tensor("rot_k", (3, HALF, T), BF16).ap(),
             "mrow": nc.dram_tensor("rot_m", (GROUPS, 3 * 4 * NT, P), BF16).ap(),
             "weq": a["rot_w"], "tables": a["rot_tables"], "wv": a["rot_wv"], "wo2": a["rot_wo"],
             "qaux": a["qaux"], "kaux": a["kaux"][:, 0:T]}
        rotary_operands(nc, PS, "rotop", x, w, V, wo)
        attention(nc, PS, "rotat", w, True, NT // 2, 0.5, True, V, H, ident, identb)
        project(nc, PS, "rotpr", wo, H, GROUPS)


CROSS_SCALE = 1.0 / float(np.sqrt(np.float32(P)))


def cross_operands(nc, PS, name, x, w, q, k, mrow, V, wo, bad, flag):
    STEPS = NC // 3
    W3 = 3 * P
    with ExitStack() as ctx:
        n = Names(nc, ctx, name)
        W = n.sb("W", [P, 3 * P])
        heads = n.sb("heads", [P, HEADS])
        C = n.sb("C", [P, 2, 3, P])
        R = n.sb("R", [P, 2, 2, W3])
        kp = n.sb("kp", [P, 3, KPAD], BF16)
        kmax = n.sb("kmax", [P, STEPS + 1])
        kh = n.sb("kh", [P, HEADS])
        qf = n.sb("qf", [P, 3, T])
        qa = n.sb("qa", [P, T])
        qp = n.sb("qp", [P, 3, T], BF16)
        bf = n.sb("bf", [HEADS, 2, T])
        bp = n.sb("bp", [HEADS, 3, T], BF16)
        one = n.sb("one", [P, 1])
        total = n.sb("total", [1, 2])
        s_w, s_c = n.sem("w"), [n.sem("c0"), n.sem("c1")]
        s_kv, s_act, s_rest = n.sem("kv"), n.sem("act"), n.sem("rest")
        s_q, s_qp, s_qr, s_qa, s_st = (n.sem(t) for t in ("q", "qp", "qr", "qa", "st"))
        s_kh, s_bound, s_b, s_bad, s_sum, s_dve = (n.sem(t) for t in ("kh", "bound", "b", "bad", "sum", "dve"))

        def flat(t):
            return t.rearrange("q a b -> q (a b)")

        def steps(eng, body):
            with eng.Fori(0, STEPS // 2) as i:
                body(2 * i, 0)
                body(2 * i + 1, 1)
            body(STEPS - 1, 0)

        assert STEPS % 2 == 1
        with nc.Block() as block:
            @block.sync
            def _(sp):
                sp.dma_start(W[:, :], w["cross_w"]).then_inc(s_w, 16)
                sp.dma_start(heads[:, :], w["heads"]).then_inc(s_w, 16)
                sp.dma_start(wo[:, :], w["cross_wo"]).then_inc(s_w, 16)

                def load(i, b):
                    sp.wait_ge(s_kv, i + 1)
                    sp.dma_start(C[:, b, :, :], w["ctx"][bass.ds(3 * i, 3), :, 0:P].rearrange("c p f -> p c f")
                                 ).then_inc(s_c[b], 16)

                steps(sp, load)
                sp.wait_ge(s_qp, 3)
                sp.dma_start(q.rearrange("r f t -> f r t"), qp[:, :, :]).then_inc(s_st, 16)
                sp.wait_ge(s_act, 3 * STEPS)
                sp.dma_start(k.rearrange("r f t -> f r t"), kp[:, :, :]).then_inc(s_st, 16)
                sp.wait_ge(s_b, 5)
                sp.dma_start(mrow.rearrange("r h t -> h r t"), bp[:, :, :]).then_inc(s_st, 16)
                sp.wait_ge(s_st, 48)

            @block.tensor
            def _(pe):
                pe.sem_inc(s_kv, 2)
                pe.wait_ge(s_w, 48)
                for h in range(2):
                    last = pe.matmul(PS[:, 4 + h, :], W[:, 2 * P:3 * P], half(x, h), start=True, stop=True)
                last.then_inc(s_q, 1)

                def product(i, b):
                    pe.wait_ge(s_c[b], (i - b) * 8 + 16)
                    pe.wait_ge(s_rest, 2 * i + 1)
                    pe.matmul(PS[:, b, 0:W3], W[:, 0:P], flat(C[:, b, :, :]), start=True, stop=True)
                    for c in range(3):
                        last = pe.matmul(PS[:, 2 + b, c * P:(c + 1) * P], C[:, b, c, :], W[:, P:2 * P],
                                         start=True, stop=True, skip_group_check=True)
                    last.then_inc(s_kv, 1)

                steps(pe, product)
                pe.wait_ge(s_kh, 1)
                pe.wait_ge(s_qa, 1)
                for h in range(2):
                    last = pe.matmul(PS[0:HEADS, 6 + h, :], kh[:, :], half(qa, h), start=True, stop=True)
                last.then_inc(s_bound, 1)
                pe.wait_ge(s_bad, 1)
                pe.matmul(PS[0:1, 0, 0:3], one[:, :], bad[:, 0:3], start=True, stop=True).then_inc(s_sum, 1)

            @block.scalar
            def _(act):
                for r in range(3):
                    act.wait_ge(s_qr, r + 1)
                    act.activation(qp[:, r, :], qf[:, r, :], ACT.Copy).then_inc(s_qp, 1)
                act.activation(qa[:, :], qf[:, 0, :], ACT.Abs).then_inc(s_qa, 1)

                def parts(i, b):
                    at = bass.ds(i * W3, W3)
                    act.wait_ge(s_kv, i + 3)
                    act.activation(kp[:, 0, at], PS[:, b, 0:W3], ACT.Copy).then_inc(s_act, 1)
                    for r in range(2):
                        act.wait_ge(s_rest, 2 * i + r + 5)
                        act.activation(kp[:, r + 1, at], R[:, b, r, :], ACT.Copy).then_inc(s_act, 1)

                steps(act, parts)

            @block.vector
            def _(dve):
                own = Count(dve, s_dve)
                dve.sem_inc(s_rest, 4)
                own.up(dve.memset(one[:, :], 1.0))
                dve.wait_ge(s_q, 1)
                dve.tensor_copy(qf[:, 0, :], flat(PS[:, 4:6, :])).then_inc(s_qr, 1)
                for r in range(2):
                    dve.wait_ge(s_qp, r + 1)
                    dve.wait_ge(s_qr, r + 1)
                    dve.tensor_tensor(qf[:, r + 1, :], qf[:, r, :], qp[:, r, :], ALU.subtract).then_inc(s_qr, 1)

                def rest(i, b):
                    at = bass.ds(i * W3, W3)
                    dve.wait_ge(s_kv, i + 3)
                    dve.tensor_copy(V[:, bass.ds(3 * i, 3), :], PS[:, 2 + b, 0:W3].rearrange("q (c f) -> q c f", f=P))
                    dve.wait_ge(s_act, 3 * i + 1)
                    dve.tensor_reduce(kmax[:, bass.ds(i, 1)], PS[:, b, 0:W3], AX.X, ALU.max, apply_absolute_value=True)
                    dve.tensor_tensor(R[:, b, 0, :], PS[:, b, 0:W3], kp[:, 0, at], ALU.subtract).then_inc(s_rest, 1)
                    dve.wait_ge(s_rest, 2 * i + 5)
                    dve.wait_ge(s_act, 3 * i + 2)
                    dve.tensor_tensor(R[:, b, 1, :], R[:, b, 0, :], kp[:, 1, at], ALU.subtract).then_inc(s_rest, 1)

                steps(dve, rest)
                dve.wait_ge(s_rest, 2 * STEPS + 4)
                own.up(dve.tensor_reduce(kmax[:, STEPS:STEPS + 1], kmax[:, 0:STEPS], AX.X, ALU.max))
                own.done()
                dve.tensor_scalar(kh[:, :], heads[:, :], kmax[:, STEPS:STEPS + 1], None, ALU.mult).then_inc(s_kh, 1)
                dve.wait_ge(s_bound, 1)
                bounds = flat(PS[0:HEADS, 6:8, :])
                dve.tensor_scalar(bp[:, 0, :], bounds, -1.0, None, ALU.mult).then_inc(s_b, 1)
                own.up(dve.tensor_reduce(bad[0:HEADS, 2:3], bounds, AX.X, ALU.max))
                dve.wait_ge(s_b, 1)
                dve.scalar_tensor_tensor(bf[:, 0, :], bounds, -1.0, bp[:, 0, :], ALU.mult, ALU.subtract).then_inc(s_b, 1)
                dve.wait_ge(s_b, 2)
                dve.tensor_copy(bp[:, 1, :], bf[:, 0, :]).then_inc(s_b, 1)
                dve.wait_ge(s_b, 3)
                dve.tensor_tensor(bf[:, 1, :], bf[:, 0, :], bp[:, 1, :], ALU.subtract).then_inc(s_b, 1)
                dve.wait_ge(s_b, 4)
                dve.tensor_copy(bp[:, 2, :], bf[:, 1, :]).then_inc(s_b, 1)
                own.done()
                dve.tensor_scalar(bad[0:HEADS, 2:3], bad[0:HEADS, 2:3], BOUND_LIMIT / CROSS_SCALE, None, ALU.is_gt
                                  ).then_inc(s_bad, 1)
                dve.wait_ge(s_sum, 1)
                own.up(dve.tensor_reduce(total[:, 0:1], PS[0:1, 0, 0:3], AX.X, ALU.add))
                own.done()
                own.up(dve.tensor_scalar(flag[:, :], total[:, 0:1], 0.0, None, ALU.is_equal))
                own.done()


def cross_general(nc, PS, name, w, V, out, ident, flag):
    STEPS = NC // 3
    W3 = 3 * P
    B = 9 * D8
    with ExitStack() as ctx:
        n = Names(nc, ctx, name)
        Q = n.sb("Q", [P, 4, T], BF16)
        K = n.sb("K", [P, 4, KPAD], BF16)
        mask = n.sb("mask", [P, KEYS], I32)
        bias = n.sb("bias", [P, KPAD])
        S = n.sb("S", [P, KPAD])
        E = n.sb("E", [P, 2, W3])
        ET = n.sb("ET", [P, 2, W3])
        ones = n.sb("ones", [P, D8])
        top = n.sb("top", [P, 1])
        rec = n.sb("rec", [P, 1])
        s_set, s_ld, s_mask = n.sem("set"), n.sem("ld"), n.sem("mask")
        s_bias = n.sem("bias")
        s_s, s_add = n.sem("s"), n.sem("add")
        s_top, s_sub = n.sem("top"), n.sem("sub")
        s_e, s_t, s_tc = n.sem("e"), n.sem("t"), n.sem("tc")
        s_pv = n.sem("pv")
        s_rec = n.sem("rec")
        s_o = n.sem("o")

        def steps(eng, body):
            body(0, 0)
            with eng.Fori(0, STEPS // 2) as i:
                body(2 * i + 1, 1)
                body(2 * i + 2, 0)

        def tiles(eng, body, before=None):
            with eng.Fori(0, GROUPS) as g:
                if before is not None:
                    before(g)
                with eng.Fori(0, NT) as t:
                    body(g, t)

        loads = 16 * 2 * len(NARROW_BLOCKS[0])
        with nc.Block() as block:
            @block.sync
            def _(sp):
              with when(sp, flag, 0):
                sp.wait_ge(s_set, 4)

                def load(g):
                    sp.wait_ge(s_o, g * (NT * 4) + 1)
                    for r, (i, j) in enumerate(NARROW_BLOCKS[0]):
                        for to, of, part in ((Q, w["q"], i), (K, w["k"], j)):
                            sp.dma_start(to[r * D8:(r + 1) * D8, :, :],
                                         of[part, bass.ds(g * 32, 32), :].rearrange("(j i) t -> i j t", i=D8)
                                         ).then_inc(s_ld, 16)

                def masks(g, t):
                    sp.wait_ge(s_bias, g * NT + t + 1)
                    sp.dma_start(mask[:, :], w["mask"][bass.ds(t * P, P), :]).then_inc(s_mask, 16)

                tiles(sp, masks, load)

            @block.tensor
            def _(pe):
              with when(pe, flag, 0):
                pe.sem_inc(s_pv, 2)
                pe.sem_inc(s_t, 2)

                def tile(g, t):
                    pe.wait_ge(s_ld, g * loads + loads)
                    for j in range(4):
                        u = (g * NT + t) * 4 + j
                        pe.wait_ge(s_add, u * STEPS + 2)

                        def scores(i, b):
                            pe.wait_ge(s_add, u * STEPS + i + 1)
                            pe.matmul(PS[:, b, 0:W3], Q[:, j, bass.ds(t * P, P)], K[:, j, bass.ds(i * W3, W3)],
                                      start=True, stop=True).then_inc(s_s, 1)

                        steps(pe, scores)
                        pe.wait_ge(s_o, u + 1)

                        def weigh(i, b):
                            pe.wait_ge(s_e, u * STEPS + i + 3)
                            pe.wait_ge(s_tc, u * STEPS + i + 1)
                            for c in range(3):
                                last = pe.transpose(PS[:, 2 + b, c * P:(c + 1) * P], E[:, b, c * P:(c + 1) * P], ident[:, :])
                            last.then_inc(s_t, 1)
                            pe.wait_ge(s_tc, u * STEPS + i + 3)
                            first = isinstance(i, int)
                            for c in range(3):
                                of = ET[:, b, c * P:(c + 1) * P]
                                pe.matmul(PS[:, 6, 0:D8], of, V[:, bass.ds(3 * i + c, 1), bass.ds(g * 32 + j * D8, D8)
                                                                ].rearrange("q a b -> q (a b)"),
                                          start=first and c == 0, stop=False, skip_group_check=True)
                                last = pe.matmul(PS[:, 7, 0:D8], of, ones[:, :], start=first and c == 0, stop=False,
                                                 skip_group_check=True)
                            last.then_inc(s_pv, 1)

                        steps(pe, weigh)

                tiles(pe, tile)

            @block.scalar
            def _(act):
              with when(act, flag, 0):
                act.sem_inc(s_e, 2)

                def tile(g, t):
                    for j in range(4):
                        u = (g * NT + t) * 4 + j
                        act.wait_ge(s_sub, u + 1)
                        act.wait_ge(s_t, u * STEPS + 2)

                        def exponentials(i, b):
                            act.wait_ge(s_t, u * STEPS + i + 1)
                            act.activation(E[:, b, :], S[:, bass.ds(i * W3, W3)], ACT.Exp, scale=CROSS_SCALE).then_inc(s_e, 1)

                        steps(act, exponentials)

                tiles(act, tile)

            @block.vector
            def _(dve):
              with when(dve, flag, 0):
                dve.sem_inc(s_add, 2)
                dve.sem_inc(s_tc, 2)
                dve.sem_inc(s_o, 1)
                dve.sem_inc(s_bias, 1)
                dve.memset(Q.rearrange("q a b -> q (a b)"), 0.0).then_inc(s_set, 1)
                dve.memset(K.rearrange("q a b -> q (a b)"), 0.0).then_inc(s_set, 1)
                dve.memset(ones[:, :], 1.0).then_inc(s_set, 1)
                dve.memset(bias[:, KEYS:KPAD], PADDED).then_inc(s_set, 1)
                dve.wait_ge(s_set, 4)

                def tile(g, t):
                    dve.wait_ge(s_mask, (g * NT + t) * 16 + 16)
                    dve.tensor_scalar(bias[:, 0:KEYS], mask[:, :], 0, MASKED, ALU.is_equal, ALU.mult).then_inc(s_bias, 1)
                    dve.wait_ge(s_bias, g * NT + t + 2)
                    for j in range(4):
                        u = (g * NT + t) * 4 + j
                        dve.wait_ge(s_e, u * STEPS + 2)

                        def add(i, b):
                            at = bass.ds(i * W3, W3)
                            dve.wait_ge(s_s, u * STEPS + i + 1)
                            dve.tensor_tensor(S[:, at], PS[:, b, 0:W3], bias[:, at], ALU.add).then_inc(s_add, 1)

                        steps(dve, add)
                        dve.wait_ge(s_add, u * STEPS + STEPS + 2)
                        dve.tensor_reduce(top[:, :], S[:, :], AX.X, ALU.max).then_inc(s_top, 1)
                        dve.wait_ge(s_top, u + 1)
                        dve.tensor_scalar(S[:, :], S[:, :], top[:, 0:1], None, ALU.subtract).then_inc(s_sub, 1)
                        dve.wait_ge(s_pv, u * STEPS + 2)

                        def copy(i, b):
                            dve.wait_ge(s_t, u * STEPS + i + 3)
                            dve.wait_ge(s_pv, u * STEPS + i + 1)
                            dve.tensor_copy(ET[:, b, :], PS[:, 2 + b, 0:W3]).then_inc(s_tc, 1)

                        steps(dve, copy)
                        dve.wait_ge(s_pv, u * STEPS + STEPS + 2)
                        dve.reciprocal(rec[:, :], PS[:, 7, 0:1]).then_inc(s_rec, 1)
                        dve.wait_ge(s_rec, u + 1)
                        dve.tensor_scalar(out[:, bass.ds(t, 1), bass.ds(g * 32 + j * D8, D8)].rearrange("q a b -> q (a b)"),
                                          PS[:, 6, 0:D8], rec[:, 0:1], None, ALU.mult).then_inc(s_o, 1)

                tiles(dve, tile)
                dve.wait_ge(s_o, GROUPS * NT * 4 + 1)


def cross_attention(nc, PS, x, a, bad, kaux, ident, identb):
    with ExitStack() as ctx:
        n = Names(nc, ctx, "cross")
        V = n.sb("V", [P, NC, P])
        H = n.sb("H", [P, NT, P])
        wo = n.sb("wo", [P, P])
        flag = n.sb("flag", [1, 1], I32)
        q = nc.dram_tensor("cross_q", (3, P, T), BF16).ap()
        k = nc.dram_tensor("cross_k", (3, P, KPAD), BF16).ap()
        mrow = nc.dram_tensor("cross_m", (3, HEADS, T), BF16).ap()
        w = {"q": q, "k": k, "qaux": a["qaux"], "kaux": kaux, "mrow": mrow, "mask": a["mask"]}
        cross_operands(nc, PS, "crop", x, a, q, k, mrow, V, wo, bad, flag)
        attention(nc, PS, "crat", w, False, NC, CROSS_SCALE, False, V, H, ident, identb, flag=flag)
        cross_general(nc, PS, "crgen", w, V, H, ident, flag)
        project(nc, PS, "crpr", wo, H, 1, ident)


def last_block(nc, PS, x, a, onesd, ident, identb, cols):
    with ExitStack() as ctx:
        n = Names(nc, ctx, "last")
        normed = n.sb("normed", [P, T])
        xa = n.sb("xa", [P, T])
        xxa = n.sb("xxa", [P, T])
        layer_norm(nc, PS, "lastn1", onesd, x, normed, scale=cols[:, 2:3], shift=cols[:, 3:4])
        with ExitStack() as inner:
            m = Names(nc, inner, "lastat")
            V = m.sb("V", [P, NT, P])
            H = m.sb("H", [P, NT, P])
            wproj = m.sb("wproj", [P, P])
            w = {"q": nc.dram_tensor("last_q", (3, P, T), BF16).ap(), "k": nc.dram_tensor("last_k", (3, P, T), BF16).ap(),
                 "mrow": nc.dram_tensor("last_m", (GROUPS, 3 * 4 * NT, P), BF16).ap(),
                 "qaux": a["qaux"], "kaux": a["kaux"][:, 0:T]}
            plain_operands(nc, PS, "lastop", normed, a["last_w"], w["q"], w["k"], V, wproj)
            attention(nc, PS, "lastat", w, False, NT, 1.0 / float(np.sqrt(D8)), True, V, H, ident, identb)
            project(nc, PS, "lastpr", wproj, H, 1, ident)
        layer_norm(nc, PS, "lastn2", onesd, x, normed, Y=0, keep=xa, also=(xxa, x), scale=cols[:, 4:5], shift=cols[:, 5:6])
        routed_mlp(nc, PS, "moe1", normed, ident, {"small": a["small1"], "experts": a["experts1"]}, ACT.Gelu_apprx_tanh, False)
        layer_norm(nc, PS, "ln6", onesd, xxa, x, Y=0)
def decoder(nc, a, out):
    with ExitStack() as ctx:
        n = Names(nc, ctx, "all")
        PS = ctx.enter_context(nc.psum_tensor("banks", [P, 8, HALF], F32))
        x = n.sb("x", [P, T])
        onesd = n.sb("onesd", [P, P])
        ident = n.sb("ident", [P, P])
        identb = n.sb("identb", [P, P], BF16)
        cols = n.sb("cols", [P, 8])
        bad = n.sb("bad", [P, 4])
        kaux = nc.dram_tensor("cross_kaux", (4, KPAD), BF16).ap()
        s_in, s_mem = n.sem("in"), n.sem("mem")
        with nc.Block() as block:
            @block.sync
            def _(sp):
                sp.dma_start(x[:, :], a["xT"]).then_inc(s_in, 16)
                sp.dma_start(ident[:, :], a["ident"]).then_inc(s_in, 16)
                sp.dma_start(identb[:, :], a["identb"]).then_inc(s_in, 16)
                sp.dma_start(cols[:, :], a["cols"]).then_inc(s_in, 16)
                sp.wait_ge(s_in, 64)

            @block.vector
            def _(dve):
                dve.memset(onesd[:, :], 1.0 / P).then_inc(s_mem, 1)
                dve.wait_ge(s_mem, 1)

        distance_attention(nc, PS, x, a, 6)
        layer_norm(nc, PS, "ln1", onesd, x, x, Y=6, bias=cols[:, 0:1])
        context_mlp(nc, PS, x, a, 6, bad, kaux)
        layer_norm(nc, PS, "ln2", onesd, x, x, Y=6)
        routed_mlp(nc, PS, "moe0", x, ident, {"small": a["small0"], "experts": a["experts0"]}, ACT.Relu, True)
        layer_norm(nc, PS, "ln3", onesd, x, x, Y=0)
        rotary_attention(nc, PS, x, a, ident, identb)
        layer_norm(nc, PS, "ln4", onesd, x, x, Y=0)
        cross_attention(nc, PS, x, a, bad, kaux, ident, identb)
        layer_norm(nc, PS, "ln5", onesd, x, x, Y=0, bias=cols[:, 1:2])
        last_block(nc, PS, x, a, onesd, ident, identb, cols)
        s_out = n.sem("stored")
        with nc.Block() as block:
            @block.sync
            def _(sp):
                sp.dma_start(out, x[:, :]).then_inc(s_out, 16)
                sp.wait_ge(s_out, 16)


def _columns(*vectors):
    a = np.zeros((P, 8), np.float32)
    for i, v in enumerate(vectors):
        a[:, i] = v
    return a


def _context(c):
    c = np.concatenate([c, np.zeros((KPAD - KEYS, P), c.dtype)]).reshape(NC, P, P)
    return np.concatenate([c.transpose(0, 2, 1), c], axis=2)


def _experts(w1, w2):
    w2 = w2.reshape(EXPERTS, FC, P, P).transpose(0, 2, 1, 3).reshape(EXPERTS, P, FF)
    return np.concatenate([w1, w2], axis=2)


def _small(router_w, router_b, b1=None, b2=None):
    a = np.zeros((P, 320), np.float32)
    a[:, 0:EXPERTS] = router_w
    a[:, 64:128] = np.broadcast_to(router_b, (NT, EXPERTS)).reshape(1, 64)
    a[:, 128:192] = np.broadcast_to(np.arange(EXPERTS, 0, -1), (NT, EXPERTS)).reshape(1, 64)
    if b1 is not None:
        a[:, EXPERTS:EXPERTS + EXPERTS * FC] = b1.reshape(EXPERTS * FC, P).T
        a[0:EXPERTS, 192:320] = b2
    return a


def _angles(width):
    theta = np.float32(1) / np.power(1250.0, np.arange(0, width, 2) / width).astype(np.float32)
    angle = (theta[:, None] * np.arange(1, T + 1, dtype=np.float32)[None, :]).astype(np.float64)
    return np.cos(angle), np.sin(angle)


def _rotary(wq, wk, wv, wo):
    cos, sin = _angles(2 * HALF)
    weights = [np.stack([wq[:, 0::2], wq[:, 1::2]])]
    tables = [np.stack([cos + sin, cos - sin])]
    cos, sin = (np.repeat(t, 2, axis=0) for t in _angles(HALF))
    odd = (np.arange(HALF) % 2 == 1)[:, None]
    weights.append(np.stack([np.repeat(wk[:, 0::2], 2, axis=1), np.repeat(wk[:, 1::2], 2, axis=1)]))
    tables.append(np.stack([np.where(odd, sin, cos), np.where(odd, cos, -sin)]))
    weights = np.stack(weights).reshape(2, 2, P, GROUPS, P).transpose(0, 3, 2, 1, 4).reshape(2 * GROUPS, P, 2 * P)
    tables = np.stack(tables).astype(np.float32).reshape(2, 2, GROUPS, P, T).transpose(0, 2, 3, 1, 4)
    wo = wo.reshape(GROUPS, P, 2, P).transpose(1, 2, 0, 3).reshape(P, 2, HALF)
    return {"rot_w": weights, "rot_tables": tables.reshape(2 * GROUPS, P, 2, T), "rot_wv": wv, "rot_wo": wo}


def _cross(wk, wv, wq, wo):
    blocks = np.zeros((P, 3, P), wk.dtype)
    heads = np.zeros((P, HEADS), np.float32)
    for h in range(HEADS):
        at = slice(h * D8, (h + 1) * D8)
        for i, m in enumerate((wk, wv, wq)):
            blocks[at, i, at] = m.T
        heads[at, h] = 1.0
    return {"cross_w": blocks.reshape(P, 3 * P), "cross_wo": wo.T, "heads": heads}


def _aux():
    bf16 = mybir.dt.np(BF16)
    return {"qaux": np.repeat(np.array([[1], [0], [0], [0]]), T, axis=1).astype(bf16),
            "kaux": np.repeat(np.array([[0], [1], [1], [1]]), KPAD, axis=1).astype(bf16),
            "identb": np.eye(P).astype(bf16)}


def _layout(inputs):
    f = {k: np.asarray(v) for k, v in inputs.items()}
    W = f["L0_attn_W_in"].reshape(P, PAIRS, 2, 4, D0)
    wpair = np.concatenate([W[:, :, 0, 0], W[:, :, 0, 1], W[:, :, 1, 0], W[:, :, 1, 1], W[:, :, 0, 2], W[:, :, 1, 2],
                            W[:, :, 0, 3], W[:, :, 1, 3]], axis=2).transpose(1, 0, 2)
    wpair = np.concatenate([wpair, f["L0_attn_W_out"].reshape(PAIRS, P, P)], axis=2)
    b = f["L0_attn_b_in"].reshape(HEADS, 4, D0)
    norms = np.zeros((P, 34), np.float32)
    norms[0:D0, 1] = 1.0
    norms[D0:P, 32] = 0.25
    rows = np.zeros((P, 2), np.float32)
    rows[64, 0] = rows[97, 1] = 1.0
    a = {
        "xT": f["x"][0].T,
        "ident": np.eye(P, dtype=np.float32),
        "cols": _columns(f["L0_attn_b_out"], f["L1_xattn_bo"], f["L1_ffn_ln1_w"], f["L1_ffn_ln1_b"],
                         f["L1_ffn_ln2_w"], f["L1_ffn_ln2_b"]),
        "wpair": wpair,
        "bqk": b[:, 0:2].transpose(2, 0, 1).reshape(D0, HEADS * 2),
        "bg": b[:, 3].reshape(PAIRS, P).T,
        "bv": np.broadcast_to(b[:, 2].reshape(1, T), (P, T)),
        "norms": norms,
        "rows": rows,
        "ctx": _context(f["ctx_1024"][0]),
        "small0": _small(f["L0_ffn_router_W"], f["L0_ffn_router_b"], f["L0_ffn_b1"], f["L0_ffn_b2"]),
        "experts0": _experts(f["L0_ffn_W1"], f["L0_ffn_W2"]),
        "small1": _small(f["L1_ffn_gate_w"], f["L1_ffn_gate_b"]),
        "experts1": _experts(f["L1_ffn_w1"], f["L1_ffn_w2"]),
        **_rotary(f["L1_attn_Wq"], f["L1_attn_Wk"], f["L1_attn_Wv"], f["L1_attn_Wo"]),
        **_aux(),
        **_cross(f["L1_xattn_Wk"], f["L1_xattn_Wv"], f["L1_xattn_Wq"], f["L1_xattn_Wo"]),
        "mask": f["mask_1x1xSxS2_ik1"][0, 0],
        "last_w": np.concatenate([f["L1_ffn_w_qkv"], f["L1_ffn_w_proj"]], axis=1),
    }
    return {k: np.ascontiguousarray(v) for k, v in a.items()}


def kernel(**inputs):
    import concourse.bacc as bacc
    from concourse.bass_utils import run_bass_kernel_spmd

    nc = bacc.Bacc("TRN2", target_bir_lowering=False, num_devices=1)
    arrays = {f"in_{k}": v for k, v in _layout(inputs).items()}
    aps = {k[3:]: nc.dram_tensor(k, v.shape, mybir.dt.from_np(v.dtype), kind="ExternalInput").ap() for k, v in arrays.items()}
    out = nc.dram_tensor("out_T", (P, T), F32, kind="ExternalOutput").ap()
    decoder(nc, aps, out)
    r = run_bass_kernel_spmd(nc, [arrays], core_ids=[0])
    return np.ascontiguousarray(r.results[0]["out_T"].T).reshape(1, T, P)
```

```python
from contextlib import ExitStack, nullcontext

import numpy as np

import concourse.bass as bass
from concourse import mybir
from concourse.alu_op_type import AluOpType as ALU

F32 = mybir.dt.float32
BF16 = mybir.dt.bfloat16
I32 = mybir.dt.int32
ACT = mybir.ActivationFunctionType
AX = mybir.AxisListType

P = 128
T = 1024
HALF = 512
NT = T // P
KEYS = 6404
NC = -(-KEYS // P)
KPAD = NC * P
HEADS = 16
GROUPS = HEADS // 4
PAIRS = HEADS // 2
D0 = 64
D1 = 32
D8 = 8
EXPERTS = 8
FF = 512
FC = FF // P
LN_EPS = 1e-5
DIST_EPS = 1e-4
MASKED = -1e20
PADDED = -1e38
BOUND_LIMIT = 30.0


class Names:

    def __init__(self, nc, ctx, stage):
        self.nc, self.ctx, self.stage, self.sems = nc, ctx, stage, []
        ctx.callback(self.clear)

    def sem(self, name):
        self.sems.append(self.nc.alloc_semaphore(f"{self.stage}_{name}"))
        return self.sems[-1]

    def sb(self, name, shape, dt=F32):
        return self.ctx.enter_context(self.nc.sbuf_tensor(f"{self.stage}_{name}", shape, dt))

    def clear(self):
        if self.sems:
            with self.nc.Block() as block:
                @block.gpsimd
                def _(pool):
                    self.nc.clear_and_free_semaphores(self.sems)


class Count:

    def __init__(self, eng, sem, base=0):
        self.eng, self.sem, self.base, self.n = eng, sem, base, 0

    def up(self, ins):
        ins.then_inc(self.sem, 1)
        self.n += 1

    def done(self):
        self.eng.wait_ge(self.sem, self.base + self.n)


def half(ap, h):
    return ap[:, h * HALF:(h + 1) * HALF]


def distance_attention(nc, PS, x, w, Y):
    MADE = 6 + 2 * NT
    BODY = MADE + 1
    with ExitStack() as ctx:
        n = Names(nc, ctx, "dist")
        wp = n.sb("wp", [P, 2, 4 * P])
        wout = n.sb("wout", [P, PAIRS, P])
        bqk = n.sb("bqk", [P, HEADS])
        bg = n.sb("bg", [P, PAIRS])
        bv = n.sb("bv", [P, PAIRS * P])
        Q = n.sb("Q", [P, 2, T])
        K = n.sb("K", [P, 2, T])
        sq = n.sb("sq", [P, 2, T])
        V = n.sb("V", [P, 2, NT, P])
        G = n.sb("G", [P, 2, T])
        D = n.sb("D", [P, 4, NT, T])
        wsum = n.sb("wsum", [P, 2, T])
        ones = n.sb("ones", [P, D0])
        eps = n.sb("eps", [P, 1])
        rec = n.sb("rec", [P, T])
        wost = n.sb("wost", [P, 2, P])
        H = n.sb("H", [P, T])
        norms = n.sb("norms", [P, 34])
        rows = n.sb("rows", [P, 2])
        s_const, s_set = n.sem("const"), n.sem("set")
        s_w = [n.sem("w0"), n.sem("w1")]
        s_unit = n.sem("unit")
        s_taken = n.sem("taken")
        s_sq = n.sem("sq")
        s_dve = n.sem("dve")
        s_act = n.sem("act")
        s_exp = n.sem("exp")
        s_wsum = n.sem("wsum")
        s_pool = n.sem("pool")
        s_pv = n.sem("pv")
        s_h = n.sem("h")
        s_proj = n.sem("proj")

        def ring(u):
            return PS[:, 2 * (u % 2):2 * (u % 2) + 2, :]

        def total(eng, own, to, W):
            own.up(eng.tensor_tensor(to, W[:, 0, :], W[:, 1, :], ALU.add))
            for c in range(2, NT - 1):
                own.done()
                own.up(eng.tensor_tensor(to, to, W[:, c, :], ALU.add))
            own.done()
            eng.tensor_tensor(to, to, W[:, NT - 1, :], ALU.add).then_inc(s_wsum, 1)

        with nc.Block() as block:
            @block.sync
            def _(sp):
                sp.dma_start(wp[:, 0, :], w["wpair"][0]).then_inc(s_w[0], 16)
                for to, of in ((bqk, "bqk"), (bg, "bg"), (bv, "bv"), (norms, "norms"), (rows, "rows")):
                    sp.dma_start(to[:, :], w[of]).then_inc(s_const, 16)
                sp.dma_start(wp[:, 1, :], w["wpair"][1]).then_inc(s_w[1], 16)
                sp.dma_start(wout[:, :, :], w["wout"]).then_inc(s_const, 16)

                def more(p, par):
                    sp.wait_ge(s_unit, BODY * p - 2 * BODY + 6)
                    sp.dma_start(wp[:, par, :], w["wpair"][bass.ds(p, 1)].rearrange("a p f -> (a p) f")
                                 ).then_inc(s_w[par], 16)

                with sp.Fori(0, PAIRS // 2 - 1) as i:
                    more(2 * i + 2, 0)
                    more(2 * i + 3, 1)

            @block.tensor
            def _(pe):
                def slot(u):
                    pe.wait_ge(s_taken, u + 1)

                def make(p, par, u0, k0, weigh, project):
                    wv = wp[:, par, :]
                    pe.wait_ge(s_w[par], ((p - par) // 2 + 1) * 16 if isinstance(p, int) else (p - par) * 8 + 16)
                    for k in range(2):
                        slot(u0 + k)
                        for h in range(2):
                            last = pe.matmul(ring(k0 + k)[:, h, :], wv[:, P * k:P * (k + 1)], half(x, h),
                                             start=True, stop=True)
                        last.then_inc(s_unit, 1)
                    if weigh is not None:
                        weigh()
                    for k in range(2):
                        slot(u0 + 2 + k)
                        pe.wait_ge(s_sq, 2 * p + k + 1)
                        for h in range(2):
                            last = pe.matmul(ring(k0 + k)[64:98, h, :], norms[:, :], sq[:, k, h * HALF:(h + 1) * HALF],
                                             start=True, stop=True)
                        last.then_inc(s_unit, 1)
                    if project is not None:
                        project()
                    slot(u0 + 4)
                    for c in range(NT):
                        last = pe.matmul(ring(k0)[:, c // 4, (c % 4) * P:(c % 4 + 1) * P], x[:, c * P:(c + 1) * P],
                                         wv[:, 256:384], start=True, stop=True, skip_group_check=True)
                    last.then_inc(s_unit, 1)
                    slot(u0 + 5)
                    for h in range(2):
                        last = pe.matmul(ring(k0 + 1)[:, h, :], wv[:, 384:512], half(x, h), start=True, stop=True)
                    last.then_inc(s_unit, 1)
                    pe.wait_ge(s_taken, u0 + 4 + 2)
                    for k in range(2):
                        for c in range(NT):
                            slot(u0 + 6 + k * NT + c)
                            for h in range(2):
                                last = pe.matmul(ring(k0 + c)[:, h, :], K[:, k, c * P:(c + 1) * P],
                                                 Q[:, k, h * HALF:(h + 1) * HALF], start=True, stop=True)
                            last.then_inc(s_unit, 2 if isinstance(p, int) and p == 0 and k and c == NT - 1 else 1)

                def sums(p, u, k):
                    slot(u)
                    pe.wait_ge(s_wsum, 2 * p + 4)
                    for h in range(2):
                        for k2 in range(2):
                            last = pe.matmul(ring(k)[64 * k2:64 * k2 + 64, h, :], ones[:, :],
                                             wsum[:, k2, h * HALF:(h + 1) * HALF], start=True, stop=True,
                                             skip_group_check=True)
                    last.then_inc(s_unit, 1)

                def values(p, par, chunks=range(NT)):
                    pe.wait_ge(s_exp, 2 * p + 2)
                    pe.wait_ge(s_h, p + 1)
                    for c in chunks:
                        for h in range(2):
                            for k2 in range(2):
                                last = pe.matmul(PS[64 * k2:64 * k2 + 64, 4 + h, :], V[:, par, c, 64 * k2:64 * k2 + 64],
                                                 D[:, 2 * par + k2, c, h * HALF:(h + 1) * HALF],
                                                 start=(c == 0), stop=(c == NT - 1), skip_group_check=True)
                    if NT - 1 in chunks:
                        last.then_inc(s_pv, 1)

                def projection(p, at, first=False, last=False):
                    pe.wait_ge(s_h, p + 2)
                    for h in range(2):
                        of = pe.matmul(PS[:, Y + h, :], at, half(H, h), start=first, stop=last, skip_group_check=True)
                    of.then_inc(s_proj, 1)

                make(0, 0, 0, 0, lambda: pe.wait_ge(s_const, 6 * 16), None)
                make(1, 1, BODY, 1, None, None)
                sums(0, BODY + MADE, 1)

                def step(p, par, first=False):
                    k = 1 - par
                    u = BODY * (p + 1)
                    make(p + 1, 1 - par, u, k, lambda: values(p - 1, 1 - par),
                         lambda: projection(p - 1, wost[:, 1 - par, :], first))
                    sums(p, u + MADE, k)

                step(1, 1, True)
                with pe.Fori(1, PAIRS // 2 - 1) as i:
                    step(2 * i, 0)
                    step(2 * i + 1, 1)
                step(PAIRS - 2, 0)
                values(PAIRS - 2, 0)
                projection(PAIRS - 2, wost[:, 0, :])
                values(PAIRS - 1, 1, range(NT // 2))
                sums(PAIRS - 1, BODY * PAIRS, 0)
                values(PAIRS - 1, 1, range(NT // 2, NT))
                projection(PAIRS - 1, wost[:, 1, :], last=True)

            @block.vector
            def _(dve):
                dve.memset(ones[:, :], 1.0).then_inc(s_set, 1)
                dve.memset(eps[:, :], DIST_EPS).then_inc(s_set, 1)
                dve.memset(Q[:, :, :], 0.0).then_inc(s_set, 1)
                dve.sem_inc(s_taken, 2)
                dve.sem_inc(s_wsum, 2)
                dve.sem_inc(s_pv, 1)
                dve.sem_inc(s_h, 1)
                dve.sem_inc(s_proj, 1)
                dve.wait_ge(s_const, 6 * 16)
                dve.wait_ge(s_set, 4)

                def take(p, par, u0, k0, weigh):
                    for k in range(2):
                        dve.wait_ge(s_unit, u0 + 1 + k)
                        dve.tensor_scalar(Q[0:D0, k, :], ring(k0 + k)[0:D0].rearrange("q a b -> q (a b)"),
                                          bqk[0:D0, bass.ds(2 * p + k, 1)], None, ALU.add)
                        dve.tensor_scalar(K[0:D0, k, :], ring(k0 + k)[D0:P].rearrange("q a b -> q (a b)"),
                                          bqk[D0:P, bass.ds(2 * p + k, 1)], -2.0, ALU.add, ALU.mult
                                          ).then_inc(s_taken, 1)
                    for k in range(2):
                        dve.wait_ge(s_taken, u0 + 2 + k + 1)
                        dve.tensor_tensor(sq[0:D0, k, :], Q[0:D0, k, :], Q[0:D0, k, :], ALU.mult)
                        dve.tensor_tensor(sq[D0:P, k, :], K[0:D0, k, :], K[0:D0, k, :], ALU.mult).then_inc(s_sq, 1)
                    if weigh is not None:
                        weigh()
                    for k in range(2):
                        dve.wait_ge(s_unit, u0 + 3 + k)
                        dve.tensor_scalar(Q[64:66, k, :], ring(k0 + k)[64:66].rearrange("q a b -> q (a b)"),
                                          rows[64:66, 0:1], None, ALU.add)
                        dve.tensor_scalar(K[64:66, k, :], ring(k0 + k)[96:98].rearrange("q a b -> q (a b)"),
                                          rows[96:98, 1:2], None, ALU.add).then_inc(s_taken, 1)
                    dve.wait_ge(s_unit, u0 + 5)
                    dve.tensor_tensor(V[:, par, :, :], ring(k0).rearrange("q a (b c) -> q (a b) c", c=P),
                                      bv[:, bass.ds(p * P, P)].unsqueeze(1).to_broadcast([P, NT, P]), ALU.add
                                      ).then_inc(s_taken, 1)
                    dve.wait_ge(s_unit, u0 + 6)
                    dve.tensor_scalar(G[:, par, :], ring(k0 + 1).rearrange("q a b -> q (a b)"), bg[:, bass.ds(p, 1)],
                                      None, ALU.add).then_inc(s_taken, 1)
                    for k in range(2):
                        for c in range(NT):
                            dve.wait_ge(s_unit, u0 + 7 + k * NT + c)
                            if k == 0 and c == 0:
                                dve.wait_ge(s_wsum, 2 * p)
                            dve.tensor_scalar(D[:, 2 * par + k, c, :], ring(k0 + c).rearrange("q a b -> q (a b)"), 0.0,
                                              None, ALU.max
                                              ).then_inc(s_taken, 2 if isinstance(p, int) and p == 0 and k and c == NT - 1 else 1)

                def divide(p, par, u, k, own):
                    dve.wait_ge(s_unit, u + 1)
                    dve.tensor_scalar(rec[:, :], ring(k).rearrange("q a b -> q (a b)"), DIST_EPS, None, ALU.add
                                      ).then_inc(s_taken, 1)
                    dve.wait_ge(s_taken, u + 3)
                    own.up(dve.reciprocal(rec[:, :], rec[:, :]))
                    own.done()
                    own.up(dve.tensor_tensor(rec[:, :], rec[:, :], G[:, par, :], ALU.mult))
                    own.done()

                def gated(p, par):
                    dve.tensor_copy(wost[:, par, :], wout[:, bass.ds(p, 1), :].rearrange("q a b -> q (a b)"))
                    dve.wait_ge(s_pv, p + 2)
                    dve.wait_ge(s_proj, p + 1)
                    dve.tensor_tensor(H[:, :], PS[:, 4:6, :].rearrange("q a b -> q (a b)"), rec[:, :], ALU.mult
                                      ).then_inc(s_h, 1)

                OWN = 2
                take(0, 0, 0, 0, None)
                take(1, 1, BODY, 1, None)
                divide(0, 0, BODY + MADE, 1, Count(dve, s_dve))

                def step(p, par):
                    k = 1 - par
                    u = BODY * (p + 1)
                    take(p + 1, 1 - par, u, k, lambda: gated(p - 1, 1 - par))
                    dve.wait_ge(s_h, p + 1)
                    divide(p, par, u + MADE, k, Count(dve, s_dve, OWN * p))

                with dve.Fori(0, PAIRS // 2 - 1) as i:
                    step(2 * i + 1, 1)
                    step(2 * i + 2, 0)
                p = PAIRS - 1
                gated(p - 1, 0)
                own = Count(dve, s_dve, OWN * p)
                dve.wait_ge(s_exp, 2 * p + 2)
                total(dve, own, wsum[:, 1, :], D[:, 3, :, :])
                dve.wait_ge(s_h, p + 1)
                divide(p, 1, BODY * PAIRS, 0, own)
                gated(p, 1)

            @block.scalar
            def _(act):
                act.wait_ge(s_set, 4)

                def weights(p, par):
                    for k in range(2):
                        W = D[:, 2 * par + k, :, :]
                        act.wait_ge(s_taken, BODY * p + 6 + NT * (k + 1) + 2)
                        act.activation(W, W, ACT.Sqrt).then_inc(s_act, 1)
                        act.wait_ge(s_act, 4 * p + 2 * k + 1)
                        act.activation(W, W, ACT.Ln, bias=eps[:, 0:1]).then_inc(s_act, 1)
                        act.wait_ge(s_act, 4 * p + 2 * k + 2)
                        act.activation(W, W, ACT.Exp, scale=-2.0).then_inc(s_exp, 1)

                with act.Fori(0, PAIRS // 2) as i:
                    weights(2 * i, 0)
                    weights(2 * i + 1, 1)

            @block.gpsimd
            def _(pool):
                pool.memset(K[:, :, :], 0.0).then_inc(s_set, 1)

                def totals(p, par, heads=2):
                    for k in range(heads):
                        pool.wait_ge(s_exp, 2 * p + k + 1)
                        pool.wait_ge(s_unit, BODY * p + MADE + 1)
                        total(pool, Count(pool, s_pool, (2 * p + k) * 6), wsum[:, k, :], D[:, 2 * par + k, :, :])

                with pool.Fori(0, PAIRS // 2 - 1) as i:
                    totals(2 * i, 0)
                    totals(2 * i + 1, 1)
                totals(PAIRS - 2, 0)
                totals(PAIRS - 1, 1, 1)


def layer_norm(nc, PS, name, onesd, resid, to, Y=None, bias=None, keep=None, also=None, scale=None, shift=None):
    with ExitStack() as ctx:
        n = Names(nc, ctx, name)
        z = keep if keep is not None else n.sb("z", [P, T])
        sq = n.sb("sq", [P, T])
        d = n.sb("d", [P, T])
        r = n.sb("r", [P, T])
        eps = n.sb("eps", [P, 1])
        early = n.sb("early", [P, 1])
        s_set, s_z, s_mean, s_d, s_sq, s_var, s_ln, s_r, s_m, s_out = (
            n.sem(k) for k in ("set", "z", "mean", "d", "sq", "var", "ln", "r", "m", "out"))
        free = [b for b in range(8) if Y is None or b not in (Y, Y + 1)]
        MEAN, VAR = free[0:2], free[2:4]
        src = z if Y is not None else resid

        with nc.Block() as block:
            @block.vector
            def _(dve):
                dve.memset(eps[:, :], LN_EPS).then_inc(s_set, 1)
                for h in range(2):
                    if Y is not None:
                        if bias is None:
                            dve.tensor_tensor(half(z, h), PS[:, Y + h, :], half(resid, h), ALU.add).then_inc(s_z, 1)
                        else:
                            dve.scalar_tensor_tensor(half(z, h), PS[:, Y + h, :], bias, half(resid, h), ALU.add, ALU.add
                                                     ).then_inc(s_z, 1)
                for h in range(2):
                    dve.wait_ge(s_mean, h + 1)
                    dve.tensor_tensor(half(d, h), half(src, h), PS[:, MEAN[h], :], ALU.subtract).then_inc(s_d, 1)
                if also is not None:
                    dve.wait_ge(s_z, 2)
                    dve.tensor_tensor(also[0][:, :], src[:, :], also[1][:, :], ALU.add).then_inc(s_out, 1)
                for h in range(2):
                    dve.wait_ge(s_r, h + 1)
                    dve.wait_ge(s_d, h + 1)
                    if scale is None:
                        dve.tensor_tensor(half(to, h), half(d, h), half(r, h), ALU.mult).then_inc(s_out, 1)
                    else:
                        dve.tensor_tensor(half(d, h), half(d, h), half(r, h), ALU.mult).then_inc(s_m, 1)
                        dve.wait_ge(s_m, h + 1)
                        dve.tensor_scalar(half(to, h), half(d, h), scale, shift, ALU.mult, ALU.add).then_inc(s_out, 1)

            @block.tensor
            def _(pe):
                for h in range(2):
                    if Y is not None:
                        pe.wait_ge(s_z, h + 1)
                    pe.matmul(PS[:, MEAN[h], :], onesd[:, :], half(src, h), start=True, stop=True).then_inc(s_mean, 1)
                for h in range(2):
                    pe.wait_ge(s_sq, h + 1)
                    pe.matmul(PS[:, VAR[h], :], onesd[:, :], half(sq, h), start=True, stop=True).then_inc(s_var, 1)

            @block.scalar
            def _(act):
                act.wait_ge(s_set, 1)
                act.activation(early[:, :], eps[:, :], ACT.Ln)
                for h in range(2):
                    act.wait_ge(s_d, h + 1)
                    act.activation(half(sq, h), half(d, h), ACT.Square).then_inc(s_sq, 1)
                for h in range(2):
                    act.wait_ge(s_var, h + 1)
                    act.activation(half(r, h), PS[:, VAR[h], :], ACT.Ln, bias=eps[:, 0:1]).then_inc(s_ln, 1)
                for h in range(2):
                    act.wait_ge(s_ln, h + 1)
                    act.activation(half(r, h), half(r, h), ACT.Exp, scale=-0.5).then_inc(s_r, 1)


def context_mlp(nc, PS, x, w, Y, cross):
    RING = 3
    STEPS = NC // RING
    W3 = RING * P
    assert NC % RING == 0 and STEPS == 2 * NT + 1 and Y == 6
    V, kmax, bad = cross["V"], cross["kmax"], cross["bad"]
    with ExitStack() as ctx:
        n = Names(nc, ctx, "mlp")
        C = n.sb("C", [P, 2, RING, 2 * P])
        A = n.sb("A", [P, RING, T])
        W = n.sb("W", [P, 2 * P])
        kp = n.sb("kp", [P, 2, 3, W3], BF16)
        R = n.sb("R", [P, 2, 2, W3])
        row = n.sb("row", [P, KEYS], I32)
        hidden0 = n.sb("hidden0", [P, KEYS], BF16)
        M = n.sb("M", [P, KEYS], I32)
        differ = n.sb("differ", [P, KEYS], BF16)
        counts = n.sb("counts", [P, NT])
        kbias = n.sb("kbias", [1, KPAD], BF16)
        s_row, s_bias, s_aux = n.sem("row"), n.sem("bias"), n.sem("aux")
        s_mask, s_looked, s_dve = n.sem("mask"), n.sem("looked"), n.sem("dve")
        s_w, s_c = n.sem("w"), [n.sem("c0"), n.sem("c1")]
        s_h = n.sem("h")
        s_gelu = n.sem("gelu")
        s_out = n.sem("out")
        s_kv = n.sem("kv")
        s_act = n.sem("act")
        s_rest = n.sem("rest")
        s_st = [n.sem("st0"), n.sem("st1")]

        def steps(eng, body):
            body(0, 0)
            with eng.Fori(0, NT) as i:
                body(2 * i + 1, 1)
                body(2 * i + 2, 0)

        def flat(t):
            return t.rearrange("q a b -> q (a b)")

        with nc.Block() as block:
            @block.sync
            def _(sp):
                def load(i, b):
                    sp.wait_ge(s_out, 3 * i if not isinstance(i, int) or i else 1)
                    sp.dma_start(C[:, b, :, :], w["ctx"][bass.ds(RING * i, RING)].rearrange("c p f -> p c f")
                                 ).then_inc(s_c[b], 16)

                sp.dma_start(W[:, :], w["cross_w"][:, 0:2 * P]).then_inc(s_w, 16)
                steps(sp, load)

            @block.tensor
            def _(pe):
                pe.sem_inc(s_out, RING)

                def hidden(i, b, k):
                    c, at = i * RING + k, 2 * ((b + k) % 2)
                    if k == 0:
                        pe.wait_ge(s_c[b], (i - b) * 8 + 16)
                    pe.wait_ge(s_gelu, c + 1)
                    for h in range(2):
                        last = pe.matmul(PS[:, at + h, :], C[:, b, k, 0:P], half(x, h), start=True, stop=True)
                    last.then_inc(s_h, 1)

                def back(i, b, k, start=False, stop=False):
                    pe.wait_ge(s_gelu, i * RING + k + 2 + 1)
                    for h in range(2):
                        last = pe.matmul(PS[:, Y + h, :], C[:, b, k, P:2 * P], A[:, k, h * HALF:(h + 1) * HALF],
                                         start=start, stop=stop, skip_group_check=True)
                    last.then_inc(s_out, 1)

                def keys_values(i, b):
                    if isinstance(i, int):
                        pe.wait_ge(s_w, 16)
                    pe.wait_ge(s_rest, 2 * i + 1)
                    pe.matmul(PS[:, 4, 0:W3], W[:, 0:P], C[:, b, :, 0:P], start=True, stop=True)
                    for c in range(RING):
                        last = pe.matmul(PS[:, 5, c * P:(c + 1) * P], C[:, b, c, 0:P], W[:, P:2 * P],
                                         start=True, stop=True, skip_group_check=True)
                    last.then_inc(s_kv, 1)

                def step(i, b):
                    first = isinstance(i, int)
                    for k in range(RING):
                        hidden(i, b, k)
                        if k == 2:
                            keys_values(i, b)
                        if k:
                            back(i, b, k - 1, start=first and k == 1)
                        elif not first:
                            back(i - 1, 1 - b, RING - 1)

                steps(pe, step)
                back(STEPS - 1, 0, RING - 1, stop=True)

            @block.gpsimd
            def _(pool):
                pool.dma_start(row[:, :], w["mask"][0].partition_broadcast(P)).then_inc(s_row, 16)
                pool.dma_start(M[:, :], w["mask"][0:P, :]).then_inc(s_mask, 16)
                with pool.Fori(1, NT) as t:
                    pool.wait_ge(s_looked, t)
                    for q in range(4):
                        pool.wait_ge(s_h, 2 * RING * t + 4 + q)
                        at = slice(q * KEYS // 4, (q + 1) * KEYS // 4)
                        pool.dma_start(M[:, at], w["mask"][bass.ds(t * P, P), at]).then_inc(s_mask, 16)
                pool.dma_start(cross["kaux"][1:4, :], w["kaux"][1:4, :]).then_inc(s_aux, 16)
                pool.wait_ge(s_bias, 2)
                pool.dma_start(cross["kaux"][0:1, :], kbias[:, :]).then_inc(s_aux, 16)
                pool.wait_ge(s_aux, 32)

            @block.vector
            def _(dve):
                own = Count(dve, s_dve)
                dve.sem_inc(s_rest, 2)

                def rest(i, b):
                    dve.wait_ge(s_kv, i + 1)
                    dve.tensor_copy(V[:, bass.ds(RING * i, RING), :], PS[:, 5, 0:W3].rearrange("q (c f) -> q c f", f=P))
                    dve.wait_ge(s_act, 3 * i + 1)
                    dve.tensor_reduce(kmax[:, bass.ds(i, 1)], PS[:, 4, 0:W3], AX.X, ALU.max, apply_absolute_value=True)
                    dve.tensor_tensor(R[:, b, 0, :], PS[:, 4, 0:W3], kp[:, b, 0, :], ALU.subtract).then_inc(s_rest, 1)
                    dve.wait_ge(s_rest, 2 * i + 3)
                    dve.wait_ge(s_act, 3 * i + 2)
                    dve.tensor_tensor(R[:, b, 1, :], R[:, b, 0, :], kp[:, b, 1, :], ALU.subtract).then_inc(s_rest, 1)

                def look(t):
                    dve.wait_ge(s_mask, 64 * t + 16)
                    dve.scalar_tensor_tensor(differ[:, :], M[:, :], 0.0, hidden0[:, :], ALU.is_equal, ALU.not_equal,
                                             accum_out=counts[:, bass.ds(t, 1)]).then_inc(s_looked, 1)
                    dve.wait_ge(s_looked, t + 1)

                rest(0, 0)
                rest(1, 1)
                dve.wait_ge(s_row, 16)
                own.up(dve.tensor_scalar(hidden0[:, :], row[:, :], 0, None, ALU.is_equal))
                own.up(dve.memset(bad[:, :], 0.0))
                rest(2, 0)
                own.done()
                dve.memset(kbias[:, KEYS:KPAD], PADDED).then_inc(s_bias, 1)
                dve.tensor_scalar(kbias[:, 0:KEYS], hidden0[0:1, :], MASKED, None, ALU.mult).then_inc(s_bias, 1)
                look(0)
                own.up(dve.tensor_reduce(bad[0:1, 1:2], hidden0[0:1, :], AX.X, ALU.add))
                with dve.Fori(1, NT) as i:
                    rest(2 * i + 1, 1)
                    look(i)
                    rest(2 * i + 2, 0)
                own.done()
                own.up(dve.tensor_scalar(bad[0:1, 1:2], bad[0:1, 1:2], float(KEYS), None, ALU.is_equal))
                own.up(dve.tensor_reduce(bad[:, 0:1], counts[:, :], AX.X, ALU.add))
                own.up(dve.tensor_reduce(kmax[:, STEPS:STEPS + 1], kmax[:, 0:STEPS], AX.X, ALU.max))
                own.done()

            @block.scalar
            def _(act):
                act.sem_inc(s_gelu, 2)
                for b in range(2):
                    act.sem_inc(s_st[b], 16)

                def gelu(i, b, k):
                    c, at = i * RING + k, 2 * ((b + k) % 2)
                    act.wait_ge(s_h, c + 1)
                    act.wait_ge(s_out, c + 1)
                    act.activation(A[:, k, :], flat(PS[:, at:at + 2, :]), ACT.Gelu_apprx_tanh).then_inc(s_gelu, 1)

                def part(i, b, r):
                    if r == 0:
                        act.wait_ge(s_kv, i + 1)
                        act.wait_ge(s_st[b], (i - b) * 8 + 16)
                        act.activation(kp[:, b, 0, :], PS[:, 4, 0:W3], ACT.Copy).then_inc(s_act, 1)
                    else:
                        act.wait_ge(s_rest, 2 * i + r + 2)
                        act.activation(kp[:, b, r, :], R[:, b, r - 1, :], ACT.Copy).then_inc(s_act, 1)
                    if r == 2:
                        act.wait_ge(s_act, 3 * i + 3)
                        act.dma_start(cross["k"][:, :, bass.ds(i * W3, W3)].rearrange("r f t -> f r t"), kp[:, b, :, :]
                                      ).then_inc(s_st[b], 16)

                def step(i, b):
                    for k in range(RING):
                        gelu(i, b, k)
                        if not isinstance(i, int):
                            part(i - 1, 1 - b, k)

                steps(act, step)
                for r in range(3):
                    part(STEPS - 1, 0, r)
                for b in range(2):
                    act.wait_ge(s_st[b], 16 * ((STEPS + 1 - b) // 2) + 16)


def routed_mlp(nc, PS, name, x, ident, w, func, weighted):
    Y = (4, 6)
    with ExitStack() as ctx:
        n = Names(nc, ctx, name)
        W = n.sb("W", [P, 2, 2 * FF])
        A = n.sb("A", [P, 2, T])
        acc = n.sb("acc", [P, NT, P])
        small = n.sb("small", [P, 320])
        wr = small[:, 0:EXPERTS]
        bias1 = small[:, EXPERTS:EXPERTS + EXPERTS * FC]
        o = 64
        routers = small[:, o:o + 64].rearrange("q (t e) -> q t e", e=EXPERTS)
        backward = small[:, o + 64:o + 128].rearrange("q (t e) -> q t e", e=EXPERTS)
        b2 = small[0:EXPERTS, o + 128:o + 256]
        L = n.sb("L", [P, NT, EXPERTS])
        E = n.sb("E", [P, NT, EXPERTS])
        top = n.sb("top", [P, NT, 1])
        G = n.sb("G", [P, NT, EXPERTS])
        GT = n.sb("GT", [EXPERTS, T])
        s_small, s_w = n.sem("small"), [n.sem("w0"), n.sem("w1")]
        s_logits, s_dve, s_e, s_gates, s_gt, s_gtc = (n.sem(k) for k in ("logits", "dve", "e", "gates", "gt", "gtc"))
        s_h, s_a, s_y, s_comb = (n.sem(k) for k in ("h", "a", "y", "comb"))

        def flat(t):
            return t.rearrange("q a b -> q (a b)")

        with nc.Block() as block:
            @block.sync
            def _(sp):
                sp.dma_start(small[:, 0:320], w["small"]).then_inc(s_small, 16)
                for e in range(2):
                    sp.dma_start(W[:, e, :], w["experts"][e]).then_inc(s_w[e], 16)
                with sp.Fori(1, EXPERTS // 2) as i:
                    for k in range(2):
                        sp.wait_ge(s_y, (2 * i + k - 1) * FC + 2)
                        sp.dma_start(W[:, k, :], w["experts"][bass.ds(2 * i + k, 1)].rearrange("a p f -> (a p) f")
                                     ).then_inc(s_w[k], 16)

            @block.tensor
            def _(pe):
                pe.sem_inc(s_y, 2)
                pe.wait_ge(s_small, 16)
                for t in range(NT):
                    last = pe.matmul(PS[:, 6, t * EXPERTS:(t + 1) * EXPERTS], x[:, t * P:(t + 1) * P], wr,
                                     start=True, stop=True, skip_group_check=True)
                last.then_inc(s_logits, 1)

                def hidden(e, k, f):
                    pe.wait_ge(s_a, e * FC + f + 1)
                    for h in range(2):
                        last = pe.matmul(PS[:, 2 * (f % 2) + h, :], W[:, k, f * P:(f + 1) * P], half(x, h),
                                         start=True, stop=True)
                    last.then_inc(s_h, 1)

                def back(e, k, f):
                    pe.wait_ge(s_a, e * FC + f + 3)
                    if f == 0:
                        pe.wait_ge(s_comb, e * NT + NT)
                    for t in range(NT):
                        last = pe.matmul(PS[:, Y[k] + t // 4, (t % 4) * P:(t % 4 + 1) * P],
                                         A[:, f % 2, t * P:(t + 1) * P], W[:, k, FF + f * P:FF + (f + 1) * P],
                                         start=(f == 0 and t % 4 == 0), stop=(f == FC - 1), skip_group_check=True)
                    last.then_inc(s_y, 1)

                def expert(e, k, first=False):
                    pe.wait_ge(s_w[k], ((e - k) // 2 + 1) * 16 if isinstance(e, int) else (e - k) * 8 + 16)
                    for f in range(FC):
                        hidden(e, k, f)
                        if f:
                            back(e, k, f - 1)
                        elif not first:
                            back(e - 1, 1 - k, FC - 1)

                expert(0, 0, True)
                pe.wait_ge(s_gates, 1)
                expert(1, 1)
                with pe.Fori(1, EXPERTS // 2) as i:
                    expert(2 * i, 0)
                    expert(2 * i + 1, 1)
                back(EXPERTS - 1, 1, FC - 1)
                if weighted:
                    for t in range(NT):
                        last = pe.transpose(PS[0:EXPERTS, 2 + t // 4, (t % 4) * P:(t % 4 + 1) * P], G[:, t, :], ident[:, :])
                    last.then_inc(s_gt, 1)
                pe.wait_ge(s_comb, EXPERTS * NT + NT)
                for t in range(NT):
                    last = pe.matmul(PS[:, t // 4, (t % 4) * P:(t % 4 + 1) * P], acc[:, t, :], ident[:, :],
                                     start=(t % 4 == 0), stop=not weighted, skip_group_check=True)
                if weighted:
                    pe.wait_ge(s_gtc, 1)
                    for h in range(2):
                        pe.matmul(PS[:, h, :], b2, half(GT, h), start=False, stop=True, skip_group_check=True)

            @block.scalar
            def _(act):
                act.sem_inc(s_a, 2)
                if weighted:
                    act.wait_ge(s_dve, 4)
                    act.activation(flat(E), flat(E), ACT.Exp).then_inc(s_e, 1)
                act.wait_ge(s_small, 16)

                def activate(e, f):
                    act.wait_ge(s_h, e * FC + f + 1)
                    act.wait_ge(s_y, e * FC + f + 1)
                    of = flat(PS[:, 2 * (f % 2):2 * (f % 2) + 2, :])
                    if weighted:
                        act.activation(A[:, f % 2, :], of, func, bias=bias1[:, bass.ds(e * FC + f, 1)]).then_inc(s_a, 1)
                    else:
                        act.activation(A[:, f % 2, :], of, func).then_inc(s_a, 1)

                with act.Fori(0, EXPERTS) as e:
                    for f in range(FC):
                        activate(e, f)

            @block.vector
            def _(dve):
                own = Count(dve, s_dve)
                dve.sem_inc(s_comb, NT)
                own.up(dve.memset(acc[:, :, :], 0.0))
                dve.wait_ge(s_logits, 1)
                dve.wait_ge(s_small, 16)
                all8 = [P, NT, EXPERTS]
                own.up(dve.tensor_tensor(L[:, :, :], PS[:, 6, 0:NT * EXPERTS].rearrange("q (t e) -> q t e", e=EXPERTS),
                                         routers, ALU.add))
                own.done()
                own.up(dve.tensor_reduce(top[:, :, 0], L[:, :, :], AX.X, ALU.max))
                own.done()
                own.up(dve.tensor_tensor(E[:, :, :], L[:, :, :], top[:, :, :].to_broadcast(all8), ALU.subtract))
                own.done()
                own.up(dve.tensor_tensor(L[:, :, :], L[:, :, :], top[:, :, :].to_broadcast(all8), ALU.is_equal))
                own.done()
                own.up(dve.tensor_tensor(L[:, :, :], L[:, :, :], backward, ALU.mult))
                own.done()
                own.up(dve.tensor_reduce(top[:, :, 0], L[:, :, :], AX.X, ALU.max))
                own.done()
                gates = dve.tensor_tensor(G[:, :, :], L[:, :, :], top[:, :, :].to_broadcast(all8), ALU.is_equal)
                if weighted:
                    own.up(gates)
                    dve.wait_ge(s_e, 1)
                    own.done()
                    own.up(dve.tensor_reduce(top[:, :, 0], E[:, :, :], AX.X, ALU.add))
                    own.done()
                    own.up(dve.reciprocal(top[:, :, 0], top[:, :, 0]))
                    own.done()
                    gates = dve.tensor_tensor(G[:, :, :], G[:, :, :], top[:, :, :].to_broadcast(all8), ALU.mult)
                gates.then_inc(s_gates, 1)
                dve.wait_ge(s_gates, 1)
                own.done()

                def combine(e, k):
                    dve.wait_ge(s_y, e * FC + FC + 2)
                    dve.wait_ge(s_comb, e * NT + NT)
                    for t in range(NT):
                        dve.scalar_tensor_tensor(acc[:, t, :], PS[:, Y[k] + t // 4, (t % 4) * P:(t % 4 + 1) * P],
                                                 flat(G)[:, bass.ds(e + t * EXPERTS, 1)], acc[:, t, :], ALU.mult, ALU.add
                                                 ).then_inc(s_comb, 1)

                with dve.Fori(0, EXPERTS // 2) as i:
                    combine(2 * i, 0)
                    combine(2 * i + 1, 1)
                if weighted:
                    dve.wait_ge(s_gt, 1)
                    dve.tensor_copy(GT[:, :], flat(PS[0:EXPERTS, 2:4, :])).then_inc(s_gtc, 1)


NARROW_BLOCKS = [[(i, j) for j in range(3) for i in range(3)]]
WIDE_BLOCKS = [[(0, 0), (0, 1), (1, 0)], [(1, 1), (0, 2), (2, 0)]]


def when(eng, flag, value):
    return nullcontext() if flag is None else eng.If(eng.value_load(flag[0:1, 0:1], min_val=0, max_val=1) == value)


def attention(nc, PS, name, w, wide, cus, scale, maxes, V, out, ident, identb, flag=None, early=None):
    d = D1 if wide else D8
    blocks = WIDE_BLOCKS if wide else NARROW_BLOCKS
    tiles = len(blocks)
    B = len(blocks[0]) * d
    EDGE = B // 32 * 32
    per = 2 if wide else 1
    nk = w["k"].shape[2]
    loads = 16 * (sum(2 * len(b) for b in blocks) + 2 + (0 if maxes else 1))
    MU = 2 * 4 * NT
    LOOK = [[t] for t in range(NT - 2)] + [[NT - 2, NT - 1], []]
    assert not maxes or per * cus == NT
    NB = 3 if maxes else 2
    RING = 2 if maxes else 3
    UNROLL = 6
    with ExitStack() as ctx:
        n = Names(nc, ctx, name)
        if early is None:
            Q = [n.sb(f"Q{b}", [P, tiles, 4, T], BF16) for b in range(NB)]
            K = [n.sb(f"K{b}", [P, tiles, 4, nk], BF16) for b in range(NB)]
        else:
            Q, K = early
        E = n.sb("E", [P, 2, 4, T])
        vst = n.sb("vst", [P, 2, per, 4, 32])
        ones = n.sb("ones", [P, 32])
        O = n.sb("O", [P, 1 if maxes else GROUPS, T])
        rc = n.sb("rc", [P, HALF if wide else 16])
        mx = n.sb("mx", [P, 2, 4, NT])
        mr = n.sb("mr", [P, 2, 4 * NT])
        mb = n.sb("mb", [P, 3, 4 * NT], BF16)
        mt = n.sb("mt", [P, P], BF16)
        s_set = [n.sem(f"set{b}") for b in range(NB)]
        s_vst = n.sem("vst")
        s_ld = [n.sem(f"ld{b}") for b in range(NB)]
        s_mr = [n.sem(f"mr{b}") for b in range(NB)]
        s_mw = n.sem("mw")
        s_s = n.sem("s")
        s_e = n.sem("e")
        s_pv = n.sem("pv")
        s_v = n.sem("v")
        s_acc = n.sem("acc")
        s_m = n.sem("m")
        s_mt = n.sem("mt")
        s_mb = n.sem("mb")
        s_tm = n.sem("tm")
        s_mc = n.sem("mc")
        s_to = n.sem("to")
        s_ot = n.sem("ot")
        s_dve = n.sem("dve")

        def flat(t):
            return t.rearrange("q a b -> q (a b)")

        def passes(eng, body):
            def run(at):
                body(1, (at + 1) % 2, True, 1)
                turns = 0 if maxes else (cus - 2) // UNROLL
                if turns:
                    with eng.Fori(0, turns) as i:
                        for k in range(UNROLL):
                            body(UNROLL * i + 2 + k, (at + k) % 2, False, 2 + k)
                for cu in range(2 + turns * UNROLL, cus):
                    body(cu, (at + cu) % 2, False, cu)
            return run

        def loaded(g):
            return (g // NB + 1) * loads - (0 if early is None or g % NB else 16 * len(blocks[0]))

        def look_bank(g, j):
            return 4 if g or j % 2 == 0 else 2

        def order(g, t, j):
            return t // 2 * 8 + 2 * j + t % 2 if g and t >= NT - 2 else t * 4 + j

        def slot(cu, j):
            return 2 * ((4 * cu + j) % RING)

        def zero(eng, b):
            for t in (Q[b], K[b]):
                eng.memset(t[EDGE:P].rearrange("q a b c -> q (a b c)").bitcast(F32), 0.0).then_inc(s_set[b], 1)

        with nc.Block() as block:
            @block.gpsimd
            def _(pool):
              with when(pool, flag, 1):
                if early is None:
                    for b in range(1, NB):
                        zero(pool, b)

            @block.sync
            def _(sp):
              with when(sp, flag, 1):
                def load(g):
                    b = g % NB
                    if g >= NB:
                        sp.wait_ge(s_s, (g - NB + 1) * per * cus * 4)
                    rows = slice(g * 4 * d, (g + 1) * 4 * d)
                    zeros = g >= NB or early is not None

                    def zeroed():
                        nonlocal zeros
                        if not zeros:
                            sp.wait_ge(s_set[b], 2)
                            zeros = True

                    for tile, bl in enumerate(blocks):
                        for r, (i, j) in enumerate(bl):
                            if (r + 1) * d > EDGE:
                                zeroed()
                            for to, of, part in ((Q[b], w["q"], i), (K[b], w["k"], j)):
                                if early is not None and g == 0 and to is K[b]:
                                    continue
                                sp.dma_start(to[r * d:(r + 1) * d, tile, :, :],
                                             of[part, rows, :].rearrange("(j i) t -> i j t", i=d)).then_inc(s_ld[b], 16)
                    zeroed()
                    sp.dma_start(K[b][B:B + 4, 0, :, :], w["kaux"].unsqueeze(1).to_broadcast([4, 4, nk])
                                 ).then_inc(s_ld[b], 16)
                    if maxes:
                        sp.dma_start(Q[b][B:B + 4, 0, :, :], w["qaux"].unsqueeze(1).to_broadcast([4, 4, T])
                                     ).then_inc(s_ld[b], 16)
                    else:
                        sp.dma_start(Q[b][B:B + 1, 0, :, :], w["qaux"][0:1].unsqueeze(1).to_broadcast([1, 4, T])
                                     ).then_inc(s_ld[b], 16)
                        sp.dma_start(Q[b][B + 1:B + 4, 0, :, :], w["mrow"][:, 4 * g:4 * g + 4, :]).then_inc(s_ld[b], 16)

                def maxima(g):
                    b = g % NB
                    sp.wait_ge(s_mc, g + 1)
                    sp.dma_start(w["mrow"][g], mt[0:3 * 4 * NT, :]).then_inc(s_mw, 16)
                    sp.wait_ge(s_mw, 16 * (g + 1))
                    sp.wait_ge(s_ld[b], loaded(g))
                    sp.wait_ge(s_m, MU * (g + 1))
                    sp.dma_start(Q[b][B + 1:B + 4, 0, :, :],
                                 w["mrow"][g].rearrange("(r j t) p -> r j (t p)", r=3, j=4)).then_inc(s_mr[b], 16)

                for g in range(NB):
                    load(g)
                if maxes:
                    maxima(0)
                for g in range(1, GROUPS):
                    if maxes:
                        maxima(g)
                    if g + NB - 1 < GROUPS:
                        load(g + NB - 1)

            @block.tensor
            def _(pe):
              with when(pe, flag, 1):
                pe.sem_inc(s_pv, 2)
                pe.wait_ge(s_vst, 1)

                def max_unit(g, j, t):
                    b = g % NB
                    if j == 0 and isinstance(t, int) and t == 0:
                        if g >= 1:
                            pe.wait_ge(s_mc, g)
                        if g >= 2 and not wide:
                            pe.wait_ge(s_ot, 2 * (g - 1))
                    for h in range(2):
                        pe.wait_ge(s_mt, g * MU + order(g, t, j) * 2 + h + (3 if g else 1))
                        pe.matmul(PS[:, look_bank(g, j) + h, :], Q[b][:, 0, j, bass.ds(t * P, P)],
                                  K[b][:, 0, j, h * HALF:(h + 1) * HALF], start=True, stop=True).then_inc(s_m, 1)

                def turn_maxima(g):
                    pe.wait_ge(s_mb, g + 1)
                    pe.transpose(PS[:, 4, :].bitcast(BF16)[0:3 * 4 * NT, 0:P], flat(mb), identb[:, :]).then_inc(s_tm, 1)

                def turn_output(g):
                    pe.wait_ge(s_acc, g + 2)
                    if maxes and g + 1 < GROUPS:
                        pe.wait_ge(s_mc, g + 2)
                    if g >= 1:
                        pe.wait_ge(s_ot, 2 * g)
                    for h in range(2):
                        for t in range(4):
                            last = pe.transpose(PS[:, 4 + h, t * P:(t + 1) * P],
                                                O[:, 0 if maxes else g, (4 * h + t) * P:(4 * h + t + 1) * P], ident[:, :])
                        last.then_inc(s_to, 1)

                def scores(sg, cu, j, k):
                    g, qh = sg // per, sg % per
                    pe.wait_ge(s_e, (sg * cus + cu) * 4 + j + 1)
                    at = slot(sg * cus + k, j)
                    for s in range(2):
                        key, q = (2 * cu + s, qh * HALF) if wide else (cu, s * HALF)
                        for tile in range(tiles):
                            last = pe.matmul(PS[:, at + s, :], K[g % NB][:, tile, j, bass.ds(key * P, P)],
                                             Q[g % NB][:, tile, j, q:q + HALF], start=(tile == 0), stop=(tile == tiles - 1))
                    last.then_inc(s_s, 1)
                    if maxes and g + 1 < GROUPS:
                        if j == 0 and qh == 0 and cu == 0:
                            pe.wait_ge(s_ld[(g + 1) % NB], loaded(g + 1))
                        for t in LOOK[qh * cus + cu]:
                            max_unit(g + 1, j, t)
                        if j == 1 and qh * cus + cu == NT - 1:
                            turn_maxima(g + 1)

                def values(gc, s, par, start, stop):
                    if s == 0:
                        pe.wait_ge(s_e, gc * 4 + 4 + RING)
                        pe.wait_ge(s_v, gc + 1)
                    src = [E[:, par, j, s * HALF:(s + 1) * HALF] for j in range(4)]
                    for j in range(4):
                        last = pe.matmul(PS[32 * j:32 * j + 32, 6 if wide else 6 + s, :], vst[:, par, s if wide else 0, j, :],
                                         src[j], start=start and not (wide and s), stop=stop, skip_group_check=True)
                    if wide:
                        for j in range(4):
                            last = pe.matmul(PS[32 * j:32 * j + 32, 7, :], ones[:, :], src[j],
                                             start=start and s == 0, stop=stop, skip_group_check=True)
                    if s == 1:
                        last.then_inc(s_pv, 1)

                if maxes:
                    pe.wait_ge(s_ld[0], loads)
                    with pe.Fori(0, NT) as t:
                        for j in range(4):
                            max_unit(0, j, t)
                    turn_maxima(0)

                for sg in range(GROUPS * per):
                    g = sg // per
                    if sg % per == 0:
                        pe.wait_ge(s_ld[g % NB], loaded(g))
                        if maxes:
                            pe.wait_ge(s_mr[g % NB], (g // NB + 1) * 16)
                    for j in range(4):
                        scores(sg, 0, j, 0)
                    pe.wait_ge(s_acc, sg + 1)

                    def body(cu, par, first, k=None):
                        gc = sg * cus + cu
                        for j in range(4):
                            scores(sg, cu, j, cu if k is None else k)
                            if j % 2:
                                values(gc - 1, j // 2, 1 - par, first, False)

                    passes(pe, body)(sg * cus)
                    last_gc = sg * cus + cus - 1
                    for s in range(2):
                        values(last_gc, s, last_gc % 2, False, True)
                    if not wide and maxes:
                        turn_output(g)
                if not wide and not maxes:
                    for g in range(GROUPS):
                        turn_output(g)

            @block.scalar
            def _(act):
              with when(act, flag, 1):
                act.sem_inc(s_e, RING)
                for sg in range(GROUPS * per):
                    def unit(cu, par, first=False, k=None):
                        gc = sg * cus + cu
                        act.wait_ge(s_pv, gc + 1)
                        for j in range(4):
                            act.wait_ge(s_s, gc * 4 + j + 1)
                            at = slot(sg * cus + (cu if k is None else k), j)
                            act.activation(E[:, par, j, :], flat(PS[:, at:at + 2, :]), ACT.Exp,
                                           scale=scale).then_inc(s_e, 1)
                    unit(0, sg * cus % 2)
                    passes(act, unit)(sg * cus)

            @block.vector
            def _(dve):
              with when(dve, flag, 1):
                own = Count(dve, s_dve)
                dve.sem_inc(s_acc, 1)
                dve.sem_inc(s_mt, 4)
                if early is None:
                    zero(dve, 0)
                own.up(dve.memset(vst[:, :, :, :, :].rearrange("q a b c e -> q (a b c e)"), 1.0))
                dve.memset(ones[:, :], 1.0).then_inc(s_vst, 1)
                own.done()

                def reduce(g, j, t):
                    for h in range(2):
                        dve.wait_ge(s_m, g * MU + order(g, t, j) * 2 + h + 1)
                        dve.tensor_reduce(mx[:, h, j, bass.ds(t, 1)], PS[:, look_bank(g, j) + h, :], AX.X, ALU.max).then_inc(s_mt, 1)

                def parts(g):
                    m = [mx[:, h, :, :].rearrange("q a b -> q (a b)") for h in range(2)]
                    dve.wait_ge(s_mt, (g + 1) * MU + 4)
                    own.up(dve.tensor_tensor(mr[:, 0, :], m[0], m[1], ALU.max))
                    own.done()
                    if g:
                        dve.wait_ge(s_tm, g)
                    own.up(dve.tensor_scalar(mb[:, 0, :], mr[:, 0, :], -1.0, None, ALU.mult))
                    own.done()
                    own.up(dve.scalar_tensor_tensor(mr[:, 1, :], mr[:, 0, :], -1.0, mb[:, 0, :], ALU.mult, ALU.subtract))
                    own.done()
                    own.up(dve.tensor_copy(mb[:, 1, :], mr[:, 1, :]))
                    own.done()
                    own.up(dve.tensor_tensor(mr[:, 0, :], mr[:, 1, :], mb[:, 1, :], ALU.subtract))
                    own.done()
                    dve.tensor_copy(mb[:, 2, :], mr[:, 0, :]).then_inc(s_mb, 1)
                    dve.wait_ge(s_tm, g + 1)
                    if g:
                        dve.wait_ge(s_mw, 16 * g)
                    dve.tensor_copy(mt[0:3 * 4 * NT, :], PS[:, 4, :].bitcast(BF16)[0:3 * 4 * NT, 0:P]).then_inc(s_mc, 1)

                def divide(g):
                    for h in range(2):
                        dve.wait_ge(s_to, 2 * g + h + 1)
                        turned = PS[:, 4 + h, :].rearrange("q (t j c) -> q t j c", t=4, c=32)
                        r = rc[:, 0:16].rearrange("q (t j c) -> q t j c", t=4, c=1)
                        own.up(dve.reciprocal(r, turned[:, :, :, D8:D8 + 1]))
                        own.done()
                        dve.tensor_tensor(
                            out[:, 4 * h:4 * h + 4, g * 32:(g + 1) * 32].rearrange("q t (j c) -> q t j c", c=D8),
                            turned[:, :, :, 0:D8], r.to_broadcast([P, 4, 4, D8]), ALU.mult).then_inc(s_ot, 1)
                        dve.wait_ge(s_ot, 2 * g + h + 1)

                def quotient(sg, piece):
                    g, qh = sg // per, sg % per
                    if sg < 0 or piece > 4:
                        return
                    if piece < 4:
                        at = slice(piece * P, (piece + 1) * P)
                        dve.wait_ge(s_acc, sg + 2)
                        own.up(dve.reciprocal(rc[:, at], O[:, 0, HALF + piece * P:HALF + (piece + 1) * P]))
                    else:
                        own.done()
                        own.up(dve.tensor_tensor(out[:, g, qh * HALF:(qh + 1) * HALF], O[:, 0, 0:HALF], rc[:, :], ALU.mult))
                        own.done()

                if maxes:
                    with dve.Fori(0, NT) as t:
                        for j in range(4):
                            reduce(0, j, t)
                    parts(0)

                for sg in range(GROUPS * per):
                    g, qh = sg // per, sg % per

                    def unit(cu, par, first=False, k=None):
                        gc = sg * cus + cu
                        dve.wait_ge(s_pv, gc + 1)
                        if wide:
                            of = V[:, bass.ds(2 * cu, 2), g * P:(g + 1) * P]
                            dve.tensor_copy(vst[:, par, :, :, :].rearrange("q a b c -> q a (b c)"), of).then_inc(s_v, 1)
                        else:
                            of = V[:, bass.ds(cu, 1), g * 32:(g + 1) * 32].rearrange("q a (b c) -> q (a b) c", c=D8)
                            dve.tensor_copy(vst[:, par, 0, :, 0:D8], of).then_inc(s_v, 1)
                        for j in range(4):
                            if maxes and g + 1 < GROUPS:
                                for t in LOOK[qh * cus + cu]:
                                    reduce(g + 1, j, t)
                            if wide and cu < 2:
                                quotient(sg - 1, cu * 4 + j)
                        if maxes and g + 1 < GROUPS and qh * cus + cu == NT - 1:
                            parts(g + 1)

                    unit(0, sg * cus % 2)
                    passes(dve, unit)(sg * cus)
                    if wide:
                        dve.wait_ge(s_pv, (sg + 1) * cus + 2)
                        dve.tensor_copy(O[:, 0, :], flat(PS[:, 6:8, :])).then_inc(s_acc, 1)
                    else:
                        if g and maxes:
                            dve.wait_ge(s_to, 2 * g)
                        dve.wait_ge(s_pv, (sg + 1) * cus + 2)
                        dve.tensor_copy(O[:, 0 if maxes else g, :], flat(PS[:, 6:8, :])).then_inc(s_acc, 1)
                    if not wide and maxes:
                        divide(g)
                if wide:
                    for piece in range(8):
                        quotient(GROUPS * per - 1, piece)
                if not wide and not maxes:
                    for g in range(GROUPS):
                        divide(g)


def project(nc, PS, name, weight, H, groups, ident=None):
    with ExitStack() as ctx:
        n = Names(nc, ctx, name)
        HT = n.sb("HT", [P, T])
        s_t, s_c, s_p = n.sem("t"), n.sem("c"), n.sem("p")
        with nc.Block() as block:
            @block.tensor
            def _(pe):
                if ident is not None:
                    for t in range(NT):
                        last = pe.transpose(PS[:, 2 + t // 4, (t % 4) * P:(t % 4 + 1) * P], H[:, t, :], ident[:, :])
                    last.then_inc(s_t, 1)
                    pe.wait_ge(s_c, 1)
                for h in range(2):
                    for g in range(groups):
                        of = half(HT, h) if ident is not None else H[:, g, h * HALF:(h + 1) * HALF]
                        pe.matmul(PS[:, h, :], weight[:, g * P:(g + 1) * P], of, start=(g == 0), stop=(g == groups - 1)
                                  ).then_inc(s_p, 1)

            @block.vector
            def _(dve):
                if ident is not None:
                    dve.wait_ge(s_t, 1)
                    dve.tensor_copy(HT[:, :], PS[:, 2:4, :].rearrange("q a b -> q (a b)")).then_inc(s_c, 1)


def rotary_operands(nc, PS, name, x, w, V, wo):
    OPS = 2 * GROUPS
    assert OPS == NT
    with ExitStack() as ctx:
        n = Names(nc, ctx, name)
        W = n.sb("W", [P, 2, 2 * P])
        C = n.sb("C", [P, 2, 2, T])
        wv = n.sb("wv", [P, HALF])
        wo2 = n.sb("wo2", [P, 2, HALF])
        A = n.sb("A", [P, 2, T])
        S = n.sb("S", [P, 2, T])
        R = n.sb("R", [P, 2, 2, T])
        parts = n.sb("parts", [P, 2, 3, T], BF16)
        s_w, s_v = [n.sem("w0"), n.sem("w1")], n.sem("v")
        s_eo, s_ta = n.sem("eo"), n.sem("ta")
        s_vals, s_prod, s_wo = n.sem("vals"), n.sem("prod"), n.sem("wo")
        s_left = [n.sem(f"left{r}") for r in range(3)]
        s_part = [n.sem(f"part{r}") for r in range(3)]
        s_st = [n.sem("st0"), n.sem("st1")]

        def flat(t):
            return t.rearrange("q a b -> q (a b)")

        with nc.Block() as block:
            @block.sync
            def _(sp):
                sp.dma_start(wv[:, :], w["wv"]).then_inc(s_v, 16)
                sp.dma_start(wo2[:, :, :], w["wo2"]).then_inc(s_v, 16)
                for o in range(OPS):
                    b = o % 2
                    if o >= 2:
                        sp.wait_ge(s_ta, 2 * (o - 1))
                    sp.dma_start(W[:, b, :], w["weq"][o]).then_inc(s_w[b], 16)
                    sp.dma_start(C[:, b, :, :], w["tables"][o]).then_inc(s_w[b], 16)

            @block.gpsimd
            def _(pool):
                pool.wait_ge(s_v, 32)
                pool.tensor_tensor(wo[:, :], wo2[:, 0, :], wo2[:, 1, :], ALU.add).then_inc(s_wo, 1)
                pool.wait_ge(s_wo, 1)
                for o in range(OPS):
                    to = w["k"] if o >= GROUPS else w["q"]
                    g = o % GROUPS
                    pool.wait_ge(s_part[2], o + 1)
                    pool.dma_start(to[:, g * P:(g + 1) * P, :].rearrange("r f t -> f r t"), parts[:, o % 2, :, :]
                                   ).then_inc(s_st[o % 2], 16)
                for b in range(2):
                    pool.wait_ge(s_st[b], 16 * OPS // 2)

            @block.tensor
            def _(pe):
                pe.wait_ge(s_v, 32)
                for o in range(OPS):
                    b = o % 2
                    pe.wait_ge(s_w[b], 32 * (o // 2 + 1))
                    for eo in range(2):
                        if o:
                            pe.wait_ge(s_ta, 2 * o - 1 + eo)
                        for h in range(2):
                            last = pe.matmul(PS[:, 2 * eo + h, :], W[:, b, eo * P:(eo + 1) * P], half(x, h),
                                             start=True, stop=True)
                        last.then_inc(s_eo, 1)
                    if o >= 4:
                        pe.wait_ge(s_vals, o - 3)
                    pe.matmul(PS[:, 4 + o % 4, :], x[:, o * P:(o + 1) * P], wv[:, :], start=True, stop=True
                              ).then_inc(s_prod, 1)

            @block.scalar
            def _(act):
                def part(o, r):
                    b = o % 2
                    act.wait_ge(s_left[r], o + 1)
                    if r == 0 and o >= 2:
                        act.wait_ge(s_st[b], 16 * (o // 2))
                    act.activation(parts[:, b, r, :], S[:, b, :] if r == 0 else R[:, b, r - 1, :], ACT.Copy
                                   ).then_inc(s_part[r], 1)

                for o in range(OPS + 1):
                    if o:
                        part(o - 1, 1)
                    if o < OPS:
                        part(o, 0)
                    if o:
                        part(o - 1, 2)
                    if o < OPS:
                        act.wait_ge(s_prod, o + 1)
                        act.activation(V[:, o, :], PS[:, 4 + o % 4, :], ACT.Copy).then_inc(s_vals, 1)

            @block.vector
            def _(dve):
                for o in range(OPS + 1):
                    b = o % 2
                    if o < OPS:
                        dve.wait_ge(s_w[b], 32 * (o // 2 + 1))
                        if o:
                            dve.wait_ge(s_left[0], o)
                        for eo in range(2):
                            dve.wait_ge(s_eo, 2 * o + eo + 1)
                            dve.tensor_tensor(A[:, eo, :], flat(PS[:, 2 * eo:2 * eo + 2, :]), C[:, b, eo, :], ALU.mult
                                              ).then_inc(s_ta, 1)
                    if o:
                        dve.wait_ge(s_part[0], o)
                        dve.wait_ge(s_left[0], o)
                        c = (o - 1) % 2
                        dve.tensor_tensor(R[:, c, 0, :], S[:, c, :], parts[:, c, 0, :], ALU.subtract).then_inc(s_left[1], 1)
                    if o < OPS:
                        dve.wait_ge(s_ta, 2 * o + 2)
                        dve.tensor_tensor(S[:, b, :], A[:, 0, :], A[:, 1, :], ALU.add).then_inc(s_left[0], 1)
                    if o:
                        dve.wait_ge(s_part[1], o)
                        dve.wait_ge(s_left[1], o)
                        if o >= 3:
                            dve.wait_ge(s_part[2], o - 2)
                        dve.tensor_tensor(R[:, c, 1, :], R[:, c, 0, :], parts[:, c, 1, :], ALU.subtract).then_inc(s_left[2], 1)

def plain_operands(nc, PS, name, x, weights, q, k, V, wproj):
    with ExitStack() as ctx:
        n = Names(nc, ctx, name)
        R = n.sb("R", [P, 2, 3, T])
        parts = n.sb("parts", [P, 2, 3, T], BF16)
        W = n.sb("W", [P, 3 * P])
        s_w, s_qk, s_act, s_rest, s_v, s_vals, s_st = (n.sem(t) for t in ("w", "qk", "act", "rest", "v", "vals", "st"))

        with nc.Block() as block:
            @block.sync
            def _(sp):
                sp.dma_start(W[:, :], weights[:, 0:3 * P]).then_inc(s_w, 16)
                sp.dma_start(wproj[:, :], weights[:, 3 * P:4 * P]).then_inc(s_w, 16)
                for o, to in enumerate((q, k)):
                    sp.wait_ge(s_act, 3 * o + 3)
                    sp.dma_start(to.rearrange("r f t -> f r t"), parts[:, o, :, :]).then_inc(s_st, 16)
                sp.wait_ge(s_st, 32)

            @block.tensor
            def _(pe):
                pe.wait_ge(s_w, 32)
                for o in range(2):
                    for h in range(2):
                        last = pe.matmul(PS[:, 2 * o + h, :], W[:, o * P:(o + 1) * P], half(x, h), start=True, stop=True)
                    last.then_inc(s_qk, 1)
                for c in range(NT):
                    last = pe.matmul(PS[:, 4 + c // 4, (c % 4) * P:(c % 4 + 1) * P], x[:, c * P:(c + 1) * P],
                                     W[:, 2 * P:3 * P], start=True, stop=True, skip_group_check=True)
                last.then_inc(s_v, 1)

            @block.scalar
            def _(act):
                for o in range(2):
                    for r in range(3):
                        if r == 0:
                            act.wait_ge(s_rest, 3 * o + 1)
                        else:
                            act.wait_ge(s_rest, 3 * o + 1 + r)
                        act.activation(parts[:, o, r, :], R[:, o, r, :], ACT.Copy).then_inc(s_act, 1)

            @block.vector
            def _(dve):
                for o in range(2):
                    dve.wait_ge(s_qk, o + 1)
                    dve.tensor_copy(R[:, o, 0, :], PS[:, 2 * o:2 * o + 2, :].rearrange("q a b -> q (a b)")).then_inc(s_rest, 1)
                    for r in range(1, 3):
                        dve.wait_ge(s_act, 3 * o + r)
                        dve.wait_ge(s_rest, 3 * o + r)
                        dve.tensor_tensor(R[:, o, r, :], R[:, o, r - 1, :], parts[:, o, r - 1, :], ALU.subtract
                                          ).then_inc(s_rest, 1)
                dve.wait_ge(s_v, 1)
                dve.tensor_copy(V[:, :, :], PS[:, 4:6, :].rearrange("q a (b c) -> q (a b) c", c=P)).then_inc(s_vals, 1)
                dve.wait_ge(s_vals, 1)


def rotary_attention(nc, PS, x, a, ident, identb):
    with ExitStack() as ctx:
        n = Names(nc, ctx, "rot")
        V = n.sb("V", [P, NT, HALF])
        wo = n.sb("wo", [P, HALF])
        H = n.sb("H", [P, GROUPS, T])
        w = {"q": nc.dram_tensor("rot_q", (3, HALF, T), BF16).ap(), "k": nc.dram_tensor("rot_k", (3, HALF, T), BF16).ap(),
             "mrow": nc.dram_tensor("rot_m", (GROUPS, 3 * 4 * NT, P), BF16).ap(),
             "weq": a["rot_w"], "tables": a["rot_tables"], "wv": a["rot_wv"], "wo2": a["rot_wo"],
             "qaux": a["qaux"], "kaux": a["kaux"][:, 0:T]}
        rotary_operands(nc, PS, "rotop", x, w, V, wo)
        attention(nc, PS, "rotat", w, True, NT // 2, 0.5, True, V, H, ident, identb)
        project(nc, PS, "rotpr", wo, H, GROUPS)


CROSS_SCALE = 1.0 / float(np.sqrt(np.float32(P)))


def cross_operands(nc, PS, name, x, w, cross, wo, Q, K, flag):
    bad = cross["bad"]
    EDGE = 9 * D8 // 32 * 32
    with ExitStack() as ctx:
        n = Names(nc, ctx, name)
        W = n.sb("W", [P, P])
        heads = n.sb("heads", [P, HEADS])
        kh = n.sb("kh", [P, HEADS])
        qf = n.sb("qf", [P, 3, T])
        qa = n.sb("qa", [P, T])
        qp = n.sb("qp", [P, 3, T], BF16)
        bf = n.sb("bf", [HEADS, 2, T])
        bp = n.sb("bp", [HEADS, 3, T], BF16)
        one = n.sb("one", [P, 1])
        total = n.sb("total", [1, 2])
        s_w, s_zero, s_k, s_ka = n.sem("w"), n.sem("zero"), n.sem("k"), n.sem("ka")
        s_q, s_qp, s_qr, s_qa, s_st = (n.sem(t) for t in ("q", "qp", "qr", "qa", "st"))
        s_kh, s_bound, s_b, s_bad, s_sum, s_dve = (n.sem(t) for t in ("kh", "bound", "b", "bad", "sum", "dve"))

        def flat(t):
            return t.rearrange("q a b -> q (a b)")

        def first_keys(eng, r):
            part = NARROW_BLOCKS[0][r][1]
            eng.dma_start(K[0][r * D8:(r + 1) * D8, 0, :, :],
                          cross["k"][part, 0:4 * D8, :].rearrange("(j i) t -> i j t", i=D8)
                          ).then_inc(s_k if r == len(NARROW_BLOCKS[0]) - 1 else s_ka, 16)

        with nc.Block() as block:
            @block.sync
            def _(sp):
                sp.dma_start(W[:, :], w["cross_w"][:, 2 * P:3 * P]).then_inc(s_w, 16)
                sp.dma_start(heads[:, :], w["heads"]).then_inc(s_w, 16)
                sp.dma_start(wo[:, :], w["cross_wo"]).then_inc(s_w, 16)
                sp.wait_ge(s_qp, 3)
                sp.dma_start(cross["q"].rearrange("r f t -> f r t"), qp[:, :, :]).then_inc(s_st, 16)
                sp.wait_ge(s_b, 5)
                sp.dma_start(cross["mrow"].rearrange("r h t -> h r t"), bp[:, :, :]).then_inc(s_st, 16)
                sp.wait_ge(s_st, 32)

            @block.tensor
            def _(pe):
                pe.wait_ge(s_w, 48)
                for h in range(2):
                    last = pe.matmul(PS[:, 4 + h, :], W[:, :], half(x, h), start=True, stop=True)
                last.then_inc(s_q, 1)
                pe.wait_ge(s_kh, 1)
                pe.wait_ge(s_qa, 1)
                for h in range(2):
                    last = pe.matmul(PS[0:HEADS, 6 + h, :], kh[:, :], half(qa, h), start=True, stop=True)
                last.then_inc(s_bound, 1)
                pe.wait_ge(s_bad, 1)
                pe.matmul(PS[0:1, 0, 0:3], one[:, :], bad[:, 0:3], start=True, stop=True).then_inc(s_sum, 1)

            @block.gpsimd
            def _(pool):
                for b in range(2):
                    pool.memset(K[b][EDGE:P].rearrange("q a b c -> q (a b c)").bitcast(F32), 0.0).then_inc(s_zero, 1)
                    if b == 0:
                        pool.wait_ge(s_zero, 1)
                        first_keys(pool, len(NARROW_BLOCKS[0]) - 1)
                pool.wait_ge(s_zero, 2)
                pool.wait_ge(s_k, 16)

            @block.scalar
            def _(act):
                for r in range(len(NARROW_BLOCKS[0]) - 1):
                    first_keys(act, r)
                act.wait_ge(s_qr, 1)
                act.activation(qa[:, :], qf[:, 0, :], ACT.Abs).then_inc(s_qa, 1)
                for r in range(3):
                    act.wait_ge(s_qr, r + 1)
                    act.activation(qp[:, r, :], qf[:, r, :], ACT.Copy).then_inc(s_qp, 1)
                act.wait_ge(s_ka, 16 * (len(NARROW_BLOCKS[0]) - 1))

            @block.vector
            def _(dve):
                own = Count(dve, s_dve)
                own.up(dve.memset(one[:, :], 1.0))
                for b in range(2):
                    own.up(dve.memset(Q[b][EDGE:P].rearrange("q a b c -> q (a b c)").bitcast(F32), 0.0))
                dve.wait_ge(s_w, 48)
                dve.tensor_scalar(kh[:, :], heads[:, :], cross["kmax"][:, NC // 3:NC // 3 + 1], None, ALU.mult
                                  ).then_inc(s_kh, 1)
                dve.wait_ge(s_q, 1)
                dve.tensor_copy(qf[:, 0, :], flat(PS[:, 4:6, :])).then_inc(s_qr, 1)
                for r in range(2):
                    dve.wait_ge(s_qp, r + 1)
                    dve.wait_ge(s_qr, r + 1)
                    dve.tensor_tensor(qf[:, r + 1, :], qf[:, r, :], qp[:, r, :], ALU.subtract).then_inc(s_qr, 1)
                dve.wait_ge(s_bound, 1)
                bounds = flat(PS[0:HEADS, 6:8, :])
                dve.tensor_scalar(bp[:, 0, :], bounds, -1.0, None, ALU.mult).then_inc(s_b, 1)
                own.up(dve.tensor_reduce(bad[0:HEADS, 2:3], bounds, AX.X, ALU.max))
                dve.wait_ge(s_b, 1)
                dve.scalar_tensor_tensor(bf[:, 0, :], bounds, -1.0, bp[:, 0, :], ALU.mult, ALU.subtract).then_inc(s_b, 1)
                dve.wait_ge(s_b, 2)
                dve.tensor_copy(bp[:, 1, :], bf[:, 0, :]).then_inc(s_b, 1)
                dve.wait_ge(s_b, 3)
                dve.tensor_tensor(bf[:, 1, :], bf[:, 0, :], bp[:, 1, :], ALU.subtract).then_inc(s_b, 1)
                dve.wait_ge(s_b, 4)
                dve.tensor_copy(bp[:, 2, :], bf[:, 1, :]).then_inc(s_b, 1)
                own.done()
                dve.tensor_scalar(bad[0:HEADS, 2:3], bad[0:HEADS, 2:3], BOUND_LIMIT / CROSS_SCALE, None, ALU.is_gt
                                  ).then_inc(s_bad, 1)
                dve.wait_ge(s_sum, 1)
                own.up(dve.tensor_reduce(total[:, 0:1], PS[0:1, 0, 0:3], AX.X, ALU.add))
                own.done()
                own.up(dve.tensor_scalar(flag[:, :], total[:, 0:1], 0.0, None, ALU.is_equal))
                own.done()


def cross_general(nc, PS, name, w, V, out, ident, flag):
    STEPS = NC // 3
    W3 = 3 * P
    B = 9 * D8
    with ExitStack() as ctx:
        n = Names(nc, ctx, name)
        Q = n.sb("Q", [P, 4, T], BF16)
        K = n.sb("K", [P, 4, KPAD], BF16)
        mask = n.sb("mask", [P, KEYS], I32)
        bias = n.sb("bias", [P, KPAD])
        S = n.sb("S", [P, KPAD])
        E = n.sb("E", [P, 2, W3])
        ET = n.sb("ET", [P, 2, W3])
        ones = n.sb("ones", [P, D8])
        top = n.sb("top", [P, 1])
        rec = n.sb("rec", [P, 1])
        s_set, s_ld, s_mask = n.sem("set"), n.sem("ld"), n.sem("mask")
        s_bias = n.sem("bias")
        s_s, s_add = n.sem("s"), n.sem("add")
        s_top, s_sub = n.sem("top"), n.sem("sub")
        s_e, s_t, s_tc = n.sem("e"), n.sem("t"), n.sem("tc")
        s_pv = n.sem("pv")
        s_rec = n.sem("rec")
        s_o = n.sem("o")

        def steps(eng, body):
            body(0, 0)
            with eng.Fori(0, STEPS // 2) as i:
                body(2 * i + 1, 1)
                body(2 * i + 2, 0)

        def tiles(eng, body, before=None):
            with eng.Fori(0, GROUPS) as g:
                if before is not None:
                    before(g)
                with eng.Fori(0, NT) as t:
                    body(g, t)

        loads = 16 * 2 * len(NARROW_BLOCKS[0])
        with nc.Block() as block:
            @block.sync
            def _(sp):
              with when(sp, flag, 0):
                sp.wait_ge(s_set, 4)

                def load(g):
                    sp.wait_ge(s_o, g * (NT * 4) + 1)
                    for r, (i, j) in enumerate(NARROW_BLOCKS[0]):
                        for to, of, part in ((Q, w["q"], i), (K, w["k"], j)):
                            sp.dma_start(to[r * D8:(r + 1) * D8, :, :],
                                         of[part, bass.ds(g * 32, 32), :].rearrange("(j i) t -> i j t", i=D8)
                                         ).then_inc(s_ld, 16)

                def masks(g, t):
                    sp.wait_ge(s_bias, g * NT + t + 1)
                    sp.dma_start(mask[:, :], w["mask"][bass.ds(t * P, P), :]).then_inc(s_mask, 16)

                tiles(sp, masks, load)

            @block.tensor
            def _(pe):
              with when(pe, flag, 0):
                pe.sem_inc(s_pv, 2)
                pe.sem_inc(s_t, 2)

                def tile(g, t):
                    pe.wait_ge(s_ld, g * loads + loads)
                    for j in range(4):
                        u = (g * NT + t) * 4 + j
                        pe.wait_ge(s_add, u * STEPS + 2)

                        def scores(i, b):
                            pe.wait_ge(s_add, u * STEPS + i + 1)
                            pe.matmul(PS[:, b, 0:W3], Q[:, j, bass.ds(t * P, P)], K[:, j, bass.ds(i * W3, W3)],
                                      start=True, stop=True).then_inc(s_s, 1)

                        steps(pe, scores)
                        pe.wait_ge(s_o, u + 1)

                        def weigh(i, b):
                            pe.wait_ge(s_e, u * STEPS + i + 3)
                            pe.wait_ge(s_tc, u * STEPS + i + 1)
                            for c in range(3):
                                last = pe.transpose(PS[:, 2 + b, c * P:(c + 1) * P], E[:, b, c * P:(c + 1) * P], ident[:, :])
                            last.then_inc(s_t, 1)
                            pe.wait_ge(s_tc, u * STEPS + i + 3)
                            first = isinstance(i, int)
                            for c in range(3):
                                of = ET[:, b, c * P:(c + 1) * P]
                                pe.matmul(PS[:, 6, 0:D8], of, V[:, bass.ds(3 * i + c, 1), bass.ds(g * 32 + j * D8, D8)
                                                                ].rearrange("q a b -> q (a b)"),
                                          start=first and c == 0, stop=False, skip_group_check=True)
                                last = pe.matmul(PS[:, 7, 0:D8], of, ones[:, :], start=first and c == 0, stop=False,
                                                 skip_group_check=True)
                            last.then_inc(s_pv, 1)

                        steps(pe, weigh)

                tiles(pe, tile)

            @block.scalar
            def _(act):
              with when(act, flag, 0):
                act.sem_inc(s_e, 2)

                def tile(g, t):
                    for j in range(4):
                        u = (g * NT + t) * 4 + j
                        act.wait_ge(s_sub, u + 1)
                        act.wait_ge(s_t, u * STEPS + 2)

                        def exponentials(i, b):
                            act.wait_ge(s_t, u * STEPS + i + 1)
                            act.activation(E[:, b, :], S[:, bass.ds(i * W3, W3)], ACT.Exp, scale=CROSS_SCALE).then_inc(s_e, 1)

                        steps(act, exponentials)

                tiles(act, tile)

            @block.vector
            def _(dve):
              with when(dve, flag, 0):
                dve.sem_inc(s_add, 2)
                dve.sem_inc(s_tc, 2)
                dve.sem_inc(s_o, 1)
                dve.sem_inc(s_bias, 1)
                dve.memset(Q.rearrange("q a b -> q (a b)"), 0.0).then_inc(s_set, 1)
                dve.memset(K.rearrange("q a b -> q (a b)"), 0.0).then_inc(s_set, 1)
                dve.memset(ones[:, :], 1.0).then_inc(s_set, 1)
                dve.memset(bias[:, KEYS:KPAD], PADDED).then_inc(s_set, 1)
                dve.wait_ge(s_set, 4)

                def tile(g, t):
                    dve.wait_ge(s_mask, (g * NT + t) * 16 + 16)
                    dve.tensor_scalar(bias[:, 0:KEYS], mask[:, :], 0, MASKED, ALU.is_equal, ALU.mult).then_inc(s_bias, 1)
                    dve.wait_ge(s_bias, g * NT + t + 2)
                    for j in range(4):
                        u = (g * NT + t) * 4 + j
                        dve.wait_ge(s_e, u * STEPS + 2)

                        def add(i, b):
                            at = bass.ds(i * W3, W3)
                            dve.wait_ge(s_s, u * STEPS + i + 1)
                            dve.tensor_tensor(S[:, at], PS[:, b, 0:W3], bias[:, at], ALU.add).then_inc(s_add, 1)

                        steps(dve, add)
                        dve.wait_ge(s_add, u * STEPS + STEPS + 2)
                        dve.tensor_reduce(top[:, :], S[:, :], AX.X, ALU.max).then_inc(s_top, 1)
                        dve.wait_ge(s_top, u + 1)
                        dve.tensor_scalar(S[:, :], S[:, :], top[:, 0:1], None, ALU.subtract).then_inc(s_sub, 1)
                        dve.wait_ge(s_pv, u * STEPS + 2)

                        def copy(i, b):
                            dve.wait_ge(s_t, u * STEPS + i + 3)
                            dve.wait_ge(s_pv, u * STEPS + i + 1)
                            dve.tensor_copy(ET[:, b, :], PS[:, 2 + b, 0:W3]).then_inc(s_tc, 1)

                        steps(dve, copy)
                        dve.wait_ge(s_pv, u * STEPS + STEPS + 2)
                        dve.reciprocal(rec[:, :], PS[:, 7, 0:1]).then_inc(s_rec, 1)
                        dve.wait_ge(s_rec, u + 1)
                        dve.tensor_scalar(out[:, bass.ds(t, 1), bass.ds(g * 32 + j * D8, D8)].rearrange("q a b -> q (a b)"),
                                          PS[:, 6, 0:D8], rec[:, 0:1], None, ALU.mult).then_inc(s_o, 1)

                tiles(dve, tile)
                dve.wait_ge(s_o, GROUPS * NT * 4 + 1)


def cross_attention(nc, PS, x, a, cross, ident, identb):
    with ExitStack() as ctx:
        n = Names(nc, ctx, "cross")
        H = n.sb("H", [P, NT, P])
        wo = n.sb("wo", [P, P])
        flag = n.sb("flag", [1, 1], I32)
        cross["q"] = nc.dram_tensor("cross_q", (3, P, T), BF16).ap()
        cross["mrow"] = nc.dram_tensor("cross_m", (3, HEADS, T), BF16).ap()
        w = {"qaux": a["qaux"], "mask": a["mask"], **cross}
        with ExitStack() as inner:
            m = Names(nc, inner, "crin")
            Q = [m.sb(f"Q{b}", [P, 1, 4, T], BF16) for b in range(2)]
            K = [m.sb(f"K{b}", [P, 1, 4, KPAD], BF16) for b in range(2)]
            cross_operands(nc, PS, "crop", x, a, cross, wo, Q, K, flag)
            attention(nc, PS, "crat", w, False, NC, CROSS_SCALE, False, cross["V"], H, ident, identb, flag=flag,
                      early=(Q, K))
        cross_general(nc, PS, "crgen", w, cross["V"], H, ident, flag)
        project(nc, PS, "crpr", wo, H, 1, ident)


def last_block(nc, PS, x, a, onesd, ident, identb, cols):
    with ExitStack() as ctx:
        n = Names(nc, ctx, "last")
        normed = n.sb("normed", [P, T])
        xa = n.sb("xa", [P, T])
        xxa = n.sb("xxa", [P, T])
        layer_norm(nc, PS, "lastn1", onesd, x, normed, scale=cols[:, 2:3], shift=cols[:, 3:4])
        with ExitStack() as inner:
            m = Names(nc, inner, "lastat")
            V = m.sb("V", [P, NT, P])
            H = m.sb("H", [P, NT, P])
            wproj = m.sb("wproj", [P, P])
            w = {"q": nc.dram_tensor("last_q", (3, P, T), BF16).ap(), "k": nc.dram_tensor("last_k", (3, P, T), BF16).ap(),
                 "mrow": nc.dram_tensor("last_m", (GROUPS, 3 * 4 * NT, P), BF16).ap(),
                 "qaux": a["qaux"], "kaux": a["kaux"][:, 0:T]}
            plain_operands(nc, PS, "lastop", normed, a["last_w"], w["q"], w["k"], V, wproj)
            attention(nc, PS, "lastat", w, False, NT, 1.0 / float(np.sqrt(D8)), True, V, H, ident, identb)
            project(nc, PS, "lastpr", wproj, H, 1, ident)
        layer_norm(nc, PS, "lastn2", onesd, x, normed, Y=0, keep=xa, also=(xxa, x), scale=cols[:, 4:5], shift=cols[:, 5:6])
        routed_mlp(nc, PS, "moe1", normed, ident, {"small": a["small1"], "experts": a["experts1"]}, ACT.Gelu_apprx_tanh, False)
        layer_norm(nc, PS, "ln6", onesd, xxa, x, Y=0)
def decoder(nc, a, out):
    with ExitStack() as ctx:
        n = Names(nc, ctx, "all")
        PS = ctx.enter_context(nc.psum_tensor("banks", [P, 8, HALF], F32))
        x = n.sb("x", [P, T])
        onesd = n.sb("onesd", [P, P])
        ident = n.sb("ident", [P, P])
        identb = n.sb("identb", [P, P], BF16)
        cols = n.sb("cols", [P, 8])
        s_in, s_mem, s_out = n.sem("in"), n.sem("mem"), n.sem("stored")
        with nc.Block() as block:
            @block.sync
            def _(sp):
                sp.dma_start(x[:, :], a["xT"]).then_inc(s_in, 16)
                sp.dma_start(ident[:, :], a["ident"]).then_inc(s_in, 16)
                sp.dma_start(identb[:, :], a["identb"]).then_inc(s_in, 16)
                sp.dma_start(cols[:, :], a["cols"]).then_inc(s_in, 16)
                sp.wait_ge(s_in, 64)

            @block.vector
            def _(dve):
                dve.memset(onesd[:, :], 1.0 / P).then_inc(s_mem, 1)
                dve.wait_ge(s_mem, 1)

        distance_attention(nc, PS, x, a, 6)
        layer_norm(nc, PS, "ln1", onesd, x, x, Y=6, bias=cols[:, 0:1])
        cross = {"V": n.sb("crossV", [P, NC, P]), "kmax": n.sb("crosskmax", [P, NC // 3 + 1]), "bad": n.sb("bad", [P, 4]),
                 "k": nc.dram_tensor("cross_k", (3, P, KPAD), BF16).ap(),
                 "kaux": nc.dram_tensor("cross_kaux", (4, KPAD), BF16).ap()}
        context_mlp(nc, PS, x, a, 6, cross)
        layer_norm(nc, PS, "ln2", onesd, x, x, Y=6)
        routed_mlp(nc, PS, "moe0", x, ident, {"small": a["small0"], "experts": a["experts0"]}, ACT.Relu, True)
        layer_norm(nc, PS, "ln3", onesd, x, x, Y=0)
        rotary_attention(nc, PS, x, a, ident, identb)
        layer_norm(nc, PS, "ln4", onesd, x, x, Y=0)
        cross_attention(nc, PS, x, a, cross, ident, identb)
        layer_norm(nc, PS, "ln5", onesd, x, x, Y=0, bias=cols[:, 1:2])
        last_block(nc, PS, x, a, onesd, ident, identb, cols)
        with nc.Block() as block:
            @block.sync
            def _(sp):
                sp.dma_start(out, x[:, :]).then_inc(s_out, 16)
                sp.wait_ge(s_out, 16)


def _columns(*vectors):
    a = np.zeros((P, 8), np.float32)
    for i, v in enumerate(vectors):
        a[:, i] = v
    return a


def _context(c):
    c = np.concatenate([c, np.zeros((KPAD - KEYS, P), c.dtype)]).reshape(NC, P, P)
    return np.concatenate([c.transpose(0, 2, 1), c], axis=2)


def _experts(w1, w2):
    w2 = w2.reshape(EXPERTS, FC, P, P).transpose(0, 2, 1, 3).reshape(EXPERTS, P, FF)
    return np.concatenate([w1, w2], axis=2)


def _small(router_w, router_b, b1=None, b2=None):
    a = np.zeros((P, 320), np.float32)
    a[:, 0:EXPERTS] = router_w
    a[:, 64:128] = np.broadcast_to(router_b, (NT, EXPERTS)).reshape(1, 64)
    a[:, 128:192] = np.broadcast_to(np.arange(EXPERTS, 0, -1), (NT, EXPERTS)).reshape(1, 64)
    if b1 is not None:
        a[:, EXPERTS:EXPERTS + EXPERTS * FC] = b1.reshape(EXPERTS * FC, P).T
        a[0:EXPERTS, 192:320] = b2
    return a


def _angles(width):
    theta = np.float32(1) / np.power(1250.0, np.arange(0, width, 2) / width).astype(np.float32)
    angle = (theta[:, None] * np.arange(1, T + 1, dtype=np.float32)[None, :]).astype(np.float64)
    return np.cos(angle), np.sin(angle)


def _rotary(wq, wk, wv, wo):
    cos, sin = _angles(2 * HALF)
    weights = [np.stack([wq[:, 0::2], wq[:, 1::2]])]
    tables = [np.stack([cos + sin, cos - sin])]
    cos, sin = (np.repeat(t, 2, axis=0) for t in _angles(HALF))
    odd = (np.arange(HALF) % 2 == 1)[:, None]
    weights.append(np.stack([np.repeat(wk[:, 0::2], 2, axis=1), np.repeat(wk[:, 1::2], 2, axis=1)]))
    tables.append(np.stack([np.where(odd, sin, cos), np.where(odd, cos, -sin)]))
    weights = np.stack(weights).reshape(2, 2, P, GROUPS, P).transpose(0, 3, 2, 1, 4).reshape(2 * GROUPS, P, 2 * P)
    tables = np.stack(tables).astype(np.float32).reshape(2, 2, GROUPS, P, T).transpose(0, 2, 3, 1, 4)
    wo = wo.reshape(GROUPS, P, 2, P).transpose(1, 2, 0, 3).reshape(P, 2, HALF)
    return {"rot_w": weights, "rot_tables": tables.reshape(2 * GROUPS, P, 2, T), "rot_wv": wv, "rot_wo": wo}


def _cross(wk, wv, wq, wo):
    blocks = np.zeros((P, 3, P), wk.dtype)
    heads = np.zeros((P, HEADS), np.float32)
    for h in range(HEADS):
        at = slice(h * D8, (h + 1) * D8)
        for i, m in enumerate((wk, wv, wq)):
            blocks[at, i, at] = m.T
        heads[at, h] = 1.0
    return {"cross_w": blocks.reshape(P, 3 * P), "cross_wo": wo.T, "heads": heads}


def _aux():
    bf16 = mybir.dt.np(BF16)
    return {"qaux": np.repeat(np.array([[1], [0], [0], [0]]), T, axis=1).astype(bf16),
            "kaux": np.repeat(np.array([[0], [1], [1], [1]]), KPAD, axis=1).astype(bf16),
            "identb": np.eye(P).astype(bf16)}


def _layout(inputs):
    f = {k: np.asarray(v) for k, v in inputs.items()}
    W = f["L0_attn_W_in"].reshape(P, PAIRS, 2, 4, D0)
    wpair = np.concatenate([W[:, :, 0, 0], W[:, :, 0, 1], W[:, :, 1, 0], W[:, :, 1, 1], W[:, :, 0, 2], W[:, :, 1, 2],
                            W[:, :, 0, 3], W[:, :, 1, 3]], axis=2).transpose(1, 0, 2)
    b = f["L0_attn_b_in"].reshape(HEADS, 4, D0)
    norms = np.zeros((P, 34), np.float32)
    norms[0:D0, 1] = 1.0
    norms[D0:P, 32] = 0.25
    rows = np.zeros((P, 2), np.float32)
    rows[64, 0] = rows[97, 1] = 1.0
    a = {
        "xT": f["x"][0].T,
        "ident": np.eye(P, dtype=np.float32),
        "cols": _columns(f["L0_attn_b_out"], f["L1_xattn_bo"], f["L1_ffn_ln1_w"], f["L1_ffn_ln1_b"],
                         f["L1_ffn_ln2_w"], f["L1_ffn_ln2_b"]),
        "wpair": wpair,
        "wout": f["L0_attn_W_out"].reshape(PAIRS, P, P).transpose(1, 0, 2),
        "bqk": b[:, 0:2].transpose(1, 2, 0).reshape(P, HEADS),
        "bg": b[:, 3].reshape(PAIRS, P).T,
        "bv": np.broadcast_to(b[:, 2].reshape(1, T), (P, T)),
        "norms": norms,
        "rows": rows,
        "ctx": _context(f["ctx_1024"][0]),
        "small0": _small(f["L0_ffn_router_W"], f["L0_ffn_router_b"], f["L0_ffn_b1"], f["L0_ffn_b2"]),
        "experts0": _experts(f["L0_ffn_W1"], f["L0_ffn_W2"]),
        "small1": _small(f["L1_ffn_gate_w"], f["L1_ffn_gate_b"]),
        "experts1": _experts(f["L1_ffn_w1"], f["L1_ffn_w2"]),
        **_rotary(f["L1_attn_Wq"], f["L1_attn_Wk"], f["L1_attn_Wv"], f["L1_attn_Wo"]),
        **_aux(),
        **_cross(f["L1_xattn_Wk"], f["L1_xattn_Wv"], f["L1_xattn_Wq"], f["L1_xattn_Wo"]),
        "mask": f["mask_1x1xSxS2_ik1"][0, 0],
        "last_w": np.concatenate([f["L1_ffn_w_qkv"], f["L1_ffn_w_proj"]], axis=1),
    }
    return {k: np.ascontiguousarray(v) for k, v in a.items()}


def kernel(**inputs):
    import concourse.bacc as bacc
    from concourse.bass_utils import run_bass_kernel_spmd

    nc = bacc.Bacc("TRN2", target_bir_lowering=False, num_devices=1)
    arrays = {f"in_{k}": v for k, v in _layout(inputs).items()}
    aps = {k[3:]: nc.dram_tensor(k, v.shape, mybir.dt.from_np(v.dtype), kind="ExternalInput").ap() for k, v in arrays.items()}
    out = nc.dram_tensor("out_T", (P, T), F32, kind="ExternalOutput").ap()
    decoder(nc, aps, out)
    r = run_bass_kernel_spmd(nc, [arrays], core_ids=[0])
    return np.ascontiguousarray(r.results[0]["out_T"].T).reshape(1, T, P)
```
